# Optimizing a Trainium2 kernel written in Bass

```python
import numpy as np
import jax
import jax.numpy as jnp

def _softmax(x, axis=-1):
    return jax.nn.softmax(x, axis=axis)

def _gelu(x):
    return jax.nn.gelu(x, approximate=True)

def _silu(x):
    return jax.nn.silu(x)

def _sigmoid(x):
    return jax.nn.sigmoid(x)

def _layernorm(x, axis=-1, eps=1e-05):
    m = jnp.mean(x, axis=axis, keepdims=True)
    v = jnp.var(x, axis=axis, keepdims=True)
    return (x - m) / jnp.sqrt(v + eps)

def _scatter_add(tgt, idx, src, axis=0):
    return tgt.at[idx].add(src)

def _segment_sum(src, seg, n):
    return jax.ops.segment_sum(src, seg, n)
kernel_name = 'mk_prb_d2_jaxref_r8_bea230'

def setup_inputs(seed: int=0):
    np.random.seed(seed)
    _w = jnp.asarray

    def _L0_attn_setup():
        import jax, jax.numpy as jnp
        import numpy as np
        ALPHA = 1.2
        A = 1.0
        BANDWIDTH = 1.0
        D_INTRINSIC = 2
        SPHERE_RADIUS = 1.0
        NUM_HEADS = 16
        HIDDEN = 128
        HEAD_DIM = HIDDEN // NUM_HEADS
        EPS = 1e-07

        def _l2norm(t):
            n = jnp.sqrt(jnp.sum(t * t, axis=-1, keepdims=True))
            return t / jnp.maximum(n, 1e-12)
        key = jax.random.key(seed)
        k1, k2, k3, k4, k5 = jax.random.split(key, 5)
        B, S = (2, 256)
        scale = 0.02
        return {'x': jax.random.normal(k1, (B, S, HIDDEN), dtype=jnp.float32), 'w_qkv': jax.random.normal(k2, (3 * HIDDEN, HIDDEN), dtype=jnp.float32) * scale, 'b_qkv': jnp.zeros((3 * HIDDEN,), dtype=jnp.float32), 'w_out': jax.random.normal(k3, (HIDDEN, HIDDEN), dtype=jnp.float32) * scale, 'b_out': jnp.zeros((HIDDEN,), dtype=jnp.float32)}
    _L0_attn_in = _L0_attn_setup()

    def _L0_ffn_setup():
        import jax, jax.numpy as jnp
        import numpy as np
        DIM = 128
        HIDDEN = 384
        SCALE = 1.0 / 127.0

        def _dequant(w_int, dtype):
            return w_int.astype(dtype) * jnp.asarray(SCALE, dtype)
        key = jax.random.key(seed)
        k_x, k_g, k_u, k_d = jax.random.split(key, 4)
        x = jax.random.normal(k_x, (4, 256, DIM), dtype=jnp.float32)
        w_gate = jax.random.randint(k_g, (HIDDEN, DIM), -127, 128, dtype=jnp.int32)
        w_up = jax.random.randint(k_u, (HIDDEN, DIM), -127, 128, dtype=jnp.int32)
        w_down = jax.random.randint(k_d, (DIM, HIDDEN), -127, 128, dtype=jnp.int32)
        return {'x': x, 'w_gate': w_gate, 'w_up': w_up, 'w_down': w_down}
    _L0_ffn_in = _L0_ffn_setup()

    def _L1_attn_setup():
        import jax, jax.numpy as jnp
        import numpy as np
        B, N, D = (4, 256, 128)
        H, HD = (16, 64)
        MAX_SEQ = 512
        INNER = H * HD

        def _rope_tables(n, head_dim):
            inv_freq = 1.0 / 10000.0 ** (jnp.arange(0, head_dim, 2, dtype=jnp.float32) / head_dim)
            pos = jnp.arange(n, dtype=jnp.float32)
            ang = pos[:, None] * inv_freq[None, :]
            return (jnp.sin(ang), jnp.cos(ang))
        key = jax.random.key(seed)
        ks = jax.random.split(key, 5)
        s = 0.02
        return {'x': jax.random.normal(ks[0], (B, N, D), dtype=jnp.float32), 'ln_gamma': jnp.ones((D,), jnp.float32), 'ln_beta': jnp.zeros((D,), jnp.float32), 'w_qkv': jax.random.normal(ks[1], (D, 3 * INNER), dtype=jnp.float32) * s, 'w_out': jax.random.normal(ks[2], (INNER, D), dtype=jnp.float32) * s, 'b_out': jnp.zeros((D,), jnp.float32)}
    _L1_attn_in = _L1_attn_setup()

    def _L1_ffn_setup():
        import jax, jax.numpy as jnp
        import numpy as np
        D_IN, D_HID = (128, 512)

        def _ternary(key, shape):
            return jax.random.randint(key, shape, -1, 2).astype(jnp.float32)

        def _tlin(x, w, s):
            return jnp.einsum('bsi,oi->bso', x, w) * s
        key = jax.random.key(seed)
        ks = jax.random.split(key, 12)
        inv = lambda fan: 1.0 / np.sqrt(fan).astype(np.float32)
        return {'x': jax.random.normal(ks[0], (4, 256, D_IN), dtype=jnp.float32), 'w1_w': _ternary(ks[1], (D_HID, D_IN)), 'w1_s': jax.random.uniform(ks[2], (D_HID,), dtype=jnp.float32) * inv(D_IN), 'w2_w': _ternary(ks[3], (D_HID, D_IN)), 'w2_s': jax.random.uniform(ks[4], (D_HID,), dtype=jnp.float32) * inv(D_IN), 'h1_w': _ternary(ks[5], (D_HID, D_HID)), 'h1_s': jax.random.uniform(ks[6], (D_HID,), dtype=jnp.float32) * inv(D_HID), 'h2_w': _ternary(ks[7], (D_HID, D_HID)), 'h2_s': jax.random.uniform(ks[8], (D_HID,), dtype=jnp.float32) * inv(D_HID), 'w3_w': _ternary(ks[9], (D_IN, D_HID)), 'w3_s': jax.random.uniform(ks[10], (D_IN,), dtype=jnp.float32) * inv(D_HID)}
    _L1_ffn_in = _L1_ffn_setup()
    _d = {'L0_attn_x': _L0_attn_in['x'], 'L0_attn_w_qkv': _L0_attn_in['w_qkv'], 'L0_attn_b_qkv': _L0_attn_in['b_qkv'], 'L0_attn_w_out': _L0_attn_in['w_out'], 'L0_attn_b_out': _L0_attn_in['b_out'], 'L0_ffn_w_gate': _L0_ffn_in['w_gate'], 'L0_ffn_w_up': _L0_ffn_in['w_up'], 'L0_ffn_w_down': _L0_ffn_in['w_down'], 'L1_attn_ln_gamma': _L1_attn_in['ln_gamma'], 'L1_attn_ln_beta': _L1_attn_in['ln_beta'], 'L1_attn_w_qkv': _L1_attn_in['w_qkv'], 'L1_attn_w_out': _L1_attn_in['w_out'], 'L1_attn_b_out': _L1_attn_in['b_out'], 'L1_ffn_w1_w': _L1_ffn_in['w1_w'], 'L1_ffn_w1_s': _L1_ffn_in['w1_s'], 'L1_ffn_w2_w': _L1_ffn_in['w2_w'], 'L1_ffn_w2_s': _L1_ffn_in['w2_s'], 'L1_ffn_h1_w': _L1_ffn_in['h1_w'], 'L1_ffn_h1_s': _L1_ffn_in['h1_s'], 'L1_ffn_h2_w': _L1_ffn_in['h2_w'], 'L1_ffn_h2_s': _L1_ffn_in['h2_s'], 'L1_ffn_w3_w': _L1_ffn_in['w3_w'], 'L1_ffn_w3_s': _L1_ffn_in['w3_s']}
    _x0 = _d['L0_attn_x']
    _d['L0_attn_x'] = jax.random.normal(jax.random.fold_in(jax.random.key(seed), 1), (1, 2048, 128), dtype=_x0.dtype)
    del _x0
    return _d

def reference(L0_attn_x, L0_attn_w_qkv, L0_attn_b_qkv, L0_attn_w_out, L0_attn_b_out, L0_ffn_w_gate, L0_ffn_w_up, L0_ffn_w_down, L1_attn_ln_gamma, L1_attn_ln_beta, L1_attn_w_qkv, L1_attn_w_out, L1_attn_b_out, L1_ffn_w1_w, L1_ffn_w1_s, L1_ffn_w2_w, L1_ffn_w2_s, L1_ffn_h1_w, L1_ffn_h1_s, L1_ffn_h2_w, L1_ffn_h2_s, L1_ffn_w3_w, L1_ffn_w3_s):

    def _L0_attn_ref(x, w_qkv, b_qkv, w_out, b_out):
        import jax, jax.numpy as jnp
        import numpy as np
        ALPHA = 1.2
        A = 1.0
        BANDWIDTH = 1.0
        D_INTRINSIC = 2
        SPHERE_RADIUS = 1.0
        NUM_HEADS = 16
        HIDDEN = 128
        HEAD_DIM = HIDDEN // NUM_HEADS
        EPS = 1e-07

        def _l2norm(t):
            n = jnp.sqrt(jnp.sum(t * t, axis=-1, keepdims=True))
            return t / jnp.maximum(n, 1e-12)
        B, S, H = x.shape
        qkv = x @ w_qkv.T + b_qkv
        q, k, v = jnp.split(qkv, 3, axis=-1)
        to_heads = lambda t: t.reshape(B, S, NUM_HEADS, HEAD_DIM).transpose(0, 2, 1, 3)
        q = _l2norm(to_heads(q))
        k = _l2norm(to_heads(k))
        v = to_heads(v)
        cos = jnp.einsum('bhsd,bhtd->bhst', q, k)
        g_dist = jnp.arccos(jnp.clip(cos, -1.0 + EPS, 1.0 - EPS)) * SPHERE_RADIUS
        attn_score = (1.0 + g_dist / BANDWIDTH ** 0.5) ** (-D_INTRINSIC - ALPHA)
        n_r = jnp.sum(attn_score, axis=-1)
        n_c = jnp.sum(attn_score, axis=-2)
        k_tilde = (n_r ** (-A))[..., :, None] * attn_score * (n_c ** (-A))[..., None, :]
        probs = k_tilde / jnp.maximum(jnp.sum(k_tilde, axis=-1, keepdims=True), 1e-12)
        out = jnp.einsum('bhst,bhtd->bhsd', probs, v)
        out = out.transpose(0, 2, 1, 3).reshape(B, S, H)
        return out @ w_out.T + b_out

    def _L0_ffn_ref(x, w_gate, w_up, w_down):
        import jax, jax.numpy as jnp
        import numpy as np
        DIM = 128
        HIDDEN = 384
        SCALE = 1.0 / 127.0

        def _dequant(w_int, dtype):
            return w_int.astype(dtype) * jnp.asarray(SCALE, dtype)
        wg = _dequant(w_gate, x.dtype)
        wu = _dequant(w_up, x.dtype)
        wd = _dequant(w_down, x.dtype)
        gate = jnp.einsum('bsd,hd->bsh', x, wg)
        up = jnp.einsum('bsd,hd->bsh', x, wu)
        h = jax.nn.silu(gate) * up
        return jnp.einsum('bsh,dh->bsd', h, wd)

    def _L1_attn_ref(x, ln_gamma, ln_beta, w_qkv, w_out, b_out):
        import jax, jax.numpy as jnp
        import numpy as np
        B, N, D = (4, 256, 128)
        H, HD = (16, 64)
        MAX_SEQ = 512
        INNER = H * HD

        def _rope_tables(n, head_dim):
            inv_freq = 1.0 / 10000.0 ** (jnp.arange(0, head_dim, 2, dtype=jnp.float32) / head_dim)
            pos = jnp.arange(n, dtype=jnp.float32)
            ang = pos[:, None] * inv_freq[None, :]
            return (jnp.sin(ang), jnp.cos(ang))
        b, n, d = x.shape
        mu = jnp.mean(x, axis=-1, keepdims=True)
        var = jnp.var(x, axis=-1, keepdims=True)
        xn = (x - mu) / jnp.sqrt(var + 1e-05) * ln_gamma + ln_beta
        qkv = xn @ w_qkv
        q, k, v = jnp.split(qkv, 3, axis=-1)

        def to_heads(t):
            return t.reshape(b, n, H, HD).transpose(0, 2, 1, 3)
        q, k, v = (to_heads(q), to_heads(k), to_heads(v))
        sin, cos = _rope_tables(n, HD)
        sin = sin[None, None]
        cos = cos[None, None]
        half = HD // 2

        def rotate(t):
            t1, t2 = (t[..., :half], t[..., half:])
            return jnp.concatenate([t1 * cos - t2 * sin, t2 * cos + t1 * sin], axis=-1)
        qr, kr = (rotate(q), rotate(k))
        scale = HD ** (-0.5)
        scores = jnp.einsum('bhid,bhjd->bhij', qr, kr) * scale
        probs = jax.nn.softmax(scores, axis=-1)
        out = jnp.einsum('bhij,bhjd->bhid', probs, v)
        out = out.transpose(0, 2, 1, 3).reshape(b, n, INNER)
        return out @ w_out + b_out

    def _L1_ffn_ref(x, w1_w, w1_s, w2_w, w2_s, h1_w, h1_s, h2_w, h2_s, w3_w, w3_s):
        import jax, jax.numpy as jnp
        import numpy as np
        D_IN, D_HID = (128, 512)

        def _ternary(key, shape):
            return jax.random.randint(key, shape, -1, 2).astype(jnp.float32)

        def _tlin(x, w, s):
            return jnp.einsum('bsi,oi->bso', x, w) * s
        h = jax.nn.silu(_tlin(x, w1_w, w1_s)) * _tlin(x, w2_w, w2_s)
        h = jax.nn.gelu(_tlin(h, h1_w, h1_s), approximate=False)
        h = jax.nn.gelu(_tlin(h, h2_w, h2_s), approximate=False)
        return _tlin(h, w3_w, w3_s)
    x = L0_attn_x
    xn = _layernorm(x, axis=-1)
    x = x + _L0_attn_ref(xn, L0_attn_w_qkv, L0_attn_b_qkv, L0_attn_w_out, L0_attn_b_out) + _L0_ffn_ref(xn, L0_ffn_w_gate, L0_ffn_w_up, L0_ffn_w_down)
    xn = _layernorm(x, axis=-1)
    x = x + _L1_attn_ref(xn, L1_attn_ln_gamma, L1_attn_ln_beta, L1_attn_w_qkv, L1_attn_w_out, L1_attn_b_out) + _L1_ffn_ref(xn, L1_ffn_w1_w, L1_ffn_w1_s, L1_ffn_w2_w, L1_ffn_w2_s, L1_ffn_h1_w, L1_ffn_h1_s, L1_ffn_h2_w, L1_ffn_h2_s, L1_ffn_w3_w, L1_ffn_w3_s)
    return x

_drawn_inputs = setup_inputs


def setup_inputs(seed=0):
    import zlib

    import numpy as np

    out = dict(_drawn_inputs(seed))
    spreads = {'L0_attn_b_qkv': (0.0, 0.1),
     'L0_attn_b_out': (0.0, 0.1),
     'L1_attn_ln_gamma': (1.0, 0.2),
     'L1_attn_ln_beta': (0.0, 0.1),
     'L1_attn_b_out': (0.0, 0.1)}
    factors = {}
    for name, (base, spread) in spreads.items():
        noise = np.random.default_rng([zlib.crc32(name.encode()), seed]).standard_normal(out[name].shape)
        drawn = base * np.exp(spread * noise) if base else spread * noise
        out[name] = jnp.asarray(drawn.astype(out[name].dtype))
    for name, factor in factors.items():
        out[name] = (out[name] * factor).astype(out[name].dtype)
    return out
```

```python
from contextlib import ExitStack
import math

import concourse.bass as bass
from concourse import mybir

ALU = mybir.AluOpType
ACT = mybir.ActivationFunctionType
AX = mybir.AxisListType
F32 = mybir.dt.float32
BF16 = mybir.dt.bfloat16
F16 = mybir.dt.float16
I32 = mybir.dt.int32

P = 128
S = 2048
D = 128
NT = S // P
BANK = 512
NCH = S // BANK
H = 16

HD0 = D // H
F0 = 384
M0 = F0 // P
DEQ = 1.0 / 127.0
NPART = 3
KST = NPART * NPART * HD0
CLIP = 1.0 - 1e-7
GEXP = -3.2
HALF_PI = math.pi / 2
BT = 8
NC = 4
VC = 32

HD1 = 64
INNER = H * HD1
F1 = 512
M1 = F1 // P
QS = 16.0
MROW = 2048.0
SM = 1.0 / (math.sqrt(HD1) * QS * QS)
SC = 1024
NS = S // SC
NP_ = 4


def stage_project0(nc, io, sb):
    v0, base, ident, ident_b = sb["v0"], sb["base"], sb["ident"], sb["ident_b"]
    with ExitStack() as ctx:
        def t(name, shape, dt=F32):
            return ctx.enter_context(nc.sbuf_tensor(name, shape, dt))

        def sem(name):
            return ctx.enter_context(nc.semaphore(name))

        x_in = t("x_in", [P, NT, D])
        xn = t("xn0", [P, NT, D])
        xnT = t("xnT0", [P, S])
        stats = t("stats0", [P, NT, 6])
        mv = t("mv0", [P, NT, 2])
        var = t("var0", [P, NT])
        sd = t("sd0", [P, NT])
        tmp = t("tmp0", [P, NT])
        w_qkv = t("w_qkv0", [P, 3 * D])
        b_qkv = t("b_qkv0", [P, 3 * D])
        wg_i = t("wg_i", [P, F0], I32)
        wu_i = t("wu_i", [P, F0], I32)
        wd_i = t("wd_i", [P, M0, D], I32)
        wg = t("wg", [P, F0])
        wu = t("wu", [P, F0])
        wd = t("wd", [P, M0, D])
        qk = t("qk0", [P, NT, 2 * D])
        sq = t("sq0", [P, NT, 2 * D])
        n2 = t("n2", [P, NT * 2 * H])
        nrm = t("nrm", [P, NT * 2 * H])
        ntmp = t("ntmp", [P, NT * 2 * H])
        parts = t("parts", [P, NPART, NT, 2 * D], BF16)
        stg = t("stg", [P, NPART, 2, S], BF16)
        hT = t("hT0", [P, M0, S])
        sil = t("sil0", [P, 2, BANK])
        psT = ctx.enter_context(nc.psum_tensor("psT0", [P, 2, BANK], F32))
        psQ = ctx.enter_context(nc.psum_tensor("psQ0", [P, 2, BANK], F32))
        psG = ctx.enter_context(nc.psum_tensor("psG0", [P, 2, BANK], F32))
        psU = ctx.enter_context(nc.psum_tensor("psU0", [P, 2, BANK], F32))

        x_loaded, w_loaded = sem("x_loaded0"), sem("w_loaded0")
        wq_loaded = sem("wq_loaded0")
        dve = sem("dve_chain0")
        var_ready, sd_ready, xn_ready = sem("var_ready0"), sem("sd_ready0"), sem("xn_ready0")
        w_cast = sem("w_cast0")
        xT_ps, xT_ready = sem("xT_ps0"), sem("xT_ready0")
        qkv_ps, qkv_taken = sem("qkv_ps0"), sem("qkv_taken0")
        n2_ready, nrm_ready, parts_ready = sem("n2_ready"), sem("nrm_ready"), sem("parts_ready")
        gate_ps, up_ps, sil_ready, h_ready = sem("gate_ps0"), sem("up_ps0"), sem("sil_ready0"), sem("h_ready0")
        pt_ps, pt_ready, stacks_stored = sem("pt_ps"), sem("pt_ready"), sem("stacks_stored")
        down_ps, base_ready = sem("down_ps0"), sem("base_ready0")
        psTb = psT[:, :, :].rearrange("p a b -> p (a b)").bitcast(BF16).rearrange("p (a b) -> p a b", a=2)

        with nc.Block() as block:
            @block.sync
            def _(sp):
                sp.dma_start(x_in[:, :, :], io["x"].rearrange("a (n p) d -> p (a n) d", p=P)).then_inc(x_loaded, 16)
                sp.dma_start(ident[:, :], io["ident"]).then_inc(wq_loaded, 16)
                sp.dma_start(w_qkv[:, :], io["w_qkv0_t"]).then_inc(wq_loaded, 16)
                sp.dma_start(b_qkv[:, :], io["b_qkv0"].partition_broadcast(P)).then_inc(wq_loaded, 16)
                sp.dma_start(wg_i[:, :], io["w_gate_t"]).then_inc(w_loaded, 16)
                sp.dma_start(wu_i[:, :], io["w_up_t"]).then_inc(w_loaded, 16)
                sp.dma_start(wd_i[:, :, :], io["w_down_t"].rearrange("(m p) d -> p m d", p=P)).then_inc(w_loaded, 16)
                for i in range(NPART):
                    for x in range(2):
                        sp.wait_ge(pt_ready, 2 * (2 * i + x) + 2)
                        for j in range(NPART):
                            row = HD0 * (NPART * j + i if x == 0 else NPART * i + j)
                            for h in range(H):
                                sp.dma_start(io["stacks"][x, h, row:row + HD0, :],
                                             stg[HD0 * h:HD0 * h + HD0, i, x, :]).then_inc(stacks_stored, 16)
                sp.wait_ge(stacks_stored, 16 * 2 * NPART * NPART * H)

            @block.vector
            def _(eng):
                n = [0]

                def link(ins):
                    n[0] += 1
                    ins.then_inc(dve, 1)
                    eng.wait_ge(dve, n[0])

                eng.wait_ge(x_loaded, 16)
                for k in range(NT):
                    last = eng.bn_stats(stats[:, k, :], x_in[:, k, :])
                link(last)
                for k in range(NT):
                    last = eng.bn_aggr(mv[:, k, :], stats[:, k, :])
                link(last)
                eng.tensor_scalar(var[:, :], mv[:, :, 1], 1e-5, None, ALU.add).then_inc(var_ready, 1)
                eng.wait_ge(sd_ready, 1)
                link(eng.reciprocal(tmp[:, :], sd[:, :]))
                link(eng.tensor_tensor(tmp[:, :], tmp[:, :], var[:, :], ALU.mult))
                link(eng.tensor_tensor(tmp[:, :], tmp[:, :], sd[:, :], ALU.add))
                link(eng.reciprocal(tmp[:, :], tmp[:, :]))
                link(eng.tensor_scalar(tmp[:, :], tmp[:, :], 2.0, None, ALU.mult))
                for k in range(NT):
                    eng.tensor_scalar(xn[:, k, :], x_in[:, k, :], mv[:, k, 0:1], tmp[:, k:k + 1],
                                      ALU.subtract, ALU.mult).then_inc(xn_ready, 1)
                eng.wait_ge(wq_loaded, 48)
                eng.tensor_copy(ident_b[:, :], ident[:, :])
                eng.wait_ge(w_loaded, 48)
                eng.tensor_copy(wg[:, :], wg_i[:, :])
                eng.tensor_copy(wu[:, :], wu_i[:, :])
                eng.tensor_copy(wd[:, :, :], wd_i[:, :, :]).then_inc(w_cast, 1)
                for k in range(NT):
                    eng.wait_ge(qkv_ps, k + 1)
                    eng.tensor_tensor(qk[:, k, :], psQ[:, k % 2, 0:2 * D], b_qkv[:, 0:2 * D], ALU.add)
                    last = eng.tensor_tensor(v0[:, k, :], psQ[:, k % 2, 2 * D:3 * D], b_qkv[:, 2 * D:3 * D], ALU.add)
                    last.then_inc(qkv_taken, 1)
                eng.wait_ge(qkv_taken, NT)
                link(eng.tensor_tensor(sq[:, :, :], qk[:, :, :], qk[:, :, :], ALU.mult))
                groups = sq[:, :, :].rearrange("p n (g d) -> p (n g) d", d=HD0)
                eng.tensor_reduce(n2[:, :], groups, AX.X, ALU.add).then_inc(n2_ready, 1)
                eng.wait_ge(nrm_ready, 1)
                link(eng.tensor_scalar(nrm[:, :], nrm[:, :], 1e-30, None, ALU.max))
                link(eng.reciprocal(ntmp[:, :], nrm[:, :]))
                link(eng.tensor_tensor(ntmp[:, :], ntmp[:, :], n2[:, :], ALU.mult))
                link(eng.tensor_tensor(ntmp[:, :], ntmp[:, :], nrm[:, :], ALU.add))
                link(eng.tensor_scalar(ntmp[:, :], ntmp[:, :], 0.5, 1e-12, ALU.mult, ALU.max))
                link(eng.reciprocal(nrm[:, :], ntmp[:, :]))
                spread = nrm[:, :].unsqueeze(2).to_broadcast([P, NT * 2 * H, HD0])
                qk_g = qk[:, :, :].rearrange("p n (g d) -> p (n g) d", d=HD0)
                link(eng.tensor_tensor(groups, qk_g, spread, ALU.mult))
                link(eng.tensor_copy(parts[:, 0, :, :], sq[:, :, :]))
                link(eng.tensor_tensor(qk[:, :, :], sq[:, :, :], parts[:, 0, :, :], ALU.subtract))
                link(eng.tensor_copy(parts[:, 1, :, :], qk[:, :, :]))
                eng.tensor_tensor(parts[:, 2, :, :], qk[:, :, :], parts[:, 1, :, :], ALU.subtract)\
                   .then_inc(parts_ready, 1)
                for k in range(NCH * M0):
                    n_, m = k // M0, k % M0
                    eng.wait_ge(up_ps, k + 1)
                    eng.wait_ge(sil_ready, k + 1)
                    eng.scalar_tensor_tensor(out=hT[:, m, n_ * BANK:(n_ + 1) * BANK], in0=psU[:, k % 2, :],
                                             scalar=DEQ, in1=sil[:, k % 2, :], op0=ALU.mult,
                                             op1=ALU.mult).then_inc(h_ready, 1)
                for k in range(NT):
                    eng.wait_ge(down_ps, k + 1)
                    eng.scalar_tensor_tensor(out=base[:, k, :], in0=psQ[:, k % 2, 0:D], scalar=DEQ,
                                             in1=x_in[:, k, :], op0=ALU.mult, op1=ALU.add).then_inc(base_ready, 1)

            @block.scalar
            def _(eng):
                eng.wait_ge(var_ready, 1)
                eng.activation(sd[:, :], var[:, :], ACT.Sqrt).then_inc(sd_ready, 1)
                for g in range(NCH):
                    eng.wait_ge(xT_ps, g + 1)
                    eng.activation(xnT[:, g * BANK:(g + 1) * BANK], psT[:, g % 2, :], ACT.Copy).then_inc(xT_ready, 1)
                eng.wait_ge(n2_ready, 1)
                eng.activation(nrm[:, :], n2[:, :], ACT.Sqrt).then_inc(nrm_ready, 1)
                for k in range(NCH * M0):
                    eng.wait_ge(gate_ps, k + 1)
                    if k >= 2:
                        eng.wait_ge(h_ready, k - 1)
                    eng.activation(sil[:, k % 2, :], psG[:, k % 2, :], ACT.Silu, scale=DEQ).then_inc(sil_ready, 1)
                for k in range(2 * NPART * 2):
                    i, x, g = k // 4, k // 2 % 2, k % 2
                    eng.wait_ge(pt_ps, k + 1)
                    eng.activation(stg[:, i, x, g * 1024:(g + 1) * 1024], psTb[:, k % 2, :],
                                   ACT.Copy).then_inc(pt_ready, 1)

            @block.tensor
            def _(eng):
                eng.wait_ge(wq_loaded, 48)
                for g in range(NCH):
                    if g >= 2:
                        eng.wait_ge(xT_ready, g - 1)
                    for j in range(4):
                        k = 4 * g + j
                        eng.wait_ge(xn_ready, k + 1)
                        mm = eng.transpose(psT[:, g % 2, j * P:(j + 1) * P], xn[:, k, :], ident[:, :])
                    mm.then_inc(xT_ps, 1)
                for k in range(NT):
                    if k % 4 == 0:
                        eng.wait_ge(xT_ready, k // 4 + 1)
                    if k >= 2:
                        eng.wait_ge(qkv_taken, k - 1)
                    eng.matmul(psQ[:, k % 2, 0:3 * D], xnT[:, k * P:(k + 1) * P], w_qkv[:, :],
                               start=True, stop=True).then_inc(qkv_ps, 1)
                eng.wait_ge(w_cast, 1)
                for k in range(NCH * M0):
                    n_, m = k // M0, k % M0
                    rhs = xnT[:, n_ * BANK:(n_ + 1) * BANK]
                    if k >= 2:
                        eng.wait_ge(sil_ready, k - 1)
                        eng.wait_ge(h_ready, k - 1)
                    eng.matmul(psG[:, k % 2, :], wg[:, m * P:(m + 1) * P], rhs, start=True, stop=True)\
                       .then_inc(gate_ps, 1)
                    eng.matmul(psU[:, k % 2, :], wu[:, m * P:(m + 1) * P], rhs, start=True, stop=True)\
                       .then_inc(up_ps, 1)
                eng.wait_ge(parts_ready, 1)
                for k in range(2 * NPART * 2):
                    i, x, g = k // 4, k // 2 % 2, k % 2
                    if k >= 2:
                        eng.wait_ge(pt_ready, k - 1)
                    for j in range(8):
                        mm = eng.transpose(psTb[:, k % 2, j * P:(j + 1) * P],
                                           parts[:, i, 8 * g + j, x * D:(x + 1) * D], ident_b[:, :])
                    mm.then_inc(pt_ps, 1)
                eng.wait_ge(h_ready, NCH * M0)
                for k in range(NT):
                    if k >= 2:
                        eng.wait_ge(base_ready, k - 1)
                    for m in range(M0):
                        mm = eng.matmul(psQ[:, k % 2, 0:D], hT[:, m, k * P:(k + 1) * P], wd[:, m, :],
                                        start=(m == 0), stop=(m == M0 - 1))
                    mm.then_inc(down_ps, 1)


def stage_attention0(nc, io, sb):
    v0, attn0, ident = sb["v0"], sb["attn0"], sb["ident"]
    with ExitStack() as ctx:
        def t(name, shape, dt=F32):
            return ctx.enter_context(nc.sbuf_tensor(name, shape, dt))

        def sem(name):
            return ctx.enter_context(nc.semaphore(name))

        qst = t("qst", [KST, S], BF16)
        kst = t("kst", [KST, S], BF16)
        cosr = t("cosr", [P, NC, S])
        wk = t("wk", [P, NT, S])
        n_c = t("n_c", [P, NT])
        r_c = t("r_c", [P, NT])
        vh = t("vh", [P, NT, VC])
        o_sb = t("o_sb", [P, BANK])
        small = t("small0", [P, NT, 4])
        quarter_bias = t("bias_theta", [P, 1])
        c_ps = ctx.enter_context(nc.psum_tensor("c_ps", [P, 2, 2 * BANK], F32))
        o_ps = ctx.enter_context(nc.psum_tensor("o_ps", [P, BANK], F32))
        t_ps = ctx.enter_context(nc.psum_tensor("t_ps", [P, 4, P], F32))

        stacks_loaded, cos_ps, cos_ready = sem("stacks_loaded"), sem("cos_ps"), sem("cos_ready")
        logs_ready, diff_ready = sem("logs_ready"), sem("diff_ready")
        tanh_ready, atan_ready = sem("tanh_ready"), sem("atan_ready")
        lnth_ready, score_ready = sem("lnth_ready"), sem("score_ready")
        rc_ready, vh_ready, pv_done = sem("rc_ready"), sem("vh_ready"), sem("pv_done")
        o_copied, o_turned, attn_ready = sem("o_copied"), sem("o_turned"), sem("attn_ready")
        dve, ones_ready = sem("dve_chain_b"), sem("ones_ready")
        rows_done = sem("rows_done")

        with nc.Block() as block:
            @block.sync
            def _(sp):
                with sp.Fori(0, H) as h:
                    sp.wait_ge(cos_ps, 2 * NT * h + 2)
                    sp.dma_start(qst[:, :], io["stacks"][0, h, :, :]).then_inc(stacks_loaded, 16)
                    sp.dma_start(kst[:, :], io["stacks"][1, h, :, :]).then_inc(stacks_loaded, 16)

            @block.vector
            def _(eng):
                n = [0]

                def link(ins):
                    n[0] += 1
                    ins.then_inc(dve, 1)
                    eng.wait_ge(dve, n[0])

                eng.memset(quarter_bias[:, :], 1.0 + HALF_PI)
                eng.memset(vh[:, :, HD0 + 2:VC], 0.0)
                eng.memset(vh[:, :, HD0 + 1:HD0 + 2], 1.0).then_inc(ones_ready, 1)

                def clip(h, k):
                    for j in range(2):
                        eng.wait_ge(cos_ps, 2 * NT * h + 2 * k + j + 3)
                        eng.tensor_scalar(cosr[:, k % NC, j * 2 * BANK:(j + 1) * 2 * BANK],
                                          c_ps[:, j, :], CLIP, -CLIP, ALU.min, ALU.max).then_inc(cos_ready, 1)

                def difference(h, k):
                    eng.wait_ge(logs_ready, NT * h + k + 1)
                    eng.tensor_tensor(wk[:, k, :], wk[:, k, :], cosr[:, k % NC, :], ALU.subtract)\
                       .then_inc(diff_ready, 1)

                def values(h, k):
                    eng.wait_ge(score_ready, NT * h + k + 1)
                    eng.wait_ge(pv_done, NT * h + k + 1)
                    eng.reciprocal(r_c[:, k:k + 1], n_c[:, k:k + 1]).then_inc(rc_ready, 1)
                    eng.wait_ge(rc_ready, NT * h + k + 1)
                    eng.tensor_copy(vh[:, k, HD0:HD0 + 1], r_c[:, k:k + 1])
                    eng.tensor_scalar(vh[:, k, 0:HD0], v0[:, k, bass.ds(h * HD0, HD0)], r_c[:, k:k + 1], None,
                                      ALU.mult).then_inc(vh_ready, 1)

                def finish(h):
                    eng.wait_ge(pv_done, NT * (h + 2))
                    eng.tensor_copy(o_sb[:, :], o_ps[:, :]).then_inc(o_copied, 1)
                    eng.wait_ge(o_turned, h + 1)
                    rows = t_ps[:, :, :].rearrange("p j (c r) -> p c j r", r=VC)
                    quad = small[:, :, :].rearrange("p (c j) r -> p c j r", j=4)
                    eng.reciprocal(quad[:, :, :, 0:1], rows[:, :, :, HD0 + 1:HD0 + 2]).then_inc(rows_done, 1)
                    eng.wait_ge(rows_done, h * 5 + 1)
                    eng.tensor_tensor(quad[:, :, :, 1:2], rows[:, :, :, HD0:HD0 + 1], quad[:, :, :, 0:1],
                                      ALU.mult).then_inc(rows_done, 1)
                    eng.wait_ge(rows_done, h * 5 + 2)
                    eng.tensor_scalar(small[:, :, 1:2], small[:, :, 1:2], 1e-12, None, ALU.max).then_inc(rows_done, 1)
                    eng.wait_ge(rows_done, h * 5 + 3)
                    eng.reciprocal(small[:, :, 2:3], small[:, :, 1:2]).then_inc(rows_done, 1)
                    eng.wait_ge(rows_done, h * 5 + 4)
                    eng.tensor_tensor(small[:, :, 3:4], small[:, :, 2:3], small[:, :, 0:1], ALU.mult)\
                       .then_inc(rows_done, 1)
                    eng.wait_ge(rows_done, h * 5 + 5)
                    for c in range(4):
                        last = eng.tensor_tensor(attn0[:, 4 * c:4 * c + 4, bass.ds(h * HD0, HD0)],
                                          t_ps[:, :, VC * c:VC * c + HD0],
                                          small[:, 4 * c:4 * c + 4, 3:4].to_broadcast([P, 4, HD0]), ALU.mult)
                    last.then_inc(attn_ready, 1)

                def round_(h, b, last=False):
                    hn, k0 = (h, BT) if b == 0 else (h + 1, 0)
                    if not last:
                        clip(hn, k0)
                        clip(hn, k0 + 1)
                    for i in range(BT):
                        values(h, b * BT + i)
                    for i in range(BT):
                        if not last and i + 2 < BT:
                            clip(hn, k0 + i + 2)
                        if not last:
                            difference(hn, k0 + i)
                        if b == 1 and i == BT - 2:
                            finish(h)

                clip(0, 0)
                clip(0, 1)
                for i in range(BT):
                    if i + 2 < BT:
                        clip(0, i + 2)
                    difference(0, i)
                eng.wait_ge(ones_ready, 1)
                with eng.Fori(0, H - 1) as h:
                    round_(h, 0)
                    round_(h, 1)
                round_(H - 1, 0)
                round_(H - 1, 1, last=True)

            @block.scalar
            def _(eng):
                def logs(h, k):
                    eng.wait_ge(cos_ready, 2 * NT * h + 2 * k + 4)
                    eng.wait_ge(pv_done, NT * h + k + 1)
                    eng.activation(wk[:, k, :], cosr[:, k % NC, :], ACT.Ln, bias=1.0, scale=1.0)
                    eng.activation(cosr[:, k % NC, :], cosr[:, k % NC, :], ACT.Ln, bias=1.0, scale=-1.0)\
                       .then_inc(logs_ready, 1)

                def round_(h, b, last=False):
                    k0 = b * BT
                    g0 = 4 * h + 2 * b
                    eng.preload_act_table_set("sigmoid_and_others")
                    for g in range(2):
                        ks = slice(k0 + 4 * g, k0 + 4 * g + 4)
                        eng.wait_ge(diff_ready, NT * h + k0 + 4 * g + 4)
                        eng.activation(wk[:, ks, :], wk[:, ks, :], ACT.Tanh, scale=0.25).then_inc(tanh_ready, 1)
                    for g in range(2):
                        ks = slice(k0 + 4 * g, k0 + 4 * g + 4)
                        eng.wait_ge(tanh_ready, g0 + g + 1)
                        eng.activation(wk[:, ks, :], wk[:, ks, :], ACT.Arctan).then_inc(atan_ready, 1)
                    eng.preload_act_table_set("natural_log_exp_and_others")
                    for g in range(2):
                        ks = slice(k0 + 4 * g, k0 + 4 * g + 4)
                        eng.wait_ge(atan_ready, g0 + g + 1)
                        eng.activation(wk[:, ks, :], wk[:, ks, :], ACT.Ln, scale=-2.0,
                                       bias=quarter_bias[:, 0:1]).then_inc(lnth_ready, 1)
                    for i in range(BT):
                        k = k0 + i
                        if i % 4 == 0:
                            eng.wait_ge(lnth_ready, g0 + i // 4 + 1)
                        eng.wait_ge(vh_ready, NT * h + k + 1)
                        eng.activation(wk[:, k, :], wk[:, k, :], ACT.Exp, scale=GEXP,
                                       accum_out=n_c[:, k:k + 1]).then_inc(score_ready, 1)
                    if not last:
                        hn, kn = (h, BT) if b == 0 else (h + 1, 0)
                        for i in range(BT):
                            logs(hn, kn + i)

                eng.preload_act_table_set("natural_log_exp_and_others")
                eng.wait_ge(ones_ready, 1)
                for i in range(BT):
                    logs(0, i)
                with eng.Fori(0, H - 1) as h:
                    round_(h, 0)
                    round_(h, 1)
                round_(H - 1, 0)
                round_(H - 1, 1, last=True)

            @block.tensor
            def _(eng):
                def cosines(h, k):
                    if k == 0:
                        eng.wait_ge(stacks_loaded, 32 * h + 32)
                    for j in range(2):
                        eng.wait_ge(cos_ready, 2 * NT * h + 2 * k + j + 1)
                        for c in range(2):
                            n_ = 2 * j + c
                            mm = eng.matmul(c_ps[:, j, c * BANK:(c + 1) * BANK], kst[:, k * P:(k + 1) * P],
                                            qst[:, n_ * BANK:(n_ + 1) * BANK], start=True, stop=True)
                        mm.then_inc(cos_ps, 1)

                def weigh(h, k):
                    if k == 0:
                        eng.wait_ge(o_copied, h + 1)
                    eng.wait_ge(vh_ready, NT * (h + 1) + k + 1)
                    for c in range(NCH):
                        mm = eng.matmul(o_ps[VC * c:VC * (c + 1), :], vh[:, k, :],
                                        wk[:, k, c * BANK:(c + 1) * BANK], start=(k == 0), stop=(k == NT - 1))
                    mm.then_inc(pv_done, 1)

                def turn(h):
                    eng.wait_ge(o_copied, h + 2)
                    eng.wait_ge(attn_ready, h + 1)
                    for j in range(4):
                        mm = eng.transpose(t_ps[:, j, :], o_sb[:, j * P:(j + 1) * P], ident[:, :])
                    mm.then_inc(o_turned, 1)

                def round_(h, b, last=False):
                    hn, kn = (h, BT) if b == 0 else (h + 1, 0)
                    k0 = b * BT
                    if not last:
                        cosines(hn, kn)
                        cosines(hn, kn + 1)
                    for i in range(4):
                        weigh(h, k0 + i)
                    for i in range(4):
                        if not last:
                            cosines(hn, kn + 2 + i)
                        weigh(h, k0 + 4 + i)
                    if not last:
                        cosines(hn, kn + 6)
                        cosines(hn, kn + 7)
                    if b == 1:
                        turn(h)

                eng.sem_inc(pv_done, NT)
                eng.sem_inc(vh_ready, NT)
                eng.sem_inc(cos_ready, 2)
                eng.sem_inc(cos_ps, 2)
                eng.sem_inc(o_copied, 1)
                eng.sem_inc(attn_ready, 1)
                for i in range(BT):
                    cosines(0, i)
                with eng.Fori(0, H - 1) as h:
                    round_(h, 0)
                    round_(h, 1)
                round_(H - 1, 0)
                round_(H - 1, 1, last=True)




def norm_on_vector(eng, link, src, dst, stats, mv, var, sd, tmp, var_ready, sd_ready, n):
    for k in range(NT):
        last = eng.bn_stats(stats[:, k, :], src[:, k, :])
    link(last)
    for k in range(NT):
        last = eng.bn_aggr(mv[:, k, :], stats[:, k, :])
    link(last)
    eng.tensor_scalar(var[:, :], mv[:, :, 1], 1e-5, None, ALU.add).then_inc(var_ready, 1)
    eng.wait_ge(sd_ready, n)
    link(eng.reciprocal(tmp[:, :], sd[:, :]))
    link(eng.tensor_tensor(tmp[:, :], tmp[:, :], var[:, :], ALU.mult))
    link(eng.tensor_tensor(tmp[:, :], tmp[:, :], sd[:, :], ALU.add))
    link(eng.reciprocal(tmp[:, :], tmp[:, :]))
    link(eng.tensor_scalar(tmp[:, :], tmp[:, :], 2.0, None, ALU.mult))
    for k in range(NT):
        last = eng.tensor_scalar(dst[:, k, :], src[:, k, :], mv[:, k, 0:1], tmp[:, k:k + 1],
                                 ALU.subtract, ALU.mult)
    link(last)


def stage_project1(nc, io, sb):
    base, attn0, ident, xn2T = sb["base"], sb["attn0"], sb["ident"], sb["xn2T"]
    HB = 8
    HALF = HD1 // 2
    with ExitStack() as ctx:
        def t(name, shape, dt=F32):
            return ctx.enter_context(nc.sbuf_tensor(name, shape, dt))

        def sem(name):
            return ctx.enter_context(nc.semaphore(name))

        attn0T = t("attn0T", [P, S])
        xn = t("xn2", [P, NT, D])
        xa = t("xa", [P, NT, D])
        xaT = attn0T
        stats, mv = t("stats1", [P, NT, 6]), t("mv1", [P, NT, 2])
        var, sd, tmp = t("var1", [P, NT]), t("sd1", [P, NT]), t("tmp1", [P, NT])
        w_out, b_out = t("w_out0", [P, D]), t("b_out0", [P, D])
        gamma, beta, b_out1 = t("gamma", [P, D]), t("beta", [P, D]), t("b_out1", [P, D])
        w_qkv = t("w_qkv1", [P, 3 * INNER])
        cos_t, sin_t = t("cos_t", [P, NT, HALF]), t("sin_t", [P, NT, 2, HALF])
        ident_h = t("ident_h", [P, P], F16)
        ra, rb = t("ra", [P, 2, BANK]), t("rb", [P, 2, BANK])
        hl = t("hl", [P, 2, 2 * H, 2, HD1], F16)
        v_st = t("v_st", [P, 2, INNER])
        stg = t("stg1", [P, 2, 2 * H, BANK], F16)
        psA = ctx.enter_context(nc.psum_tensor("psA1", [P, 2, BANK], F32))
        psR = ctx.enter_context(nc.psum_tensor("psR1", [P, 4, BANK], F32))
        psB = ctx.enter_context(nc.psum_tensor("psB1", [P, 2, 2 * BANK], F16))

        loaded, dve = sem("loaded1"), sem("dve_chain1")
        turned, taken = sem("turned1"), sem("taken1")
        out_ps, x1_ready = sem("out_ps1"), sem("x1_ready")
        var_ready, sd_ready = sem("var_ready1"), sem("sd_ready1")
        xn_ready, xa_ready = sem("xn_ready1"), sem("xa_ready1")
        qkv_ps, rope_read, v_read = sem("qkv_ps1"), sem("rope_read"), sem("v_read")
        rot_ready, hi_ready, lo_ready = sem("rot_ready"), sem("hi_ready"), sem("lo_ready")
        hl_ps, hl_taken = sem("hl_ps"), sem("hl_taken")
        v_stored = [sem("v_stored_0"), sem("v_stored_1")]
        qk_stored = [sem("qk_stored_0"), sem("qk_stored_1")]

        with nc.Block() as block:
            @block.sync
            def _(sp):
                for dst, src in ((w_out[:, :], io["w_out0_t"]), (b_out[:, :], io["b_out0"].partition_broadcast(P)),
                                 (gamma[:, :], io["gamma"].partition_broadcast(P)),
                                 (beta[:, :], io["beta"].partition_broadcast(P)),
                                 (b_out1[:, :], io["b_out1"].partition_broadcast(P)),
                                 (w_qkv[:, :], io["w_qkv1"]),
                                 (cos_t[:, :, :], io["cos_t"].rearrange("(n p) f -> p n f", p=P)),
                                 (sin_t[:, :, :, :], io["sin_t"].rearrange("(n p) a f -> p n a f", p=P))):
                    sp.dma_start(dst, src).then_inc(loaded, 16)
                for k in range(NT):
                    sp.wait_ge(v_read, 2 * k + 2)
                    sp.dma_start(io["v1"][k * P:(k + 1) * P, :], v_st[:, k % 2, :]).then_inc(v_stored[k % 2], 16)
                    if k % 4 == 3:
                        n_ = k // 4
                        sp.wait_ge(hl_taken, 4 * (k + 1))
                        for x in range(2):
                            sp.dma_start(io["qk1"][x, :, :, n_ * BANK:(n_ + 1) * BANK].rearrange("h p t -> p h t"),
                                         stg[:, n_ % 2, x * H:(x + 1) * H, :]).then_inc(qk_stored[n_ % 2], 16)
                for slot in range(2):
                    sp.wait_ge(v_stored[slot], 16 * NT // 2)
                    sp.wait_ge(qk_stored[slot], 32 * NCH // 2)

            @block.vector
            def _(eng):
                n = [0]

                def link(ins):
                    n[0] += 1
                    ins.then_inc(dve, 1)
                    eng.wait_ge(dve, n[0])

                eng.wait_ge(loaded, 16 * 8)
                eng.tensor_copy(ident_h[:, :], ident[:, :])
                link(eng.tensor_tensor(base[:, :, :], base[:, :, :],
                                       b_out[:, :].unsqueeze(1).to_broadcast([P, NT, D]), ALU.add))
                for k in range(NT):
                    eng.wait_ge(out_ps, k + 1)
                    eng.tensor_tensor(base[:, k, :], base[:, k, :], psR[:, k % 4, 0:D], ALU.add).then_inc(x1_ready, 1)
                eng.wait_ge(x1_ready, NT)
                norm_on_vector(eng, link, base, xn, stats, mv, var, sd, tmp, var_ready, sd_ready, 1)
                eng.sem_inc(xn_ready, 1)
                norm_on_vector(eng, link, xn, xa, stats, mv, var, sd, tmp, var_ready, sd_ready, 2)
                link(eng.tensor_tensor(xa[:, :, :], xa[:, :, :], gamma[:, :].unsqueeze(1).to_broadcast([P, NT, D]),
                                       ALU.mult))
                eng.tensor_tensor(xa[:, :, :], xa[:, :, :], beta[:, :].unsqueeze(1).to_broadcast([P, NT, D]),
                                  ALU.add).then_inc(xa_ready, 1)
                eng.tensor_tensor(base[:, :, :], base[:, :, :], b_out1[:, :].unsqueeze(1).to_broadcast([P, NT, D]),
                                  ALU.add)

                for k in range(NT):
                    for b in range(4):
                        u = 4 * k + b
                        src = psR[:, b, :].rearrange("p (h a f) -> p h a f", h=HB, a=2)
                        a_ = ra[:, u % 2, :].rearrange("p (h a f) -> p h a f", h=HB, a=2)
                        b_ = rb[:, u % 2, :].rearrange("p (h a f) -> p h a f", h=HB, a=2)
                        eng.wait_ge(qkv_ps, 6 * k + b + 1)
                        if u >= 2:
                            eng.wait_ge(lo_ready, u - 1)
                        for a in range(2):
                            eng.tensor_tensor(a_[:, :, a, :], src[:, :, a, :],
                                              cos_t[:, k, :].unsqueeze(1).to_broadcast([P, HB, HALF]), ALU.mult)
                        eng.tensor_tensor(b_[:, :, 0, :], src[:, :, 1, :],
                                          sin_t[:, k, 0, :].unsqueeze(1).to_broadcast([P, HB, HALF]), ALU.mult)
                        eng.tensor_tensor(b_[:, :, 1, :], src[:, :, 0, :],
                                          sin_t[:, k, 1, :].unsqueeze(1).to_broadcast([P, HB, HALF]), ALU.mult)\
                           .then_inc(rope_read, 1)
                        eng.wait_ge(rope_read, u + 1)
                        if u >= 1:
                            low_half(eng, hl, ra, rb, u - 1, hi_ready, lo_ready)
                        eng.tensor_tensor(ra[:, u % 2, :], ra[:, u % 2, :], rb[:, u % 2, :], ALU.add)\
                           .then_inc(rot_ready, 1)
                        if u == 4 * NT - 1:
                            low_half(eng, hl, ra, rb, u, hi_ready, lo_ready)

            @block.scalar
            def _(eng):
                for g in range(NCH):
                    eng.wait_ge(turned, g + 1)
                    eng.activation(attn0T[:, g * BANK:(g + 1) * BANK], psA[:, g % 2, :], ACT.Copy).then_inc(taken, 1)
                for i in range(2):
                    eng.wait_ge(var_ready, i + 1)
                    eng.activation(sd[:, :], var[:, :], ACT.Sqrt).then_inc(sd_ready, 1)
                    for g in range(NCH):
                        eng.wait_ge(turned, NCH * (i + 1) + g + 1)
                        dst = (xn2T, xaT)[i]
                        eng.activation(dst[:, g * BANK:(g + 1) * BANK], psA[:, g % 2, :], ACT.Copy).then_inc(taken, 1)
                for k in range(NT + 1):
                    if k < NT:
                        for b in range(4):
                            u = 4 * k + b
                            eng.wait_ge(rot_ready, u + 1)
                            if k >= 2:
                                eng.wait_ge(hl_ps, 4 * (k - 1))
                            eng.activation(hl[:, k % 2, b * HB:(b + 1) * HB, 0, :],
                                           ra[:, u % 2, :].rearrange("p (h e) -> p h e", h=HB),
                                           ACT.Copy).then_inc(hi_ready, 1)
                        for b in range(2):
                            eng.wait_ge(qkv_ps, 6 * k + 5 + b)
                            if k >= 2:
                                eng.wait_ge(v_stored[k % 2], 16 * (k // 2))
                            eng.activation(v_st[:, k % 2, b * BANK:(b + 1) * BANK], psA[:, b, :], ACT.Copy)\
                               .then_inc(v_read, 1)
                    if k >= 1:
                        kk = k - 1
                        for g in range(4):
                            eng.wait_ge(hl_ps, 4 * kk + g + 1)
                            if kk % 4 == 0 and kk >= 8:
                                eng.wait_ge(qk_stored[kk // 4 % 2], 32 * (kk // 8))
                            eng.activation(stg[:, kk // 4 % 2, g * HB:(g + 1) * HB, kk % 4 * P:(kk % 4 + 1) * P],
                                           psB[:, g % 2, :].rearrange("p (h t) -> p h t", h=HB),
                                           ACT.Copy).then_inc(hl_taken, 1)

            @block.tensor
            def _(eng):
                def turn(src, i):
                    for g in range(NCH):
                        if 4 * i + g >= 2:
                            eng.wait_ge(taken, 4 * i + g - 1)
                        for j in range(4):
                            mm = eng.transpose(psA[:, g % 2, j * P:(j + 1) * P], src[:, 4 * g + j, :], ident[:, :])
                        mm.then_inc(turned, 1)

                eng.wait_ge(loaded, 16 * 8)
                turn(attn0, 0)
                for k in range(NT):
                    if k % 4 == 0:
                        eng.wait_ge(taken, k // 4 + 1)
                    if k >= 4:
                        eng.wait_ge(x1_ready, k - 3)
                    eng.matmul(psR[:, k % 4, 0:D], attn0T[:, k * P:(k + 1) * P], w_out[:, :], start=True, stop=True)\
                       .then_inc(out_ps, 1)
                eng.wait_ge(xn_ready, 1)
                turn(xn, 1)
                eng.wait_ge(xa_ready, 1)
                turn(xa, 2)
                for k in range(NT + 1):
                    if k < NT:
                        if k % 4 == 0:
                            eng.wait_ge(taken, 2 * NCH + k // 4 + 1)
                        if k == 0:
                            eng.wait_ge(taken, 3 * NCH)
                        for b in range(6):
                            if k >= 1:
                                if b < 4:
                                    eng.wait_ge(rope_read, 4 * (k - 1) + b + 1)
                                else:
                                    eng.wait_ge(v_read, 2 * (k - 1) + b - 3)
                            dst = psR[:, b, :] if b < 4 else psA[:, b - 4, :]
                            eng.matmul(dst, xaT[:, k * P:(k + 1) * P], w_qkv[:, b * BANK:(b + 1) * BANK],
                                       start=True, stop=True).then_inc(qkv_ps, 1)
                    if k >= 1:
                        kk = k - 1
                        for g in range(4):
                            eng.wait_ge(lo_ready, 4 * kk + g + 1)
                            if 4 * kk + g >= 2:
                                eng.wait_ge(hl_taken, 4 * kk + g - 1)
                            for j in range(HB):
                                mm = eng.transpose(psB[:, g % 2, j * P:(j + 1) * P],
                                                   hl[:, kk % 2, g * HB + j, :, :].rearrange("p a e -> p (a e)"),
                                                   ident_h[:, :])
                            mm.then_inc(hl_ps, 1)


def low_half(eng, hl, ra, rb, u, hi_ready, lo_ready):
    k, b = u // 4, u % 4
    dst = hl[:, k % 2, b * 8:(b + 1) * 8, :, :]
    eng.wait_ge(hi_ready, u + 1)
    eng.tensor_tensor(dst[:, :, 1, :], ra[:, u % 2, :].rearrange("p (h e) -> p h e", h=8), dst[:, :, 0, :],
                      ALU.subtract).then_inc(lo_ready, 1)


def stage_attention1(nc, io, sb):
    attn1T, ident = sb["attn1T"], sb["ident"]
    STEPS = NS * NT
    NMX = NT * NCH
    MX0, MXS = 6, 3
    with ExitStack() as ctx:
        def t(name, shape, dt=F32):
            return ctx.enter_context(nc.sbuf_tensor(name, shape, dt))

        def sem(name):
            return ctx.enter_context(nc.semaphore(name))

        qa, qb = t("qa", [P, 2, S], F16), t("qb", [P, 2, S], F16)
        ka, kb = t("ka", [P, 2, S], F16), t("kb", [P, 2, S], F16)
        vh = t("vh1", [P, 2, NT, P])
        pr = t("pr", [P, NP_, SC])
        mx4, mx = t("mx4", [P, NT, NCH]), t("mx", [P, NT])
        mrow = t("mrow", [NT, P], F16)
        ob, rden = t("ob", [P, SC]), t("rden", [P, SC])
        s_ps = ctx.enter_context(nc.psum_tensor("s_ps", [P, 2, SC], F32))
        pv_ps = ctx.enter_context(nc.psum_tensor("pv_ps", [P, SC], F32))
        mx_ps = ctx.enter_context(nc.psum_tensor("mx_ps", [P, 2, BANK], F32))

        const_ready, loaded, mrow_loaded = sem("const_ready"), sem("loaded_d"), sem("mrow_loaded")
        mx_done, mx_taken, mx_ready = sem("mx_done"), sem("mx_taken"), sem("mx_ready")
        mt_ps, mt_copied = sem("mt_ps"), sem("mt_copied")
        s_done, exp_done, pv_done1 = sem("s_done"), sem("exp_done"), sem("pv_done1")
        ob_ready, rden_ready, attn_ready1 = sem("ob_ready"), sem("rden_ready"), sem("attn_ready1")
        LOADS = 16 * 6

        def head(g, par):
            return 2 * g + par

        with nc.Block() as block:
            @block.sync
            def _(sp):
                def load(g, par):
                    h = head(g, par)
                    sp.wait_ge(pv_done1, STEPS * (h + 1))
                    q, k = io["qk1"][0], io["qk1"][1]
                    off = HD1 * par
                    for dst, src in ((qa[:, par, :], q[h, :, :]), (ka[0:HD1, par, :], k[h, 0:HD1, :]),
                                     (ka[HD1:P, par, :], k[h, 0:HD1, :]), (qb[0:HD1, par, :], q[h, 0:HD1, :]),
                                     (kb[0:HD1, par, :], k[h, HD1:P, :]),
                                     (vh[:, par, :, off:off + HD1],
                                      io["v1"][:, bass.ds(h * HD1, HD1)].rearrange("(n p) e -> p n e", p=P))):
                        sp.dma_start(dst, src).then_inc(loaded, 16)

                def maxima(g, par):
                    sp.wait_ge(mt_copied, head(g, par) + 2)
                    sp.dma_start(qb[HD1:HD1 + 1, par, :].rearrange("a (n t) -> a n t", t=P),
                                 mrow[:, :]).then_inc(mrow_loaded, 16)

                with sp.Fori(0, H // 2) as g:
                    for par in range(2):
                        load(g, par)
                        maxima(g, par)

            @block.vector
            def _(eng):
                for par in range(2):
                    eng.memset(kb[HD1:HD1 + 1, par, :], MROW)
                    off = HD1 * (1 - par)
                    last = eng.memset(vh[:, par, :, off:off + HD1], 1.0)
                last.then_inc(const_ready, 1)

                def reduce_bank(h, q):
                    eng.wait_ge(mx_done, NMX * h + q + 1)
                    eng.tensor_reduce(mx4[:, q // NCH, q % NCH:q % NCH + 1], mx_ps[:, q % 2, :], AX.X, ALU.max)\
                       .then_inc(mx_taken, 1)

                def maxima(h):
                    eng.wait_ge(mx_taken, NMX * (h + 1) + 2)
                    eng.tensor_reduce(mx[:, :], mx4[:, :, :], AX.X, ALU.max).then_inc(mx_ready, 1)
                    eng.wait_ge(mt_ps, h + 1)
                    eng.wait_ge(mrow_loaded, 16 * h + 16)
                    eng.tensor_scalar(mrow[:, :], mx_ps[0:NT, 0, 0:P], -1.0 / MROW, None, ALU.mult)\
                       .then_inc(mt_copied, 1)

                def take(h, c):
                    eng.wait_ge(attn_ready1, NS * h + c + 1)
                    eng.wait_ge(pv_done1, STEPS * (h + 2) + (c + 1) * NT)
                    eng.tensor_copy(ob[:, :], pv_ps[:, :]).then_inc(ob_ready, 1)

                def invert(h, c, par, i):
                    num, den = HD1 * par, HD1 * (1 - par)
                    eng.wait_ge(ob_ready, NS * h + c + 2)
                    w = slice(i * SC // 4, (i + 1) * SC // 4)
                    eng.reciprocal(rden[num:num + HD1, w], ob[den:den + HD1, w]).then_inc(rden_ready, 1)

                def divide(g, h, c, par):
                    num = HD1 * par
                    eng.wait_ge(rden_ready, 4 * (NS * h + c + 1))
                    eng.tensor_tensor(attn1T[num:num + HD1, bass.ds(g, 1), c * SC:(c + 1) * SC].rearrange("p a t -> p (a t)"),
                                      ob[num:num + HD1, :], rden[num:num + HD1, :], ALU.mult)\
                       .then_inc(attn_ready1, 1)

                def rest(g, par, c):
                    h = head(g, par)
                    take(h, c)
                    for i in range(4):
                        invert(h, c, par, i)
                    divide(g, h, c, par)

                def one(g, par, first=False, last=False):
                    h = head(g, par)
                    if not first:
                        rest(g - 1 if par == 0 else g, 1 - par, NS - 1)
                    if last:
                        rest(g, par, 0)
                        rest(g, par, 1)
                        return
                    cut = MXS * (NT - MX0)
                    for q in range(cut):
                        reduce_bank(h + 1, q)
                    take(h, 0)
                    for q in range(cut, NMX):
                        reduce_bank(h + 1, q)
                        if (q - cut) % 3 == 0 and (q - cut) // 3 < 4:
                            invert(h, 0, par, (q - cut) // 3)
                    divide(g, h, 0, par)
                    maxima(h + 1)

                for q in range(NMX):
                    reduce_bank(0, q)
                maxima(0)
                one(0, 0, first=True)
                one(0, 1)
                with eng.Fori(1, H // 2 - 1) as g:
                    one(g, 0)
                    one(g, 1)
                one(H // 2 - 1, 0)
                one(H // 2 - 1, 1, last=True)

            @block.scalar
            def _(eng):
                eng.preload_act_table(ACT.Exp)

                def exps(h):
                    for i in range(STEPS):
                        eng.wait_ge(s_done, STEPS * h + i + 1)
                        eng.wait_ge(pv_done1, STEPS * (h + 2) + i + 1 - NP_)
                        eng.activation(pr[:, i % NP_, :], s_ps[:, i % 2, :], ACT.Exp, scale=SM).then_inc(exp_done, 1)

                with eng.Fori(0, H) as h:
                    exps(h)

            @block.tensor
            def _(eng):
                def mx_bank(h, par, q):
                    if q == 0:
                        eng.wait_ge(loaded, LOADS * (h + 1))
                        eng.wait_ge(mt_copied, h + 1)
                    eng.wait_ge(mx_taken, NMX * h + q + 1)
                    j, c = q // NCH, q % NCH
                    eng.matmul(mx_ps[:, q % 2, :], qa[:, par, j * P:(j + 1) * P],
                               ka[:, par, c * BANK:(c + 1) * BANK], start=True, stop=True).then_inc(mx_done, 1)

                def mx_turn(h):
                    eng.wait_ge(mx_ready, h + 1)
                    eng.transpose(mx_ps[0:NT, 0, 0:P], mx[:, :], ident[:, :]).then_inc(mt_ps, 1)

                def scores(h, par, i):
                    if i == 0:
                        eng.wait_ge(mrow_loaded, 16 * (h + 2))
                    eng.wait_ge(exp_done, STEPS * h + i + 1)
                    c, k = i // NT, i % NT
                    for n_ in range(2):
                        eng.matmul(s_ps[:, i % 2, n_ * BANK:(n_ + 1) * BANK], ka[:, par, k * P:(k + 1) * P],
                                   qa[:, par, c * SC + n_ * BANK:c * SC + (n_ + 1) * BANK], start=True, stop=False)
                    for n_ in range(2):
                        mm = eng.matmul(s_ps[:, i % 2, n_ * BANK:(n_ + 1) * BANK],
                                        kb[0:HD1 + 1, par, k * P:(k + 1) * P],
                                        qb[0:HD1 + 1, par, c * SC + n_ * BANK:c * SC + (n_ + 1) * BANK],
                                        start=False, stop=True)
                    mm.then_inc(s_done, 1)

                def weigh(h, par, i):
                    c, k = i // NT, i % NT
                    if k == 0:
                        eng.wait_ge(ob_ready, NS * h + c + 1)
                    eng.wait_ge(exp_done, STEPS * h + i + 3)
                    for n_ in range(2):
                        mm = eng.matmul(pv_ps[:, n_ * BANK:(n_ + 1) * BANK], vh[:, par, k, :],
                                        pr[:, i % NP_, n_ * BANK:(n_ + 1) * BANK], start=(k == 0), stop=(k == NT - 1))
                    mm.then_inc(pv_done1, 1)

                def one(g, par, last=False):
                    h = head(g, par)
                    for i in range(STEPS):
                        if i + 1 < STEPS:
                            scores(h, par, i + 1)
                        if not last:
                            for q in range(MXS * (i - MX0), min(MXS * (i - MX0 + 1), NMX)):
                                if q >= 0:
                                    mx_bank(h + 1, 1 - par, q)
                            if i == STEPS - 3:
                                mx_turn(h + 1)
                        if i == STEPS - 1 and not last:
                            scores(h + 1, 1 - par, 0)
                        weigh(h, par, i)

                eng.sem_inc(pv_done1, 2 * STEPS)
                eng.sem_inc(mx_taken, 2)
                eng.sem_inc(mt_copied, 1)
                eng.sem_inc(exp_done, 2)
                eng.sem_inc(ob_ready, 1)
                eng.sem_inc(attn_ready1, 1)
                eng.sem_inc(mrow_loaded, 16)
                eng.wait_ge(const_ready, 1)
                for q in range(NMX):
                    mx_bank(0, 0, q)
                mx_turn(0)
                scores(0, 0, 0)
                with eng.Fori(0, H // 2 - 1) as g:
                    one(g, 0)
                    one(g, 1)
                one(H // 2 - 1, 0)
                one(H // 2 - 1, 1, last=True)


def stage_output(nc, io, sb):
    base, attn1T, xn2T = sb["base"], sb["attn1T"], sb["xn2T"]
    MO = INNER // P
    with ExitStack() as ctx:
        def t(name, shape, dt=F32):
            return ctx.enter_context(nc.sbuf_tensor(name, shape, dt))

        def sem(name):
            return ctx.enter_context(nc.semaphore(name))

        w1, w2 = t("w1", [P, F1]), t("w2", [P, F1])
        h1, h2 = t("h1", [P, M1, F1]), t("h2", [P, M1, F1])
        w3, wo = t("w3", [P, M1, D]), t("wo", [P, MO, D])
        s3 = t("s3", [P, D])
        sc = t("sc", [P, 4, M1])
        ha, hb = t("ha", [P, M1, S]), t("hb", [P, M1, S])
        sil = t("sil1", [P, 2, BANK])
        y = t("y", [P, NT, D])
        psG = ctx.enter_context(nc.psum_tensor("psG1", [P, 2, BANK], F32))
        psU = ctx.enter_context(nc.psum_tensor("psU1", [P, 2, BANK], F32))
        psH = ctx.enter_context(nc.psum_tensor("psH1", [P, 2, BANK], F32))
        psO = ctx.enter_context(nc.psum_tensor("psO1", [P, 2, BANK], F32))

        loaded = sem("loaded_e")
        gate_ps, up_ps, sil_ready, ha_ready = sem("gate_ps1"), sem("up_ps1"), sem("sil_ready1"), sem("ha_ready")
        hid_ps, hid_ready = sem("hid_ps"), sem("hid_ready")
        down_ps, out_ps, y_scaled, y_sum, y_ready = (sem("down_ps1"), sem("out_ps_e"), sem("y_scaled"),
                                                     sem("y_sum"), sem("y_ready"))
        stored = sem("stored")
        NM = NCH * M1

        with nc.Block() as block:
            @block.sync
            def _(sp):
                for dst, src in ((w1[:, :], io["w1_t"]), (w2[:, :], io["w2_t"]),
                                 (sc[:, 0, :], io["w1_s"]),
                                 (sc[:, 1, :], io["w2_s"]),
                                 (sc[:, 2, :], io["h1_s"]),
                                 (sc[:, 3, :], io["h2_s"]),
                                 (h1[:, :, :], io["h1_t"].rearrange("(k p) o -> p k o", p=P)),
                                 (h2[:, :, :], io["h2_t"].rearrange("(k p) o -> p k o", p=P)),
                                 (w3[:, :, :], io["w3_t"].rearrange("(k p) o -> p k o", p=P)),
                                 (wo[:, :, :], io["w_out1"].rearrange("(k p) o -> p k o", p=P)),
                                 (s3[:, :], io["w3_s"].partition_broadcast(P))):
                    sp.dma_start(dst, src).then_inc(loaded, 16)
                out = io["out"].rearrange("a (n p) d -> p (a n) d", p=P)
                for g in range(4):
                    sp.wait_ge(y_ready, 4 * g + 4)
                    sp.dma_start(out[:, 4 * g:4 * g + 4, :], y[:, 4 * g:4 * g + 4, :]).then_inc(stored, 16)
                sp.wait_ge(stored, 64)

            @block.tensor
            def _(eng):
                eng.wait_ge(loaded, 16 * 11)
                for k in range(NM):
                    n_, m = k // M1, k % M1
                    rhs = xn2T[:, n_ * BANK:(n_ + 1) * BANK]
                    if k >= 2:
                        eng.wait_ge(sil_ready, k - 1)
                        eng.wait_ge(ha_ready, k - 1)
                    eng.matmul(psG[:, k % 2, :], w1[:, m * P:(m + 1) * P], rhs, start=True, stop=True)\
                       .then_inc(gate_ps, 1)
                    eng.matmul(psU[:, k % 2, :], w2[:, m * P:(m + 1) * P], rhs, start=True, stop=True)\
                       .then_inc(up_ps, 1)
                for l, (w, src) in enumerate(((h1, ha), (h2, hb))):
                    for k in range(NM):
                        n_, m = k // M1, k % M1
                        if m == 0:
                            eng.wait_ge((ha_ready, hid_ready)[l], (n_ + 1) * M1)
                        if l * NM + k >= 2:
                            eng.wait_ge(hid_ready, l * NM + k - 1)
                        for j in range(M1):
                            mm = eng.matmul(psH[:, k % 2, :], w[:, j, m * P:(m + 1) * P],
                                            src[:, j, n_ * BANK:(n_ + 1) * BANK], start=(j == 0), stop=(j == M1 - 1))
                        mm.then_inc(hid_ps, 1)
                for k in range(NT):
                    if k % 4 == 0:
                        eng.wait_ge(hid_ready, NM + (k // 4 + 1) * M1)
                    if k >= 2:
                        eng.wait_ge(y_sum, k - 1)
                    for j in range(M1):
                        mm = eng.matmul(psG[:, k % 2, 0:D], ha[:, j, k * P:(k + 1) * P], w3[:, j, :],
                                        start=(j == 0), stop=(j == M1 - 1))
                    mm.then_inc(down_ps, 1)
                    for j in range(MO):
                        mm = eng.matmul(psO[:, k % 2, 0:D], attn1T[:, j, k * P:(k + 1) * P], wo[:, j, :],
                                        start=(j == 0), stop=(j == MO - 1))
                    mm.then_inc(out_ps, 1)

            @block.scalar
            def _(eng):
                for k in range(NM):
                    m = k % M1
                    eng.wait_ge(gate_ps, k + 1)
                    if k >= 2:
                        eng.wait_ge(ha_ready, k - 1)
                    eng.activation(sil[:, k % 2, :], psG[:, k % 2, :], ACT.Silu, scale=sc[:, 0, m:m + 1])\
                       .then_inc(sil_ready, 1)
                for l, dst in enumerate((hb, ha)):
                    for k in range(NM):
                        n_, m = k // M1, k % M1
                        eng.wait_ge(hid_ps, l * NM + k + 1)
                        eng.activation(dst[:, m, n_ * BANK:(n_ + 1) * BANK], psH[:, k % 2, :], ACT.Gelu,
                                       scale=sc[:, 2 + l, m:m + 1]).then_inc(hid_ready, 1)

            @block.vector
            def _(eng):
                for k in range(NM):
                    n_, m = k // M1, k % M1
                    eng.wait_ge(up_ps, k + 1)
                    eng.wait_ge(sil_ready, k + 1)
                    eng.scalar_tensor_tensor(out=ha[:, m, n_ * BANK:(n_ + 1) * BANK], in0=psU[:, k % 2, :],
                                             scalar=sc[:, 1, m:m + 1], in1=sil[:, k % 2, :], op0=ALU.mult,
                                             op1=ALU.mult).then_inc(ha_ready, 1)
                for k in range(NT):
                    eng.wait_ge(down_ps, k + 1)
                    eng.tensor_tensor(y[:, k, :], psG[:, k % 2, 0:D], s3[:, :], ALU.mult).then_inc(y_scaled, 1)
                    eng.wait_ge(y_scaled, k + 1)
                    eng.wait_ge(out_ps, k + 1)
                    eng.tensor_tensor(y[:, k, :], y[:, k, :], psO[:, k % 2, 0:D], ALU.add).then_inc(y_sum, 1)
                    eng.wait_ge(y_sum, k + 1)
                    eng.tensor_tensor(y[:, k, :], y[:, k, :], base[:, k, :], ALU.add).then_inc(y_ready, 1)


def program(nc, io, debug=None):
    with ExitStack() as ctx:
        def keep(stack, name, shape, dt=F32):
            return stack.enter_context(nc.sbuf_tensor(name, shape, dt))

        sb = dict(ident=keep(ctx, "ident", [P, P]), base=keep(ctx, "base", [P, NT, D]),
                  xn2T=keep(ctx, "xn2T", [P, S]))
        with ExitStack() as layer0:
            sb |= dict(ident_b=keep(layer0, "ident_b", [P, P], BF16), v0=keep(layer0, "v0", [P, NT, D]),
                       attn0=keep(layer0, "attn0", [P, NT, D]))
            stage_project0(nc, io, sb)
            stage_attention0(nc, io, sb)
            stage_project1(nc, io, sb)
        with ExitStack() as layer1:
            sb |= dict(attn1T=keep(layer1, "attn1T", [P, H // 2, S]))
            stage_attention1(nc, io, sb)
            stage_output(nc, io, sb)


DEBUG = None


def kernel(**inputs):
    import numpy as _np
    import concourse.bacc as _bacc
    from concourse.bass_utils import run_bass_kernel_spmd as _run

    a = {k: _np.asarray(v) for k, v in inputs.items()}
    half = HD1 // 2
    freq = (_np.float32(1.0) / _np.float32(10000.0) ** (_np.arange(0, HD1, 2, dtype=_np.float32)
                                                        / _np.float32(HD1))).astype(_np.float32)
    ang = _np.arange(S, dtype=_np.float32)[:, None] * freq[None, :]
    cos_t = (QS * _np.cos(ang)).astype(_np.float32)
    sin_t = (QS * _np.sin(ang)).astype(_np.float32)
    ins = {
        "x": a["L0_attn_x"],
        "ident": _np.eye(P, dtype=_np.float32),
        "cos_t": cos_t,
        "sin_t": _np.stack([-sin_t, sin_t], axis=1),
        "w_qkv0_t": a["L0_attn_w_qkv"].T,
        "b_qkv0": a["L0_attn_b_qkv"],
        "w_out0_t": a["L0_attn_w_out"].T,
        "b_out0": a["L0_attn_b_out"],
        "w_gate_t": a["L0_ffn_w_gate"].T,
        "w_up_t": a["L0_ffn_w_up"].T,
        "w_down_t": a["L0_ffn_w_down"].T,
        "gamma": a["L1_attn_ln_gamma"],
        "beta": a["L1_attn_ln_beta"],
        "w_qkv1": a["L1_attn_w_qkv"],
        "w_out1": a["L1_attn_w_out"],
        "b_out1": a["L1_attn_b_out"],
        "w1_t": a["L1_ffn_w1_w"].T, "w1_s": a["L1_ffn_w1_s"].reshape(M1, P).T,
        "w2_t": a["L1_ffn_w2_w"].T, "w2_s": a["L1_ffn_w2_s"].reshape(M1, P).T,
        "h1_t": a["L1_ffn_h1_w"].T, "h1_s": a["L1_ffn_h1_s"].reshape(M1, P).T,
        "h2_t": a["L1_ffn_h2_w"].T, "h2_s": a["L1_ffn_h2_s"].reshape(M1, P).T,
        "w3_t": a["L1_ffn_w3_w"].T, "w3_s": a["L1_ffn_w3_s"],
    }
    nc = _bacc.Bacc("TRN2", target_bir_lowering=False, num_devices=1)
    arrays, io = {}, {}
    for name, v in ins.items():
        v = _np.ascontiguousarray(v)
        arrays[f"in_{name}"] = v
        io[name] = nc.dram_tensor(f"in_{name}", v.shape, mybir.dt.from_np(v.dtype), kind="ExternalInput").ap()
    io["stacks"] = nc.dram_tensor("stacks", (2, H, KST, S), BF16).ap()
    io["qk1"] = nc.dram_tensor("qk1", (2, H, P, S), F16).ap()
    io["v1"] = nc.dram_tensor("v1", (S, INNER), F32).ap()
    io["out"] = nc.dram_tensor("out", (1, S, D), F32, kind="ExternalOutput").ap()
    program(nc, io, DEBUG)
    r = _run(nc, [arrays], core_ids=[0])
    return r.results[0]["out"]
```

```python
from contextlib import ExitStack
import math

import concourse.bass as bass
from concourse import mybir

ALU = mybir.AluOpType
ACT = mybir.ActivationFunctionType
AX = mybir.AxisListType
F32 = mybir.dt.float32
BF16 = mybir.dt.bfloat16
F16 = mybir.dt.float16
I32 = mybir.dt.int32

P = 128
S = 2048
D = 128
NT = S // P
BANK = 512
NCH = S // BANK
H = 16

HD0 = D // H
F0 = 384
M0 = F0 // P
DEQ = 1.0 / 127.0
NPART = 3
KST = NPART * NPART * HD0
CLIP = 1.0 - 1e-7
GEXP = -3.2
HALF_PI = math.pi / 2
BT = 8
H_POLY = (1.55792178484, -0.644009720053, 0.259267954814, -0.0718242089177, 0.00936488352299)
VC = 32

HD1 = 64
INNER = H * HD1
F1 = 512
M1 = F1 // P
QS = 16.0
MROW = 2048.0
SM = 1.0 / (math.sqrt(HD1) * QS * QS)
SC = BANK
NS = S // SC
TS = SC // P
VW = 2 * HD1 + 2
VN = 2 * HD1 + 1
OW = BANK // 2
NPR = 4
NHL = 4


def stage_project0(nc, io, sb):
    v0, base, ident, ident_b = sb["v0"], sb["base"], sb["ident"], sb["ident_b"]
    with ExitStack() as ctx:
        def t(name, shape, dt=F32):
            return ctx.enter_context(nc.sbuf_tensor(name, shape, dt))

        def sem(name):
            return ctx.enter_context(nc.semaphore(name))

        x_in = t("x_in", [P, NT, D])
        xn = t("xn0", [P, NT, D])
        xnT = t("xnT0", [P, S])
        stats = t("stats0", [P, NT, 6])
        mv = t("mv0", [P, NT, 2])
        var = t("var0", [P, NT])
        sd = t("sd0", [P, NT])
        tmp = t("tmp0", [P, NT])
        w_qkv = t("w_qkv0", [P, 3 * D])
        b_qkv = t("b_qkv0", [P, 3 * D])
        wg_i = t("wg_i", [P, F0], I32)
        wu_i = t("wu_i", [P, F0], I32)
        wd_i = t("wd_i", [P, M0, D], I32)
        wg = t("wg", [P, F0])
        wu = t("wu", [P, F0])
        wd = t("wd", [P, M0, D])
        qk = t("qk0", [P, NT, 2 * D])
        sq = t("sq0", [P, NT, 2 * D])
        n2 = t("n2", [P, NT * 2 * H])
        nrm = t("nrm", [P, NT * 2 * H])
        ntmp = t("ntmp", [P, NT * 2 * H])
        parts = t("parts", [P, NPART, NT, 2 * D], BF16)
        stg = t("stg", [P, NPART, 2, S], BF16)
        hT = t("hT0", [P, M0, S])
        sil = t("sil0", [P, 2, BANK])
        psT = ctx.enter_context(nc.psum_tensor("psT0", [P, 2, BANK], F32))
        psQ = ctx.enter_context(nc.psum_tensor("psQ0", [P, 2, BANK], F32))
        psG = ctx.enter_context(nc.psum_tensor("psG0", [P, 2, BANK], F32))
        psU = ctx.enter_context(nc.psum_tensor("psU0", [P, 2, BANK], F32))

        x_loaded, w_loaded = sem("x_loaded0"), sem("w_loaded0")
        wq_loaded = sem("wq_loaded0")
        dve = sem("dve_chain0")
        var_ready, sd_ready, xn_ready = sem("var_ready0"), sem("sd_ready0"), sem("xn_ready0")
        w_cast = sem("w_cast0")
        xT_ps, xT_ready = sem("xT_ps0"), sem("xT_ready0")
        qkv_ps, qkv_taken = sem("qkv_ps0"), sem("qkv_taken0")
        n2_ready, nrm_ready, parts_ready = sem("n2_ready"), sem("nrm_ready"), sem("parts_ready")
        gate_ps, up_ps, sil_ready, h_ready = sem("gate_ps0"), sem("up_ps0"), sem("sil_ready0"), sem("h_ready0")
        pt_ps, pt_ready, parts_stored = sem("pt_ps"), sem("pt_ready"), sem("parts_stored")
        down_ps, base_ready = sem("down_ps0"), sem("base_ready0")
        psTb = psT[:, :, :].rearrange("p a b -> p (a b)").bitcast(BF16).rearrange("p (a b) -> p a b", a=2)

        with nc.Block() as block:
            @block.sync
            def _(sp):
                sp.dma_start(x_in[:, :, :], io["x"].rearrange("a (n p) d -> p (a n) d", p=P)).then_inc(x_loaded, 16)
                sp.dma_start(ident[:, :], io["ident"]).then_inc(wq_loaded, 16)
                sp.dma_start(w_qkv[:, :], io["w_qkv0_t"]).then_inc(wq_loaded, 16)
                sp.dma_start(b_qkv[:, :], io["b_qkv0"].partition_broadcast(P)).then_inc(wq_loaded, 16)
                sp.dma_start(wg_i[:, :], io["w_gate_t"]).then_inc(w_loaded, 16)
                sp.dma_start(wu_i[:, :], io["w_up_t"]).then_inc(w_loaded, 16)
                sp.dma_start(wd_i[:, :, :], io["w_down_t"].rearrange("(m p) d -> p m d", p=P)).then_inc(w_loaded, 16)
                for i in range(NPART):
                    for x in range(2):
                        sp.wait_ge(pt_ready, 2 * (2 * i + x) + 2)
                        sp.dma_start(io["parts"][i, x].rearrange("h d t -> (h d) t"), stg[:, i, x, :])\
                          .then_inc(parts_stored, 16)
                sp.wait_ge(parts_stored, 16 * 2 * NPART)

            @block.vector
            def _(eng):
                n = [0]

                def link(ins):
                    n[0] += 1
                    ins.then_inc(dve, 1)
                    eng.wait_ge(dve, n[0])

                eng.wait_ge(x_loaded, 16)
                for k in range(NT):
                    last = eng.bn_stats(stats[:, k, :], x_in[:, k, :])
                link(last)
                for k in range(NT):
                    last = eng.bn_aggr(mv[:, k, :], stats[:, k, :])
                link(last)
                eng.tensor_scalar(var[:, :], mv[:, :, 1], 1e-5, None, ALU.add).then_inc(var_ready, 1)
                eng.wait_ge(sd_ready, 1)
                link(eng.reciprocal(tmp[:, :], sd[:, :]))
                link(eng.tensor_tensor(tmp[:, :], tmp[:, :], var[:, :], ALU.mult))
                link(eng.tensor_tensor(tmp[:, :], tmp[:, :], sd[:, :], ALU.add))
                link(eng.reciprocal(tmp[:, :], tmp[:, :]))
                link(eng.tensor_scalar(tmp[:, :], tmp[:, :], 2.0, None, ALU.mult))
                for k in range(NT):
                    eng.tensor_scalar(xn[:, k, :], x_in[:, k, :], mv[:, k, 0:1], tmp[:, k:k + 1],
                                      ALU.subtract, ALU.mult).then_inc(xn_ready, 1)
                eng.wait_ge(wq_loaded, 48)
                eng.tensor_copy(ident_b[:, :], ident[:, :])
                eng.wait_ge(w_loaded, 48)
                eng.tensor_copy(wg[:, :], wg_i[:, :])
                eng.tensor_copy(wu[:, :], wu_i[:, :])
                eng.tensor_copy(wd[:, :, :], wd_i[:, :, :]).then_inc(w_cast, 1)
                for k in range(NT):
                    eng.wait_ge(qkv_ps, k + 1)
                    eng.tensor_tensor(qk[:, k, :], psQ[:, k % 2, 0:2 * D], b_qkv[:, 0:2 * D], ALU.add)
                    last = eng.tensor_tensor(v0[:, k, :], psQ[:, k % 2, 2 * D:3 * D], b_qkv[:, 2 * D:3 * D], ALU.add)
                    last.then_inc(qkv_taken, 1)
                eng.wait_ge(qkv_taken, NT)
                link(eng.tensor_tensor(sq[:, :, :], qk[:, :, :], qk[:, :, :], ALU.mult))
                groups = sq[:, :, :].rearrange("p n (g d) -> p (n g) d", d=HD0)
                eng.tensor_reduce(n2[:, :], groups, AX.X, ALU.add).then_inc(n2_ready, 1)
                eng.wait_ge(nrm_ready, 1)
                link(eng.tensor_scalar(nrm[:, :], nrm[:, :], 1e-30, None, ALU.max))
                link(eng.reciprocal(ntmp[:, :], nrm[:, :]))
                link(eng.tensor_tensor(ntmp[:, :], ntmp[:, :], n2[:, :], ALU.mult))
                link(eng.tensor_tensor(ntmp[:, :], ntmp[:, :], nrm[:, :], ALU.add))
                link(eng.tensor_scalar(ntmp[:, :], ntmp[:, :], 0.5, 1e-12, ALU.mult, ALU.max))
                link(eng.reciprocal(nrm[:, :], ntmp[:, :]))
                spread = nrm[:, :].unsqueeze(2).to_broadcast([P, NT * 2 * H, HD0])
                qk_g = qk[:, :, :].rearrange("p n (g d) -> p (n g) d", d=HD0)
                link(eng.tensor_tensor(groups, qk_g, spread, ALU.mult))
                link(eng.tensor_copy(parts[:, 0, :, :], sq[:, :, :]))
                link(eng.tensor_tensor(qk[:, :, :], sq[:, :, :], parts[:, 0, :, :], ALU.subtract))
                link(eng.tensor_copy(parts[:, 1, :, :], qk[:, :, :]))
                eng.tensor_tensor(parts[:, 2, :, :], qk[:, :, :], parts[:, 1, :, :], ALU.subtract)\
                   .then_inc(parts_ready, 1)
                for k in range(NCH * M0):
                    n_, m = k // M0, k % M0
                    eng.wait_ge(up_ps, k + 1)
                    eng.wait_ge(sil_ready, k + 1)
                    eng.scalar_tensor_tensor(out=hT[:, m, n_ * BANK:(n_ + 1) * BANK], in0=psU[:, k % 2, :],
                                             scalar=DEQ, in1=sil[:, k % 2, :], op0=ALU.mult,
                                             op1=ALU.mult).then_inc(h_ready, 1)
                for k in range(NT):
                    eng.wait_ge(down_ps, k + 1)
                    eng.scalar_tensor_tensor(out=base[:, k, :], in0=psQ[:, k % 2, 0:D], scalar=DEQ,
                                             in1=x_in[:, k, :], op0=ALU.mult, op1=ALU.add).then_inc(base_ready, 1)

            @block.scalar
            def _(eng):
                eng.wait_ge(var_ready, 1)
                eng.activation(sd[:, :], var[:, :], ACT.Sqrt).then_inc(sd_ready, 1)
                for g in range(NCH):
                    eng.wait_ge(xT_ps, g + 1)
                    eng.activation(xnT[:, g * BANK:(g + 1) * BANK], psT[:, g % 2, :], ACT.Copy).then_inc(xT_ready, 1)
                eng.wait_ge(n2_ready, 1)
                eng.activation(nrm[:, :], n2[:, :], ACT.Sqrt).then_inc(nrm_ready, 1)
                for k in range(NCH * M0):
                    eng.wait_ge(gate_ps, k + 1)
                    if k >= 2:
                        eng.wait_ge(h_ready, k - 1)
                    eng.activation(sil[:, k % 2, :], psG[:, k % 2, :], ACT.Silu, scale=DEQ).then_inc(sil_ready, 1)
                for k in range(2 * NPART * 2):
                    i, x, g = k // 4, k // 2 % 2, k % 2
                    eng.wait_ge(pt_ps, k + 1)
                    eng.activation(stg[:, i, x, g * 1024:(g + 1) * 1024], psTb[:, k % 2, :],
                                   ACT.Copy).then_inc(pt_ready, 1)

            @block.tensor
            def _(eng):
                eng.wait_ge(wq_loaded, 48)
                for g in range(NCH):
                    if g >= 2:
                        eng.wait_ge(xT_ready, g - 1)
                    for j in range(4):
                        k = 4 * g + j
                        eng.wait_ge(xn_ready, k + 1)
                        mm = eng.transpose(psT[:, g % 2, j * P:(j + 1) * P], xn[:, k, :], ident[:, :])
                    mm.then_inc(xT_ps, 1)
                for k in range(NT):
                    if k % 4 == 0:
                        eng.wait_ge(xT_ready, k // 4 + 1)
                    if k >= 2:
                        eng.wait_ge(qkv_taken, k - 1)
                    eng.matmul(psQ[:, k % 2, 0:3 * D], xnT[:, k * P:(k + 1) * P], w_qkv[:, :],
                               start=True, stop=True).then_inc(qkv_ps, 1)
                eng.wait_ge(w_cast, 1)
                for k in range(NCH * M0):
                    n_, m = k // M0, k % M0
                    rhs = xnT[:, n_ * BANK:(n_ + 1) * BANK]
                    if k >= 2:
                        eng.wait_ge(sil_ready, k - 1)
                        eng.wait_ge(h_ready, k - 1)
                    eng.matmul(psG[:, k % 2, :], wg[:, m * P:(m + 1) * P], rhs, start=True, stop=True)\
                       .then_inc(gate_ps, 1)
                    eng.matmul(psU[:, k % 2, :], wu[:, m * P:(m + 1) * P], rhs, start=True, stop=True)\
                       .then_inc(up_ps, 1)
                eng.wait_ge(parts_ready, 1)
                for k in range(2 * NPART * 2):
                    i, x, g = k // 4, k // 2 % 2, k % 2
                    if k >= 2:
                        eng.wait_ge(pt_ready, k - 1)
                    for j in range(8):
                        mm = eng.transpose(psTb[:, k % 2, j * P:(j + 1) * P],
                                           parts[:, i, 8 * g + j, x * D:(x + 1) * D], ident_b[:, :])
                    mm.then_inc(pt_ps, 1)
                eng.wait_ge(h_ready, NCH * M0)
                for k in range(NT):
                    if k >= 2:
                        eng.wait_ge(base_ready, k - 1)
                    for m in range(M0):
                        mm = eng.matmul(psQ[:, k % 2, 0:D], hT[:, m, k * P:(k + 1) * P], wd[:, m, :],
                                        start=(m == 0), stop=(m == M0 - 1))
                    mm.then_inc(down_ps, 1)


def stage_attention0(nc, io, sb):
    v0, attn0, ident = sb["v0"], sb["attn0"], sb["ident"]
    BJ = BT // 2
    CPOS = 1.0 - 2.0 ** -23
    LN_MIN = math.log(2.0 ** -23)
    D_MAX = math.log(1.0 + CPOS) - LN_MIN
    U_MIN = math.sqrt((1.0 - CPOS) / 2)
    A0, A1, A2, A3, A4 = H_POLY
    Z_SCALE = math.sqrt(2.0) * A4
    Z_MAX = (math.acos(-CPOS) - HALF_PI) / Z_SCALE
    with ExitStack() as ctx:
        def t(name, shape, dt=F32):
            return ctx.enter_context(nc.sbuf_tensor(name, shape, dt))

        def sem(name):
            return ctx.enter_context(nc.semaphore(name))

        qst = t("qst", [KST, S], BF16)
        kst = t("kst", [KST, S], BF16)
        wt = t("wt", [P, BJ, S])
        wp = t("wp", [P, 2, BJ, S])
        aux = t("aux", [P, BJ + 1, S])
        s_buf = t("s_buf", [P, S])
        n_c = t("n_c", [P, NT])
        r_c = t("r_c", [P, NT])
        vh = t("vh", [P, NT, VC])
        o_sb = t("o_sb", [P, BANK])
        small = t("small0", [P, NT, 4])
        theta_bias, half_bias = t("theta_bias", [P, 1]), t("half_bias", [P, 1])
        c_ps = ctx.enter_context(nc.psum_tensor("c_ps", [P, 2, 2 * BANK], F32))
        o_ps = ctx.enter_context(nc.psum_tensor("o_ps", [P, BANK], F32))
        t_ps = ctx.enter_context(nc.psum_tensor("t_ps", [P, 4, P], F32))

        const_ready, stacks_loaded = sem("const_ready0"), sem("stacks_loaded")
        cos_ps, cos_read = sem("cos_ps"), sem("cos_read")
        diff_ready = sem("diff_ready")
        tanh_ready, atan_ready = sem("tanh_ready"), sem("atan_ready")
        poly, poly_ready, guard = sem("poly"), sem("poly_ready"), sem("guard")
        lnth_ready, score_ready = sem("lnth_ready"), sem("score_ready")
        rc_ready, vh_ready, pv_done = sem("rc_ready"), sem("vh_ready"), sem("pv_done")
        o_copied, o_turned, attn_ready = sem("o_copied"), sem("o_turned"), sem("attn_ready")
        rows_done = sem("rows_done")

        def w_slot(b, j):
            return j if j < BJ - 1 else BJ - 1 + b

        def halves_read(n, i):
            return 2 * (BT * n + i) + 2 + 2

        def place_p(n, j):
            return BT * n + j

        def place_t(n, j):
            return BT * n + BJ + j

        def before(h, b):
            return (h, 0) if b == 1 else (h - 1, 1)

        with nc.Block() as block:
            @block.sync
            def _(sp):
                with sp.Fori(0, H) as h:
                    sp.wait_ge(cos_ps, 2 * NT * h + 2)
                    for i in range(NPART):
                        for j in range(NPART):
                            row = HD0 * (NPART * j + i)
                            sp.dma_start(qst[row:row + HD0, :], io["parts"][i, 0, h, :, :]).then_inc(stacks_loaded, 16)
                            sp.dma_start(kst[row:row + HD0, :], io["parts"][j, 1, h, :, :]).then_inc(stacks_loaded, 16)

            @block.vector
            def _(eng):
                eng.memset(theta_bias[:, :], 1.0 + HALF_PI)
                eng.memset(half_bias[:, :], 0.5)
                eng.memset(vh[:, :, HD0 + 2:VC], 0.0)
                eng.memset(vh[:, :, HD0 + 1:HD0 + 2], 1.0).then_inc(const_ready, 1)

                def difference(n, j):
                    eng.wait_ge(cos_read, halves_read(n, j))
                    eng.scalar_tensor_tensor(out=wt[:, j, :], in0=wt[:, j, :], scalar=LN_MIN, in1=aux[:, j % 2, :],
                                             op0=ALU.max, op1=ALU.subtract).then_inc(guard, 1)

                def limit(n, j):
                    eng.wait_ge(guard, BJ * n + j + 1)
                    eng.tensor_scalar(wt[:, j, :], wt[:, j, :], D_MAX, None, ALU.min).then_inc(diff_ready, 1)

                def chain(n, b, j):
                    u, w = wp[:, b, j, :], aux[:, w_slot(b, j), :]
                    at = 6 * (BJ * n + j)

                    def split_s():
                        eng.wait_ge(cos_read, halves_read(n, BJ + j))
                        if not (isinstance(n, int) and n == 0 and j == 0):
                            eng.wait_ge(poly, at)
                        eng.scalar_tensor_tensor(out=s_buf[:, :], in0=u, scalar=U_MIN, in1=w, op0=ALU.max,
                                                 op1=ALU.subtract).then_inc(poly, 1)

                    def split_y():
                        eng.wait_ge(poly, at + 1)
                        eng.scalar_tensor_tensor(out=w, in0=u, scalar=U_MIN, in1=w, op0=ALU.max,
                                                 op1=ALU.add).then_inc(poly, 1)

                    def horner(i, c, src, by):
                        def step():
                            eng.wait_ge(poly, at + i)
                            eng.scalar_tensor_tensor(out=u, in0=src, scalar=c, in1=by, op0=ALU.add,
                                                     op1=ALU.mult).then_inc(poly, 1)
                        return step

                    def limit_z():
                        eng.wait_ge(poly, at + 6)
                        eng.tensor_scalar(u, u, Z_MAX, None, ALU.min).then_inc(poly_ready, 1)

                    return [split_s, split_y, horner(2, A3 / A4, w, w), horner(3, A2 / A4, u, w),
                            horner(4, A1 / A4, u, w), horner(5, A0 / A4, u, s_buf[:, :]), limit_z]

                def values(h, k, place):
                    eng.wait_ge(score_ready, place + 1)
                    if not (isinstance(h, int) and h == 0):
                        eng.wait_ge(pv_done, place - NT + 1)
                    eng.reciprocal(r_c[:, k:k + 1], n_c[:, k:k + 1]).then_inc(rc_ready, 1)
                    eng.wait_ge(rc_ready, place + 1)
                    eng.tensor_copy(vh[:, k, HD0:HD0 + 1], r_c[:, k:k + 1])
                    eng.tensor_scalar(vh[:, k, 0:HD0], v0[:, k, bass.ds(h * HD0, HD0)], r_c[:, k:k + 1], None,
                                      ALU.mult).then_inc(vh_ready, 1)

                def finish(h):
                    eng.wait_ge(pv_done, NT * (h + 1) + BJ)
                    eng.tensor_copy(o_sb[:, :], o_ps[:, :]).then_inc(o_copied, 1)
                    eng.wait_ge(o_turned, h + 1)
                    rows = t_ps[:, :, :].rearrange("p j (c r) -> p c j r", r=VC)
                    quad = small[:, :, :].rearrange("p (c j) r -> p c j r", j=4)
                    eng.reciprocal(quad[:, :, :, 0:1], rows[:, :, :, HD0 + 1:HD0 + 2]).then_inc(rows_done, 1)
                    eng.wait_ge(rows_done, h * 5 + 1)
                    eng.tensor_tensor(quad[:, :, :, 1:2], rows[:, :, :, HD0:HD0 + 1], quad[:, :, :, 0:1],
                                      ALU.mult).then_inc(rows_done, 1)
                    eng.wait_ge(rows_done, h * 5 + 2)
                    eng.tensor_scalar(small[:, :, 1:2], small[:, :, 1:2], 1e-12, None, ALU.max).then_inc(rows_done, 1)
                    eng.wait_ge(rows_done, h * 5 + 3)
                    eng.reciprocal(small[:, :, 2:3], small[:, :, 1:2]).then_inc(rows_done, 1)
                    eng.wait_ge(rows_done, h * 5 + 4)
                    eng.tensor_tensor(small[:, :, 3:4], small[:, :, 2:3], small[:, :, 0:1], ALU.mult)\
                       .then_inc(rows_done, 1)
                    eng.wait_ge(rows_done, h * 5 + 5)
                    for c in range(4):
                        last = eng.tensor_tensor(attn0[:, 4 * c:4 * c + 4, bass.ds(h * HD0, HD0)],
                                                 t_ps[:, :, VC * c:VC * c + HD0],
                                                 small[:, 4 * c:4 * c + 4, 3:4].to_broadcast([P, 4, HD0]), ALU.mult)
                    last.then_inc(attn_ready, 1)

                CUT = 4
                P_AT, FINISH_AT, T_AT = 10, 14, 14

                def round_(h, b, first=False):
                    n = 2 * h + b
                    for j in range(BJ):
                        difference(n, j)
                        if j > 0:
                            limit(n, j - 1)
                    limit(n, BJ - 1)
                    hp, bp = before(h, b)
                    if not first:
                        for step in (chain(n - 1, bp, 2) + chain(n - 1, bp, 3))[CUT:]:
                            step()
                    steps = chain(n, b, 0) + chain(n, b, 1) + chain(n, b, 2)[:CUT]
                    for i, step in enumerate(steps):
                        step()
                        if not first and P_AT <= i < P_AT + BJ:
                            values(hp, BT * bp + BJ + i - P_AT, place_p(n, i - P_AT))
                        if i == FINISH_AT and b == 0 and not first:
                            finish(hp)
                        if T_AT <= i < T_AT + BJ:
                            values(h, BT * b + i - T_AT, place_t(n, i - T_AT))

                round_(0, 0, first=True)
                round_(0, 1)
                with eng.Fori(1, H) as h:
                    round_(h, 0)
                    round_(h, 1)
                for step in (chain(2 * H - 1, 1, 2) + chain(2 * H - 1, 1, 3))[CUT:]:
                    step()
                for j in range(BJ):
                    values(H - 1, NT - BJ + j, place_p(2 * H, j))
                finish(H - 1)

            @block.scalar
            def _(eng):
                def halves(n, j0, func_a, func_b, j):
                    for i in range(2):
                        eng.wait_ge(cos_ps, 2 * (BT * n + j0 + j) + i + 1 + 2)
                        w = slice(i * 2 * BANK, (i + 1) * 2 * BANK)
                        func_a(w, c_ps[:, i, :])
                        func_b(w, c_ps[:, i, :]).then_inc(cos_read, 1)

                def logs(n, j, first):
                    if not first:
                        eng.wait_ge(pv_done, place_t(n - 1, j) + 1)
                    if j < 2:
                        if not first:
                            eng.wait_ge(poly_ready, BJ * (n - 1) + j + 1)
                    else:
                        eng.wait_ge(guard, BJ * n + j - 1)
                    halves(n, 0, lambda w, c: eng.activation(wt[:, j, w], c, ACT.Ln, bias=1.0, scale=1.0),
                           lambda w, c: eng.activation(aux[:, j % 2, w], c, ACT.Ln, bias=1.0, scale=-1.0), j)

                def roots(n, b, j, first):
                    if not first:
                        eng.wait_ge(pv_done, place_p(n - 1, j) + 1)
                    if j == 2 and not first:
                        eng.wait_ge(poly_ready, BJ * (n - 1) + 3)
                    halves(n, BJ, lambda w, c: eng.activation(wp[:, b, j, w], c, ACT.Sqrt, scale=-0.5,
                                                              bias=half_bias[:, 0:1]),
                           lambda w, c: eng.activation(aux[:, w_slot(b, j), w], c, ACT.Sqrt, scale=0.5,
                                                       bias=half_bias[:, 0:1]), j)

                def scores(tile, n, at, scale, place, tiles, first):
                    for g in range(2):
                        eng.activation(tile[:, 2 * g:2 * g + 2, :], tile[:, 2 * g:2 * g + 2, :], ACT.Ln, scale=scale,
                                       bias=theta_bias[:, 0:1]).then_inc(lnth_ready, 1)
                    for j in range(BJ):
                        if j % 2 == 0:
                            eng.wait_ge(lnth_ready, at + j // 2 + 1)
                        if not first:
                            eng.wait_ge(vh_ready, place(n, j) - NT + 1)
                        eng.activation(tile[:, j, :], tile[:, j, :], ACT.Exp, scale=GEXP,
                                       accum_out=n_c[:, tiles + j:tiles + j + 1]).then_inc(score_ready, 1)

                def scores_p(n, bp, first):
                    eng.wait_ge(poly_ready, BJ * n)
                    scores(wp[:, bp, :, :], n, 4 * n, Z_SCALE, place_p, BT * bp + BJ, first)

                def round_(h, b, first=False):
                    n = 2 * h + b
                    head0 = isinstance(h, int) and h == 0
                    for j in range(BJ):
                        logs(n, j, first)
                    eng.preload_act_table_set("sigmoid_and_others")
                    for g in range(2):
                        eng.wait_ge(diff_ready, BJ * n + 2 * g + 2)
                        eng.activation(wt[:, 2 * g:2 * g + 2, :], wt[:, 2 * g:2 * g + 2, :], ACT.Tanh, scale=0.25)\
                           .then_inc(tanh_ready, 1)
                    for g in range(2):
                        eng.wait_ge(tanh_ready, 2 * n + g + 1)
                        eng.activation(wt[:, 2 * g:2 * g + 2, :], wt[:, 2 * g:2 * g + 2, :], ACT.Arctan)\
                           .then_inc(atan_ready, 1)
                    for j in range(BJ):
                        roots(n, b, j, first)
                    eng.preload_act_table_set("natural_log_exp_and_others")
                    if not first:
                        scores_p(n, before(h, b)[1], head0)
                    eng.wait_ge(atan_ready, 2 * n + 2)
                    scores(wt, n, 4 * n + 2, -2.0, place_t, BT * b, head0)

                eng.preload_act_table_set("natural_log_exp_and_others")
                eng.wait_ge(const_ready, 1)
                round_(0, 0, first=True)
                round_(0, 1)
                with eng.Fori(1, H) as h:
                    round_(h, 0)
                    round_(h, 1)
                scores_p(2 * H, 1, False)

            @block.tensor
            def _(eng):
                def cosines(h, k):
                    if k == 0:
                        eng.wait_ge(stacks_loaded, 16 * 2 * NPART * NPART * (h + 1))
                    for i in range(2):
                        eng.wait_ge(cos_read, 2 * NT * h + 2 * k + i + 1)
                        for c in range(2):
                            n_ = 2 * i + c
                            mm = eng.matmul(c_ps[:, i, c * BANK:(c + 1) * BANK], kst[:, k * P:(k + 1) * P],
                                            qst[:, n_ * BANK:(n_ + 1) * BANK], start=True, stop=True)
                        mm.then_inc(cos_ps, 1)

                def weigh(tile, k, place, start=False, stop=False):
                    eng.wait_ge(vh_ready, place + 1)
                    for c in range(NCH):
                        mm = eng.matmul(o_ps[VC * c:VC * (c + 1), :], vh[:, k, :],
                                        tile[:, c * BANK:(c + 1) * BANK], start=start, stop=stop)
                    mm.then_inc(pv_done, 1)

                def turn(h):
                    eng.wait_ge(o_copied, h + 1)
                    eng.wait_ge(attn_ready, h + 1)
                    for j in range(4):
                        mm = eng.transpose(t_ps[:, j, :], o_sb[:, j * P:(j + 1) * P], ident[:, :])
                    mm.then_inc(o_turned, 1)

                def weigh_p(n, bp):
                    for j in range(BJ):
                        weigh(wp[:, bp, j, :], BT * bp + BJ + j, place_p(n, j), stop=(bp == 1 and j == BJ - 1))

                def round_(h, b, first=False, last=False):
                    n = 2 * h + b
                    if first:
                        cosines(h, BT * b)
                        cosines(h, BT * b + 1)
                    for j in range(2, BT):
                        cosines(h, BT * b + j)
                    if not first:
                        weigh_p(n, before(h, b)[1])
                    if b == 0 and not first:
                        turn(h - 1)
                    for j in range(BJ):
                        if j in (0, 2) and not last:
                            cosines(h if b == 0 else h + 1, BT * (1 - b) + j // 2)
                        weigh(wt[:, j, :], BT * b + j, place_t(n, j), start=(b == 0 and j == 0))

                eng.sem_inc(score_ready, BJ)
                eng.sem_inc(rc_ready, BJ)
                eng.sem_inc(vh_ready, BJ)
                eng.sem_inc(pv_done, BJ)
                eng.sem_inc(lnth_ready, 2)
                eng.sem_inc(cos_read, 2)
                eng.sem_inc(cos_ps, 2)
                eng.sem_inc(attn_ready, 1)
                round_(0, 0, first=True)
                round_(0, 1)
                with eng.Fori(1, H - 1) as h:
                    round_(h, 0)
                    round_(h, 1)
                round_(H - 1, 0)
                round_(H - 1, 1, last=True)
                weigh_p(2 * H, 1)
                turn(H - 1)


def norm_on_vector(eng, link, src, dst, stats, mv, var, sd, tmp, var_ready, sd_ready, n):
    for k in range(NT):
        last = eng.bn_stats(stats[:, k, :], src[:, k, :])
    link(last)
    for k in range(NT):
        last = eng.bn_aggr(mv[:, k, :], stats[:, k, :])
    link(last)
    eng.tensor_scalar(var[:, :], mv[:, :, 1], 1e-5, None, ALU.add).then_inc(var_ready, 1)
    eng.wait_ge(sd_ready, n)
    link(eng.reciprocal(tmp[:, :], sd[:, :]))
    link(eng.tensor_tensor(tmp[:, :], tmp[:, :], var[:, :], ALU.mult))
    link(eng.tensor_tensor(tmp[:, :], tmp[:, :], sd[:, :], ALU.add))
    link(eng.reciprocal(tmp[:, :], tmp[:, :]))
    link(eng.tensor_scalar(tmp[:, :], tmp[:, :], 2.0, None, ALU.mult))
    for k in range(NT):
        last = eng.tensor_scalar(dst[:, k, :], src[:, k, :], mv[:, k, 0:1], tmp[:, k:k + 1],
                                 ALU.subtract, ALU.mult)
    link(last)


def stage_project1(nc, io, sb):
    base, attn0, ident, xn2T = sb["base"], sb["attn0"], sb["ident"], sb["xn2T"]
    HB = 8
    HALF = HD1 // 2
    with ExitStack() as ctx:
        def t(name, shape, dt=F32):
            return ctx.enter_context(nc.sbuf_tensor(name, shape, dt))

        def sem(name):
            return ctx.enter_context(nc.semaphore(name))

        attn0T = t("attn0T", [P, S])
        xn = t("xn2", [P, NT, D])
        xa = t("xa", [P, NT, D])
        xaT = attn0T
        stats, mv = t("stats1", [P, NT, 6]), t("mv1", [P, NT, 2])
        var, sd, tmp = t("var1", [P, NT]), t("sd1", [P, NT]), t("tmp1", [P, NT])
        w_out, b_out = t("w_out0", [P, D]), t("b_out0", [P, D])
        gamma, beta, b_out1 = t("gamma", [P, D]), t("beta", [P, D]), t("b_out1", [P, D])
        w_qkv = t("w_qkv1", [P, 3 * INNER])
        cos_t, sin_t = t("cos_t", [P, NT, HALF]), t("sin_t", [P, NT, 2, HALF])
        ident_h = t("ident_h", [P, P], F16)
        ra, rb = t("ra", [P, 2, BANK]), t("rb", [P, 2, BANK])
        hl = t("hl", [P, 2, 2 * H, 2, HD1], F16)
        v_st = t("v_st", [P, 2, H, 4, VW], F16)
        stg = t("stg1", [P, 2, 2 * H, BANK], F16)
        psA = ctx.enter_context(nc.psum_tensor("psA1", [P, 2, BANK], F32))
        psR = ctx.enter_context(nc.psum_tensor("psR1", [P, 4, BANK], F32))
        psB = ctx.enter_context(nc.psum_tensor("psB1", [P, 2, 2 * BANK], F16))

        loaded, dve = sem("loaded1"), sem("dve_chain1")
        turned, taken = sem("turned1"), sem("taken1")
        out_ps, x1_ready = sem("out_ps1"), sem("x1_ready")
        var_ready, sd_ready = sem("var_ready1"), sem("sd_ready1")
        xn_ready, xa_ready = sem("xn_ready1"), sem("xa_ready1")
        qkv_ps, rope_read = sem("qkv_ps1"), sem("rope_read")
        v_high, v_low = sem("v_high"), sem("v_low")
        rot_ready, hi_ready, lo_ready = sem("rot_ready"), sem("hi_ready"), sem("lo_ready")
        hl_ps, hl_taken = sem("hl_ps"), sem("hl_taken")
        v_stored = [sem("v_stored_0"), sem("v_stored_1")]
        qk_stored = [sem("qk_stored_0"), sem("qk_stored_1")]

        with nc.Block() as block:
            @block.sync
            def _(sp):
                for dst, src in ((w_out[:, :], io["w_out0_t"]), (b_out[:, :], io["b_out0"].partition_broadcast(P)),
                                 (gamma[:, :], io["gamma"].partition_broadcast(P)),
                                 (beta[:, :], io["beta"].partition_broadcast(P)),
                                 (b_out1[:, :], io["b_out1"].partition_broadcast(P)),
                                 (w_qkv[:, :], io["w_qkv1"]),
                                 (cos_t[:, :, :], io["cos_t"].rearrange("(n p) f -> p n f", p=P)),
                                 (sin_t[:, :, :, :], io["sin_t"].rearrange("(n p) a f -> p n a f", p=P))):
                    sp.dma_start(dst, src).then_inc(loaded, 16)
                for k in range(NT):
                    if k % 4 == 3:
                        n_ = k // 4
                        sp.wait_ge(v_low, 2 * k + 2)
                        sp.dma_start(io["v1"][:, :, 4 * n_:4 * n_ + 4, :].rearrange("h p n e -> p h n e"),
                                     v_st[:, n_ % 2, :, :, :]).then_inc(v_stored[n_ % 2], 16)
                        sp.wait_ge(hl_taken, 4 * (k + 1))
                        for x in range(2):
                            sp.dma_start(io["qk1"][x, :, :, n_ * BANK:(n_ + 1) * BANK].rearrange("h p t -> p h t"),
                                         stg[:, n_ % 2, x * H:(x + 1) * H, :]).then_inc(qk_stored[n_ % 2], 16)
                for slot in range(2):
                    sp.wait_ge(v_stored[slot], 16 * NCH // 2)
                    sp.wait_ge(qk_stored[slot], 32 * NCH // 2)

            @block.vector
            def _(eng):
                n = [0]

                def link(ins):
                    n[0] += 1
                    ins.then_inc(dve, 1)
                    eng.wait_ge(dve, n[0])

                eng.wait_ge(loaded, 16 * 8)
                eng.tensor_copy(ident_h[:, :], ident[:, :])
                eng.memset(v_st[:, :, :, :, HD1:HD1 + 1], QS)
                eng.memset(v_st[:, :, :, :, VN:VW], 0.0)
                link(eng.tensor_tensor(base[:, :, :], base[:, :, :],
                                       b_out[:, :].unsqueeze(1).to_broadcast([P, NT, D]), ALU.add))
                for k in range(NT):
                    eng.wait_ge(out_ps, k + 1)
                    eng.tensor_tensor(base[:, k, :], base[:, k, :], psR[:, k % 4, 0:D], ALU.add).then_inc(x1_ready, 1)
                eng.wait_ge(x1_ready, NT)
                norm_on_vector(eng, link, base, xn, stats, mv, var, sd, tmp, var_ready, sd_ready, 1)
                eng.sem_inc(xn_ready, 1)
                norm_on_vector(eng, link, xn, xa, stats, mv, var, sd, tmp, var_ready, sd_ready, 2)
                link(eng.tensor_tensor(xa[:, :, :], xa[:, :, :], gamma[:, :].unsqueeze(1).to_broadcast([P, NT, D]),
                                       ALU.mult))
                eng.tensor_tensor(xa[:, :, :], xa[:, :, :], beta[:, :].unsqueeze(1).to_broadcast([P, NT, D]),
                                  ALU.add).then_inc(xa_ready, 1)
                eng.tensor_tensor(base[:, :, :], base[:, :, :], b_out1[:, :].unsqueeze(1).to_broadcast([P, NT, D]),
                                  ALU.add)

                for k in range(NT):
                    for b in range(4):
                        u = 4 * k + b
                        src = psR[:, b, :].rearrange("p (h a f) -> p h a f", h=HB, a=2)
                        a_ = ra[:, u % 2, :].rearrange("p (h a f) -> p h a f", h=HB, a=2)
                        b_ = rb[:, u % 2, :].rearrange("p (h a f) -> p h a f", h=HB, a=2)
                        eng.wait_ge(qkv_ps, 6 * k + b + 1)
                        if u >= 2:
                            eng.wait_ge(lo_ready, u - 1)
                        for a in range(2):
                            eng.tensor_tensor(a_[:, :, a, :], src[:, :, a, :],
                                              cos_t[:, k, :].unsqueeze(1).to_broadcast([P, HB, HALF]), ALU.mult)
                        eng.tensor_tensor(b_[:, :, 0, :], src[:, :, 1, :],
                                          sin_t[:, k, 0, :].unsqueeze(1).to_broadcast([P, HB, HALF]), ALU.mult)
                        eng.tensor_tensor(b_[:, :, 1, :], src[:, :, 0, :],
                                          sin_t[:, k, 1, :].unsqueeze(1).to_broadcast([P, HB, HALF]), ALU.mult)\
                           .then_inc(rope_read, 1)
                        eng.wait_ge(rope_read, u + 1)
                        if u >= 1:
                            low_half(eng, hl, ra, rb, u - 1, hi_ready, lo_ready)
                        eng.tensor_tensor(ra[:, u % 2, :], ra[:, u % 2, :], rb[:, u % 2, :], ALU.add)\
                           .then_inc(rot_ready, 1)
                        if u == 4 * NT - 1:
                            low_half(eng, hl, ra, rb, u, hi_ready, lo_ready)
                    for b in range(2):
                        eng.wait_ge(v_high, 2 * k + b + 1)
                        vv = v_st[:, k // 4 % 2, b * HB:(b + 1) * HB, k % 4, :]
                        eng.scalar_tensor_tensor(out=vv[:, :, HD1 + 1:VN],
                                                 in0=psA[:, b, :].rearrange("p (h e) -> p h e", h=HB), scalar=QS,
                                                 in1=vv[:, :, 0:HD1], op0=ALU.mult, op1=ALU.subtract)\
                           .then_inc(v_low, 1)

            @block.scalar
            def _(eng):
                for g in range(NCH):
                    eng.wait_ge(turned, g + 1)
                    eng.activation(attn0T[:, g * BANK:(g + 1) * BANK], psA[:, g % 2, :], ACT.Copy).then_inc(taken, 1)
                for i in range(2):
                    eng.wait_ge(var_ready, i + 1)
                    eng.activation(sd[:, :], var[:, :], ACT.Sqrt).then_inc(sd_ready, 1)
                    for g in range(NCH):
                        eng.wait_ge(turned, NCH * (i + 1) + g + 1)
                        dst = (xn2T, xaT)[i]
                        eng.activation(dst[:, g * BANK:(g + 1) * BANK], psA[:, g % 2, :], ACT.Copy).then_inc(taken, 1)
                for k in range(NT + 1):
                    if k < NT:
                        for b in range(4):
                            u = 4 * k + b
                            eng.wait_ge(rot_ready, u + 1)
                            if k >= 2:
                                eng.wait_ge(hl_ps, 4 * (k - 1))
                            eng.activation(hl[:, k % 2, b * HB:(b + 1) * HB, 0, :],
                                           ra[:, u % 2, :].rearrange("p (h e) -> p h e", h=HB),
                                           ACT.Copy).then_inc(hi_ready, 1)
                        for b in range(2):
                            eng.wait_ge(qkv_ps, 6 * k + 5 + b)
                            if k == 8 or k == 12:
                                eng.wait_ge(v_stored[k // 4 % 2], 16)
                            eng.activation(v_st[:, k // 4 % 2, b * HB:(b + 1) * HB, k % 4, 0:HD1],
                                           psA[:, b, :].rearrange("p (h e) -> p h e", h=HB),
                                           ACT.Copy, scale=QS).then_inc(v_high, 1)
                    if k >= 1:
                        kk = k - 1
                        for g in range(4):
                            eng.wait_ge(hl_ps, 4 * kk + g + 1)
                            if kk % 4 == 0 and kk >= 8:
                                eng.wait_ge(qk_stored[kk // 4 % 2], 32 * (kk // 8))
                            eng.activation(stg[:, kk // 4 % 2, g * HB:(g + 1) * HB, kk % 4 * P:(kk % 4 + 1) * P],
                                           psB[:, g % 2, :].rearrange("p (h t) -> p h t", h=HB),
                                           ACT.Copy).then_inc(hl_taken, 1)

            @block.tensor
            def _(eng):
                def turn(src, i):
                    for g in range(NCH):
                        if 4 * i + g >= 2:
                            eng.wait_ge(taken, 4 * i + g - 1)
                        for j in range(4):
                            mm = eng.transpose(psA[:, g % 2, j * P:(j + 1) * P], src[:, 4 * g + j, :], ident[:, :])
                        mm.then_inc(turned, 1)

                eng.wait_ge(loaded, 16 * 8)
                turn(attn0, 0)
                for k in range(NT):
                    if k % 4 == 0:
                        eng.wait_ge(taken, k // 4 + 1)
                    if k >= 4:
                        eng.wait_ge(x1_ready, k - 3)
                    eng.matmul(psR[:, k % 4, 0:D], attn0T[:, k * P:(k + 1) * P], w_out[:, :], start=True, stop=True)\
                       .then_inc(out_ps, 1)
                eng.wait_ge(xn_ready, 1)
                turn(xn, 1)
                eng.wait_ge(xa_ready, 1)
                turn(xa, 2)
                for k in range(NT + 1):
                    if k < NT:
                        if k % 4 == 0:
                            eng.wait_ge(taken, 2 * NCH + k // 4 + 1)
                        if k == 0:
                            eng.wait_ge(taken, 3 * NCH)
                        for b in range(6):
                            if k >= 1:
                                if b < 4:
                                    eng.wait_ge(rope_read, 4 * (k - 1) + b + 1)
                                else:
                                    eng.wait_ge(v_low, 2 * (k - 1) + b - 3)
                            dst = psR[:, b, :] if b < 4 else psA[:, b - 4, :]
                            eng.matmul(dst, xaT[:, k * P:(k + 1) * P], w_qkv[:, b * BANK:(b + 1) * BANK],
                                       start=True, stop=True).then_inc(qkv_ps, 1)
                    if k >= 1:
                        kk = k - 1
                        for g in range(4):
                            eng.wait_ge(lo_ready, 4 * kk + g + 1)
                            if 4 * kk + g >= 2:
                                eng.wait_ge(hl_taken, 4 * kk + g - 1)
                            for j in range(HB):
                                mm = eng.transpose(psB[:, g % 2, j * P:(j + 1) * P],
                                                   hl[:, kk % 2, g * HB + j, :, :].rearrange("p a e -> p (a e)"),
                                                   ident_h[:, :])
                            mm.then_inc(hl_ps, 1)


def low_half(eng, hl, ra, rb, u, hi_ready, lo_ready):
    k, b = u // 4, u % 4
    dst = hl[:, k % 2, b * 8:(b + 1) * 8, :, :]
    eng.wait_ge(hi_ready, u + 1)
    eng.tensor_tensor(dst[:, :, 1, :], ra[:, u % 2, :].rearrange("p (h e) -> p h e", h=8), dst[:, :, 0, :],
                      ALU.subtract).then_inc(lo_ready, 1)


def stage_attention1(nc, io, sb):
    attn1, ident = sb["attn1"], sb["ident"]
    KP = NT // 2
    STEPS = NS * KP
    NMX = NT * NCH
    MX0, MX1 = 2, STEPS - 3
    mx_at = [min(NMX, max(0, -(-NMX * (i - MX0) // (MX1 - MX0)))) for i in range(STEPS + 1)]
    LOW, SUM = 2, 3
    with ExitStack() as ctx:
        def t(name, shape, dt=F32):
            return ctx.enter_context(nc.sbuf_tensor(name, shape, dt))

        def sem(name):
            return ctx.enter_context(nc.semaphore(name))

        qa, qb = t("qa", [P, 2, S], F16), t("qb", [P, 2, S], F16)
        ka, kb = t("ka", [P, 2, S], F16), t("kb", [P, 2, S], F16)
        vh = t("vh1", [P, 2, NT, VW], F16)
        pr = t("pr", [P, NPR, 2, SC])
        hi, lo = t("hi", [P, NHL, 2, SC], F16), t("lo", [P, NHL, 2, SC], F16)
        mx4, mx = t("mx4", [P, NT, NCH]), t("mx", [P, NT])
        mrow = t("mrow", [NT, P], F16)
        sums, rden = t("sums", [P, TS, VN]), t("rden", [P, TS])
        s_ps = ctx.enter_context(nc.psum_tensor("s_ps", [P, 2, 2, SC], F32))
        pv_ps = ctx.enter_context(nc.psum_tensor("pv_ps", [P, 2, BANK], F32))
        mx_ps = ctx.enter_context(nc.psum_tensor("mx_ps", [P, 2, BANK], F32))

        const_ready, loaded, mrow_loaded = sem("const_ready"), sem("loaded_d"), sem("mrow_loaded")
        mx_done, mx_taken, mx_ready = sem("mx_done"), sem("mx_taken"), sem("mx_ready")
        mt_ps, mt_copied = sem("mt_ps"), sem("mt_copied")
        s_done, exp_done, hi_done, lo_done = sem("s_done"), sem("exp_done"), sem("hi_done"), sem("lo_done")
        pv_done = sem("pv_done1")
        sums_taken, div_ready, attn_ready = sem("sums_taken"), sem("div_ready"), sem("attn_ready1")
        LOADS = 16 * 5
        v_loaded = sem("v_loaded")

        def head(g, par):
            return 2 * g + par

        def pr_slot(i):
            return pr[:, i % NPR, :, :]

        with nc.Block() as block:
            @block.sync
            def _(sp):
                def load(g, par):
                    h = head(g, par)
                    sp.wait_ge(s_done, STEPS * (h + 1))
                    q, k = io["qk1"][0], io["qk1"][1]
                    for dst, src in ((qa[:, par, :], q[h, :, :]), (ka[0:HD1, par, :], k[h, 0:HD1, :]),
                                     (ka[HD1:P, par, :], k[h, 0:HD1, :]), (qb[0:HD1, par, :], q[h, 0:HD1, :]),
                                     (kb[0:HD1, par, :], k[h, HD1:P, :])):
                        sp.dma_start(dst, src).then_inc(loaded, 16)
                    sp.wait_ge(pv_done, STEPS * (h + 1))
                    sp.dma_start(vh[:, par, :, :].rearrange("p n e -> p (n e)"),
                                 io["v1"][h, :, :, :].rearrange("p n e -> p (n e)")).then_inc(v_loaded, 16)

                def maxima(g, par):
                    sp.wait_ge(mt_copied, head(g, par) + 2)
                    sp.dma_start(qb[HD1:HD1 + 1, par, :].rearrange("a (n t) -> a n t", t=P),
                                 mrow[:, :]).then_inc(mrow_loaded, 16)

                with sp.Fori(0, H // 2) as g:
                    for par in range(2):
                        load(g, par)
                        maxima(g, par)

            @block.vector
            def _(eng):
                for par in range(2):
                    last = eng.memset(kb[HD1:HD1 + 1, par, :], MROW)
                last.then_inc(const_ready, 1)

                def reduce_bank(h, q):
                    eng.wait_ge(mx_done, NMX * h + q + 1)
                    eng.tensor_reduce(mx4[:, q // NCH, q % NCH:q % NCH + 1], mx_ps[:, q % 2, :], AX.X, ALU.max)\
                       .then_inc(mx_taken, 1)

                def maxima(h):
                    eng.wait_ge(mx_taken, NMX * (h + 1) + 2)
                    eng.tensor_reduce(mx[:, :], mx4[:, :, :], AX.X, ALU.max).then_inc(mx_ready, 1)

                def row(h):
                    eng.wait_ge(mt_ps, h + 1)
                    eng.wait_ge(mrow_loaded, 16 * h + 16)
                    eng.tensor_scalar(mrow[:, :], mx_ps[0:NT, 0, 0:P], -1.0 / MROW, None, ALU.mult)\
                       .then_inc(mt_copied, 1)

                def low(h, i):
                    eng.wait_ge(hi_done, STEPS * h + i + 1)
                    eng.wait_ge(pv_done, STEPS * (h + 2) + i + 1 - NHL)
                    eng.tensor_tensor(lo[:, i % NHL, :, :], pr_slot(i), hi[:, i % NHL, :, :],
                                      ALU.subtract).then_inc(lo_done, 1)

                def take(h, c):
                    n_ = NS * h + c
                    eng.wait_ge(sums_taken, n_ + 2)
                    eng.reciprocal(rden[:, :].unsqueeze(2), sums[:, :, HD1:HD1 + 1])
                    eng.tensor_tensor(sums[:, :, 0:HD1], sums[:, :, 0:HD1], sums[:, :, HD1 + 1:VN], ALU.add)\
                       .then_inc(div_ready, 1)
                    eng.wait_ge(div_ready, n_ + 1)
                    eng.tensor_tensor(attn1[:, c * TS:(c + 1) * TS, bass.ds(h * HD1, HD1)], sums[:, :, 0:HD1],
                                      rden[:, :].unsqueeze(2).to_broadcast([P, TS, HD1]), ALU.mult)\
                       .then_inc(attn_ready, 1)

                def one(g, par, first=False, last=False):
                    h = head(g, par)
                    for i in range(STEPS):
                        if not last:
                            for q in range(mx_at[i], mx_at[i + 1]):
                                reduce_bank(h + 1, q)
                            if i == MX1:
                                maxima(h + 1)
                            if i == MX1 + 1:
                                row(h + 1)
                        if i % KP == SUM and not (first and i == SUM):
                            take(h - 1 if i == SUM else h, (i // KP - 1) % NS)
                        if i >= LOW or not first:
                            low(h, i - LOW)
                    if last:
                        for i in range(STEPS - LOW, STEPS):
                            low(h, i)
                        take(h, NS - 1)

                for q in range(NMX):
                    reduce_bank(0, q)
                maxima(0)
                row(0)
                one(0, 0, first=True)
                one(0, 1)
                with eng.Fori(1, H // 2 - 1) as g:
                    one(g, 0)
                    one(g, 1)
                one(H // 2 - 1, 0)
                one(H // 2 - 1, 1, last=True)

            @block.scalar
            def _(eng):
                eng.preload_act_table(ACT.Exp)

                def high(h, i):
                    eng.wait_ge(exp_done, STEPS * h + i + 3)
                    eng.wait_ge(pv_done, STEPS * (h + 2) + i + 1 - NHL)
                    eng.activation(hi[:, i % NHL, :, :], pr_slot(i), ACT.Copy).then_inc(hi_done, 1)

                def take(h, c):
                    eng.wait_ge(attn_ready, NS * h + c + 1)
                    eng.wait_ge(pv_done, STEPS * (h + 2) + (c + 1) * KP)
                    eng.activation(sums[:, :, :].rearrange("p (b j) e -> p b j e", b=2),
                                   pv_ps[:, :, :].rearrange("p b (j e) -> p b j e", e=OW)[:, :, :, 0:VN],
                                   ACT.Copy).then_inc(sums_taken, 1)

                def one(h, first=False, last=False):
                    for i in range(STEPS):
                        eng.wait_ge(s_done, STEPS * (h + 2) + i + 1)
                        eng.wait_ge(lo_done, STEPS * (h + 1) + i + 1 - NPR)
                        eng.activation(pr_slot(i), s_ps[:, i % 2, :, :], ACT.Exp, scale=SM).then_inc(exp_done, 1)
                        if i % KP == SUM and not (first and i == SUM):
                            take(h - 1 if i == SUM else h, (i // KP - 1) % NS)
                        if i >= 1 or not first:
                            high(h, i - 1)
                    if last:
                        high(h, STEPS - 1)
                        take(h, NS - 1)

                one(0, first=True)
                with eng.Fori(1, H - 1) as h:
                    one(h)
                one(H - 1, last=True)

            @block.tensor
            def _(eng):
                def mx_bank(h, par, q):
                    if q == 0:
                        eng.wait_ge(loaded, LOADS * (h + 1))
                        eng.wait_ge(mt_copied, h + 1)
                    eng.wait_ge(mx_taken, NMX * h + q + 1)
                    j, c = q // NCH, q % NCH
                    eng.matmul(mx_ps[:, q % 2, :], qa[:, par, j * P:(j + 1) * P],
                               ka[:, par, c * BANK:(c + 1) * BANK], start=True, stop=True).then_inc(mx_done, 1)

                def mx_turn(h):
                    eng.wait_ge(mx_ready, h + 1)
                    eng.transpose(mx_ps[0:NT, 0, 0:P], mx[:, :], ident[:, :]).then_inc(mt_ps, 1)

                def scores(h, par, i):
                    if i == 0:
                        eng.wait_ge(mrow_loaded, 16 * (h + 2))
                    eng.wait_ge(exp_done, STEPS * h + i + 1)
                    c, kp = i // KP, i % KP
                    w = slice(c * SC, (c + 1) * SC)
                    for n_ in range(2):
                        k = 2 * kp + n_
                        eng.matmul(s_ps[:, i % 2, n_, :], ka[:, par, k * P:(k + 1) * P], qa[:, par, w],
                                   start=True, stop=False)
                        mm = eng.matmul(s_ps[:, i % 2, n_, :], kb[0:HD1 + 1, par, k * P:(k + 1) * P],
                                        qb[0:HD1 + 1, par, w], start=False, stop=True)
                    mm.then_inc(s_done, 1)

                def weigh(h, par, i):
                    c, kp = i // KP % NS, i % KP
                    if i == 0:
                        eng.wait_ge(v_loaded, 16 * (h + 1))
                    if kp == 0:
                        eng.wait_ge(sums_taken, NS * h + c + 1)
                    eng.wait_ge(lo_done, STEPS * (h + 1) + i + 1)
                    for n_ in range(2):
                        k = 2 * kp + n_
                        for j in range(TS):
                            for half in (hi, lo):
                                mm = eng.matmul(pv_ps[:, j // 2, j % 2 * OW:j % 2 * OW + VN],
                                                half[:, i % NHL, n_, j * P:(j + 1) * P], vh[:, par, k, 0:VN],
                                                start=(k == 0 and j % 2 == 0 and half is hi),
                                                stop=(k == NT - 1 and half is lo), skip_group_check=True)
                    mm.then_inc(pv_done, 1)

                def one(g, par, first=False, last=False):
                    h = head(g, par)
                    for i in range(STEPS):
                        q0, q1 = (mx_at[i], mx_at[i + 1]) if not last else (0, 0)
                        for q in range(q0, min(q0 + 1, q1)):
                            mx_bank(h + 1, 1 - par, q)
                        if i + 1 < STEPS:
                            scores(h, par, i + 1)
                        elif not last:
                            scores(h + 1, 1 - par, 0)
                        for q in range(q0 + 1, q1):
                            mx_bank(h + 1, 1 - par, q)
                        if i == MX1 and not last:
                            mx_turn(h + 1)
                        if i >= SUM or not first:
                            weigh(h, par if i >= SUM else 1 - par, i - SUM)
                    if last:
                        for i in range(STEPS - SUM, STEPS):
                            weigh(h, par, i)

                eng.sem_inc(pv_done, 2 * STEPS)
                eng.sem_inc(lo_done, STEPS)
                eng.sem_inc(s_done, 2 * STEPS)
                eng.sem_inc(mx_taken, 2)
                eng.sem_inc(mt_copied, 1)
                eng.sem_inc(exp_done, 2)
                eng.sem_inc(sums_taken, 1)
                eng.sem_inc(attn_ready, 1)
                eng.sem_inc(mrow_loaded, 16)
                eng.wait_ge(const_ready, 1)
                for q in range(NMX):
                    mx_bank(0, 0, q)
                mx_turn(0)
                scores(0, 0, 0)
                one(0, 0, first=True)
                one(0, 1)
                with eng.Fori(1, H // 2 - 1) as g:
                    one(g, 0)
                    one(g, 1)
                one(H // 2 - 1, 0)
                one(H // 2 - 1, 1, last=True)


def stage_output(nc, io, sb):
    base, attn1, xn2T, ident = sb["base"], sb["attn1"], sb["xn2T"], sb["ident"]
    MO = INNER // P
    with ExitStack() as ctx:
        def t(name, shape, dt=F32):
            return ctx.enter_context(nc.sbuf_tensor(name, shape, dt))

        def sem(name):
            return ctx.enter_context(nc.semaphore(name))

        w1, w2 = t("w1", [P, F1]), t("w2", [P, F1])
        h1, h2 = t("h1", [P, M1, F1]), t("h2", [P, M1, F1])
        w3, wo = t("w3", [P, M1, D]), t("wo", [P, MO, D])
        s3 = t("s3", [P, D])
        sc = t("sc", [P, 4, M1])
        ha, hb = t("ha", [P, M1, S]), t("hb", [P, M1, S])
        sil = t("sil1", [P, 2, BANK])
        y = t("y", [P, NT, D])
        psG = ctx.enter_context(nc.psum_tensor("psG1", [P, 2, BANK], F32))
        psU = ctx.enter_context(nc.psum_tensor("psU1", [P, 2, BANK], F32))
        psH = ctx.enter_context(nc.psum_tensor("psH1", [P, 2, BANK], F32))
        psO = ctx.enter_context(nc.psum_tensor("psO1", [P, 2, BANK], F32))
        aT = t("aT", [P, 2, MO, P])
        turned, aT_ready = sem("turned_e"), sem("aT_ready")

        loaded = sem("loaded_e")
        gate_ps, up_ps, sil_ready, ha_ready = sem("gate_ps1"), sem("up_ps1"), sem("sil_ready1"), sem("ha_ready")
        hid_ps, hid_ready = sem("hid_ps"), sem("hid_ready")
        down_ps, out_ps, y_scaled, y_sum, y_ready = (sem("down_ps1"), sem("out_ps_e"), sem("y_scaled"),
                                                     sem("y_sum"), sem("y_ready"))
        stored = sem("stored")
        NM = NCH * M1

        with nc.Block() as block:
            @block.sync
            def _(sp):
                for dst, src in ((w1[:, :], io["w1_t"]), (w2[:, :], io["w2_t"]),
                                 (sc[:, 0, :], io["w1_s"]),
                                 (sc[:, 1, :], io["w2_s"]),
                                 (sc[:, 2, :], io["h1_s"]),
                                 (sc[:, 3, :], io["h2_s"]),
                                 (h1[:, :, :], io["h1_t"].rearrange("(k p) o -> p k o", p=P)),
                                 (h2[:, :, :], io["h2_t"].rearrange("(k p) o -> p k o", p=P)),
                                 (w3[:, :, :], io["w3_t"].rearrange("(k p) o -> p k o", p=P)),
                                 (wo[:, :, :], io["w_out1"].rearrange("(k p) o -> p k o", p=P)),
                                 (s3[:, :], io["w3_s"].partition_broadcast(P))):
                    sp.dma_start(dst, src).then_inc(loaded, 16)
                out = io["out"].rearrange("a (n p) d -> p (a n) d", p=P)
                for g in range(4):
                    sp.wait_ge(y_ready, 4 * g + 4)
                    sp.dma_start(out[:, 4 * g:4 * g + 4, :], y[:, 4 * g:4 * g + 4, :]).then_inc(stored, 16)
                sp.wait_ge(stored, 64)

            @block.tensor
            def _(eng):
                eng.wait_ge(loaded, 16 * 11)
                for k in range(NM):
                    n_, m = k // M1, k % M1
                    rhs = xn2T[:, n_ * BANK:(n_ + 1) * BANK]
                    if k >= 2:
                        eng.wait_ge(sil_ready, k - 1)
                        eng.wait_ge(ha_ready, k - 1)
                    eng.matmul(psG[:, k % 2, :], w1[:, m * P:(m + 1) * P], rhs, start=True, stop=True)\
                       .then_inc(gate_ps, 1)
                    eng.matmul(psU[:, k % 2, :], w2[:, m * P:(m + 1) * P], rhs, start=True, stop=True)\
                       .then_inc(up_ps, 1)
                for l, (w, src) in enumerate(((h1, ha), (h2, hb))):
                    for k in range(NM):
                        n_, m = k // M1, k % M1
                        if m == 0:
                            eng.wait_ge((ha_ready, hid_ready)[l], (n_ + 1) * M1)
                        if l * NM + k >= 2:
                            eng.wait_ge(hid_ready, l * NM + k - 1)
                        for j in range(M1):
                            mm = eng.matmul(psH[:, k % 2, :], w[:, j, m * P:(m + 1) * P],
                                            src[:, j, n_ * BANK:(n_ + 1) * BANK], start=(j == 0), stop=(j == M1 - 1))
                        mm.then_inc(hid_ps, 1)
                def turn(k):
                    for b in range(2):
                        if k >= 1:
                            eng.wait_ge(aT_ready, 2 * (k - 1) + b + 1)
                        for j in range(4):
                            mm = eng.transpose(psU[:, b, j * P:(j + 1) * P],
                                               attn1[:, k, (4 * b + j) * P:(4 * b + j + 1) * P], ident[:, :])
                        mm.then_inc(turned, 1)

                turn(0)
                for k in range(NT):
                    if k + 1 < NT:
                        turn(k + 1)
                    if k % 4 == 0:
                        eng.wait_ge(hid_ready, NM + (k // 4 + 1) * M1)
                    if k >= 2:
                        eng.wait_ge(y_sum, k - 1)
                    for j in range(M1):
                        mm = eng.matmul(psG[:, k % 2, 0:D], ha[:, j, k * P:(k + 1) * P], w3[:, j, :],
                                        start=(j == 0), stop=(j == M1 - 1))
                    mm.then_inc(down_ps, 1)
                    eng.wait_ge(aT_ready, 2 * k + 2)
                    for j in range(MO):
                        mm = eng.matmul(psO[:, k % 2, 0:D], aT[:, k % 2, j, :], wo[:, j, :],
                                        start=(j == 0), stop=(j == MO - 1))
                    mm.then_inc(out_ps, 1)

            @block.scalar
            def _(eng):
                for k in range(NM):
                    m = k % M1
                    eng.wait_ge(gate_ps, k + 1)
                    if k >= 2:
                        eng.wait_ge(ha_ready, k - 1)
                    eng.activation(sil[:, k % 2, :], psG[:, k % 2, :], ACT.Silu, scale=sc[:, 0, m:m + 1])\
                       .then_inc(sil_ready, 1)
                for l, dst in enumerate((hb, ha)):
                    for k in range(NM):
                        n_, m = k // M1, k % M1
                        eng.wait_ge(hid_ps, l * NM + k + 1)
                        eng.activation(dst[:, m, n_ * BANK:(n_ + 1) * BANK], psH[:, k % 2, :], ACT.Gelu,
                                       scale=sc[:, 2 + l, m:m + 1]).then_inc(hid_ready, 1)
                for k in range(NT):
                    for b in range(2):
                        eng.wait_ge(turned, 2 * k + b + 1)
                        if k >= 2:
                            eng.wait_ge(out_ps, k - 1)
                        eng.activation(aT[:, k % 2, 4 * b:4 * b + 4, :],
                                       psU[:, b, :].rearrange("p (j t) -> p j t", j=4), ACT.Copy)\
                           .then_inc(aT_ready, 1)

            @block.vector
            def _(eng):
                for k in range(NM):
                    n_, m = k // M1, k % M1
                    eng.wait_ge(up_ps, k + 1)
                    eng.wait_ge(sil_ready, k + 1)
                    eng.scalar_tensor_tensor(out=ha[:, m, n_ * BANK:(n_ + 1) * BANK], in0=psU[:, k % 2, :],
                                             scalar=sc[:, 1, m:m + 1], in1=sil[:, k % 2, :], op0=ALU.mult,
                                             op1=ALU.mult).then_inc(ha_ready, 1)
                for k in range(NT):
                    eng.wait_ge(down_ps, k + 1)
                    eng.tensor_tensor(y[:, k, :], psG[:, k % 2, 0:D], s3[:, :], ALU.mult).then_inc(y_scaled, 1)
                    eng.wait_ge(y_scaled, k + 1)
                    eng.wait_ge(out_ps, k + 1)
                    eng.tensor_tensor(y[:, k, :], y[:, k, :], psO[:, k % 2, 0:D], ALU.add).then_inc(y_sum, 1)
                    eng.wait_ge(y_sum, k + 1)
                    eng.tensor_tensor(y[:, k, :], y[:, k, :], base[:, k, :], ALU.add).then_inc(y_ready, 1)


def program(nc, io, debug=None):
    with ExitStack() as ctx:
        def keep(stack, name, shape, dt=F32):
            return stack.enter_context(nc.sbuf_tensor(name, shape, dt))

        sb = dict(ident=keep(ctx, "ident", [P, P]), base=keep(ctx, "base", [P, NT, D]),
                  xn2T=keep(ctx, "xn2T", [P, S]))
        with ExitStack() as layer0:
            sb |= dict(ident_b=keep(layer0, "ident_b", [P, P], BF16), v0=keep(layer0, "v0", [P, NT, D]),
                       attn0=keep(layer0, "attn0", [P, NT, D]))
            stage_project0(nc, io, sb)
            stage_attention0(nc, io, sb)
            stage_project1(nc, io, sb)
        with ExitStack() as layer1:
            sb |= dict(attn1=keep(layer1, "attn1", [P, NT, INNER]))
            stage_attention1(nc, io, sb)
            stage_output(nc, io, sb)


DEBUG = None


def kernel(**inputs):
    import numpy as _np
    import concourse.bacc as _bacc
    from concourse.bass_utils import run_bass_kernel_spmd as _run

    a = {k: _np.asarray(v) for k, v in inputs.items()}
    half = HD1 // 2
    freq = (_np.float32(1.0) / _np.float32(10000.0) ** (_np.arange(0, HD1, 2, dtype=_np.float32)
                                                        / _np.float32(HD1))).astype(_np.float32)
    ang = _np.arange(S, dtype=_np.float32)[:, None] * freq[None, :]
    cos_t = (QS * _np.cos(ang)).astype(_np.float32)
    sin_t = (QS * _np.sin(ang)).astype(_np.float32)
    ins = {
        "x": a["L0_attn_x"],
        "ident": _np.eye(P, dtype=_np.float32),
        "cos_t": cos_t,
        "sin_t": _np.stack([-sin_t, sin_t], axis=1),
        "w_qkv0_t": a["L0_attn_w_qkv"].T,
        "b_qkv0": a["L0_attn_b_qkv"],
        "w_out0_t": a["L0_attn_w_out"].T,
        "b_out0": a["L0_attn_b_out"],
        "w_gate_t": a["L0_ffn_w_gate"].T,
        "w_up_t": a["L0_ffn_w_up"].T,
        "w_down_t": a["L0_ffn_w_down"].T,
        "gamma": a["L1_attn_ln_gamma"],
        "beta": a["L1_attn_ln_beta"],
        "w_qkv1": a["L1_attn_w_qkv"],
        "w_out1": a["L1_attn_w_out"],
        "b_out1": a["L1_attn_b_out"],
        "w1_t": a["L1_ffn_w1_w"].T, "w1_s": a["L1_ffn_w1_s"].reshape(M1, P).T,
        "w2_t": a["L1_ffn_w2_w"].T, "w2_s": a["L1_ffn_w2_s"].reshape(M1, P).T,
        "h1_t": a["L1_ffn_h1_w"].T, "h1_s": a["L1_ffn_h1_s"].reshape(M1, P).T,
        "h2_t": a["L1_ffn_h2_w"].T, "h2_s": a["L1_ffn_h2_s"].reshape(M1, P).T,
        "w3_t": a["L1_ffn_w3_w"].T, "w3_s": a["L1_ffn_w3_s"],
    }
    nc = _bacc.Bacc("TRN2", target_bir_lowering=False, num_devices=1)
    arrays, io = {}, {}
    for name, v in ins.items():
        v = _np.ascontiguousarray(v)
        arrays[f"in_{name}"] = v
        io[name] = nc.dram_tensor(f"in_{name}", v.shape, mybir.dt.from_np(v.dtype), kind="ExternalInput").ap()
    io["parts"] = nc.dram_tensor("parts_dram", (NPART, 2, H, HD0, S), BF16).ap()
    io["qk1"] = nc.dram_tensor("qk1", (2, H, P, S), F16).ap()
    io["v1"] = nc.dram_tensor("v1", (H, P, NT, VW), F16).ap()
    io["out"] = nc.dram_tensor("out", (1, S, D), F32, kind="ExternalOutput").ap()
    program(nc, io, DEBUG)
    r = _run(nc, [arrays], core_ids=[0])
    return r.results[0]["out"]
```

```python
from contextlib import ExitStack
import math

import concourse.bass as bass
from concourse import mybir

ALU = mybir.AluOpType
ACT = mybir.ActivationFunctionType
AX = mybir.AxisListType
F32 = mybir.dt.float32
BF16 = mybir.dt.bfloat16
F16 = mybir.dt.float16
I32 = mybir.dt.int32

P = 128
S = 2048
D = 128
NT = S // P
BANK = 512
NCH = S // BANK
H = 16

HD0 = D // H
F0 = 384
M0 = F0 // P
DEQ = 1.0 / 127.0
NPART = 3
KST = NPART * NPART * HD0
GEXP = -3.2
HALF_PI = math.pi / 2
BT = 8
H_POLY = (1.55792178484, -0.644009720053, 0.259267954814, -0.0718242089177, 0.00936488352299)
VC = 32

HD1 = 64
INNER = H * HD1
F1 = 512
M1 = F1 // P
QS = 16.0
MROW = 2048.0
SM = 1.0 / (math.sqrt(HD1) * QS * QS)
SC = BANK
NS = S // SC
TS = SC // P
VW = 2 * HD1 + 2
VN = 2 * HD1 + 1
OW = BANK // 2
NPR = 8
NHL = 8


def stage_project0(nc, io, sb):
    v0, base, ident, ident_b = sb["v0"], sb["base"], sb["ident"], sb["ident_b"]
    with ExitStack() as ctx:
        def t(name, shape, dt=F32):
            return ctx.enter_context(nc.sbuf_tensor(name, shape, dt))

        def sem(name):
            return ctx.enter_context(nc.semaphore(name))

        x_in = t("x_in", [P, NT, D])
        xn = t("xn0", [P, NT, D])
        xnT = t("xnT0", [P, S])
        stats = t("stats0", [P, NT, 6])
        mv = t("mv0", [P, NT, 2])
        var = t("var0", [P, NT])
        sd = t("sd0", [P, NT])
        tmp = t("tmp0", [P, NT])
        w_qkv = t("w_qkv0", [P, 3 * D])
        b_qkv = t("b_qkv0", [P, 3 * D])
        wg_i = t("wg_i", [P, F0], I32)
        wu_i = t("wu_i", [P, F0], I32)
        wd_i = t("wd_i", [P, M0, D], I32)
        wg = t("wg", [P, F0])
        wu = t("wu", [P, F0])
        wd = t("wd", [P, M0, D])
        qk = t("qk0", [P, NT, 2 * D])
        sq = t("sq0", [P, NT, 2 * D])
        n2 = t("n2", [P, NT * 2 * H])
        nrm = t("nrm", [P, NT * 2 * H])
        ntmp = t("ntmp", [P, NT * 2 * H])
        parts = t("parts", [P, NPART, NT, 2 * D], BF16)
        stg = t("stg", [P, NPART, 2, S], BF16)
        hT = t("hT0", [P, M0, S])
        sil = t("sil0", [P, 2, BANK])
        psT = ctx.enter_context(nc.psum_tensor("psT0", [P, 2, BANK], F32))
        psQ = ctx.enter_context(nc.psum_tensor("psQ0", [P, 2, BANK], F32))
        psG = ctx.enter_context(nc.psum_tensor("psG0", [P, 2, BANK], F32))
        psU = ctx.enter_context(nc.psum_tensor("psU0", [P, 2, BANK], F32))

        x_loaded, w_loaded = sem("x_loaded0"), sem("w_loaded0")
        wq_loaded = sem("wq_loaded0")
        dve = sem("dve_chain0")
        var_ready, sd_ready, xn_ready = sem("var_ready0"), sem("sd_ready0"), sem("xn_ready0")
        w_cast = sem("w_cast0")
        xT_ps, xT_ready = sem("xT_ps0"), sem("xT_ready0")
        qkv_ps, qkv_taken = sem("qkv_ps0"), sem("qkv_taken0")
        n2_ready, nrm_ready, parts_ready = sem("n2_ready"), sem("nrm_ready"), sem("parts_ready")
        gate_ps, up_ps, sil_ready, h_ready = sem("gate_ps0"), sem("up_ps0"), sem("sil_ready0"), sem("h_ready0")
        pt_ps, pt_ready, parts_stored = sem("pt_ps"), sem("pt_ready"), sem("parts_stored")
        down_ps, base_ready = sem("down_ps0"), sem("base_ready0")
        psTb = psT[:, :, :].rearrange("p a b -> p (a b)").bitcast(BF16).rearrange("p (a b) -> p a b", a=2)

        with nc.Block() as block:
            @block.sync
            def _(sp):
                sp.dma_start(x_in[:, :, :], io["x"].rearrange("a (n p) d -> p (a n) d", p=P)).then_inc(x_loaded, 16)
                sp.dma_start(ident[:, :], io["ident"]).then_inc(wq_loaded, 16)
                sp.dma_start(w_qkv[:, :], io["w_qkv0_t"]).then_inc(wq_loaded, 16)
                sp.dma_start(b_qkv[:, :], io["b_qkv0"].partition_broadcast(P)).then_inc(wq_loaded, 16)
                sp.dma_start(wg_i[:, :], io["w_gate_t"]).then_inc(w_loaded, 16)
                sp.dma_start(wu_i[:, :], io["w_up_t"]).then_inc(w_loaded, 16)
                sp.dma_start(wd_i[:, :, :], io["w_down_t"].rearrange("(m p) d -> p m d", p=P)).then_inc(w_loaded, 16)
                for i in range(NPART):
                    for x in range(2):
                        sp.wait_ge(pt_ready, 2 * (2 * i + x) + 2)
                        sp.dma_start(io["parts"][i, x].rearrange("h d t -> (h d) t"), stg[:, i, x, :])\
                          .then_inc(parts_stored, 16)
                sp.wait_ge(parts_stored, 16 * 2 * NPART)

            @block.vector
            def _(eng):
                n = [0]

                def link(ins):
                    n[0] += 1
                    ins.then_inc(dve, 1)
                    eng.wait_ge(dve, n[0])

                eng.wait_ge(x_loaded, 16)
                for k in range(NT):
                    last = eng.bn_stats(stats[:, k, :], x_in[:, k, :])
                link(last)
                for k in range(NT):
                    last = eng.bn_aggr(mv[:, k, :], stats[:, k, :])
                link(last)
                eng.tensor_scalar(var[:, :], mv[:, :, 1], 1e-5, None, ALU.add).then_inc(var_ready, 1)
                eng.wait_ge(sd_ready, 1)
                link(eng.reciprocal(tmp[:, :], sd[:, :]))
                link(eng.tensor_tensor(tmp[:, :], tmp[:, :], var[:, :], ALU.mult))
                link(eng.tensor_tensor(tmp[:, :], tmp[:, :], sd[:, :], ALU.add))
                link(eng.reciprocal(tmp[:, :], tmp[:, :]))
                link(eng.tensor_scalar(tmp[:, :], tmp[:, :], 2.0, None, ALU.mult))
                for k in range(NT):
                    eng.tensor_scalar(xn[:, k, :], x_in[:, k, :], mv[:, k, 0:1], tmp[:, k:k + 1],
                                      ALU.subtract, ALU.mult).then_inc(xn_ready, 1)
                eng.wait_ge(wq_loaded, 48)
                eng.tensor_copy(ident_b[:, :], ident[:, :])
                eng.wait_ge(w_loaded, 48)
                eng.tensor_copy(wg[:, :], wg_i[:, :])
                eng.tensor_copy(wu[:, :], wu_i[:, :])
                eng.tensor_copy(wd[:, :, :], wd_i[:, :, :]).then_inc(w_cast, 1)
                for k in range(NT):
                    eng.wait_ge(qkv_ps, k + 1)
                    eng.tensor_tensor(qk[:, k, :], psQ[:, k % 2, 0:2 * D], b_qkv[:, 0:2 * D], ALU.add)
                    last = eng.tensor_tensor(v0[:, k, :], psQ[:, k % 2, 2 * D:3 * D], b_qkv[:, 2 * D:3 * D], ALU.add)
                    last.then_inc(qkv_taken, 1)
                eng.wait_ge(qkv_taken, NT)
                link(eng.tensor_tensor(sq[:, :, :], qk[:, :, :], qk[:, :, :], ALU.mult))
                groups = sq[:, :, :].rearrange("p n (g d) -> p (n g) d", d=HD0)
                eng.tensor_reduce(n2[:, :], groups, AX.X, ALU.add).then_inc(n2_ready, 1)
                eng.wait_ge(nrm_ready, 1)
                link(eng.tensor_scalar(nrm[:, :], nrm[:, :], 1e-30, None, ALU.max))
                link(eng.reciprocal(ntmp[:, :], nrm[:, :]))
                link(eng.tensor_tensor(ntmp[:, :], ntmp[:, :], n2[:, :], ALU.mult))
                link(eng.tensor_tensor(ntmp[:, :], ntmp[:, :], nrm[:, :], ALU.add))
                link(eng.tensor_scalar(ntmp[:, :], ntmp[:, :], 0.5, 1e-12, ALU.mult, ALU.max))
                link(eng.reciprocal(nrm[:, :], ntmp[:, :]))
                spread = nrm[:, :].unsqueeze(2).to_broadcast([P, NT * 2 * H, HD0])
                qk_g = qk[:, :, :].rearrange("p n (g d) -> p (n g) d", d=HD0)
                link(eng.tensor_tensor(groups, qk_g, spread, ALU.mult))
                link(eng.tensor_copy(parts[:, 0, :, :], sq[:, :, :]))
                link(eng.tensor_tensor(qk[:, :, :], sq[:, :, :], parts[:, 0, :, :], ALU.subtract))
                link(eng.tensor_copy(parts[:, 1, :, :], qk[:, :, :]))
                eng.tensor_tensor(parts[:, 2, :, :], qk[:, :, :], parts[:, 1, :, :], ALU.subtract)\
                   .then_inc(parts_ready, 1)
                for k in range(NCH * M0):
                    n_, m = k // M0, k % M0
                    eng.wait_ge(up_ps, k + 1)
                    eng.wait_ge(sil_ready, k + 1)
                    eng.scalar_tensor_tensor(out=hT[:, m, n_ * BANK:(n_ + 1) * BANK], in0=psU[:, k % 2, :],
                                             scalar=DEQ, in1=sil[:, k % 2, :], op0=ALU.mult,
                                             op1=ALU.mult).then_inc(h_ready, 1)
                for k in range(NT):
                    eng.wait_ge(down_ps, k + 1)
                    eng.scalar_tensor_tensor(out=base[:, k, :], in0=psQ[:, k % 2, 0:D], scalar=DEQ,
                                             in1=x_in[:, k, :], op0=ALU.mult, op1=ALU.add).then_inc(base_ready, 1)

            @block.scalar
            def _(eng):
                eng.wait_ge(var_ready, 1)
                eng.activation(sd[:, :], var[:, :], ACT.Sqrt).then_inc(sd_ready, 1)
                for g in range(NCH):
                    eng.wait_ge(xT_ps, g + 1)
                    eng.activation(xnT[:, g * BANK:(g + 1) * BANK], psT[:, g % 2, :], ACT.Copy).then_inc(xT_ready, 1)
                eng.wait_ge(n2_ready, 1)
                eng.activation(nrm[:, :], n2[:, :], ACT.Sqrt).then_inc(nrm_ready, 1)
                for k in range(NCH * M0):
                    eng.wait_ge(gate_ps, k + 1)
                    if k >= 2:
                        eng.wait_ge(h_ready, k - 1)
                    eng.activation(sil[:, k % 2, :], psG[:, k % 2, :], ACT.Silu, scale=DEQ).then_inc(sil_ready, 1)
                for k in range(2 * NPART * 2):
                    i, x, g = k // 4, k // 2 % 2, k % 2
                    eng.wait_ge(pt_ps, k + 1)
                    eng.activation(stg[:, i, x, g * 1024:(g + 1) * 1024], psTb[:, k % 2, :],
                                   ACT.Copy).then_inc(pt_ready, 1)

            @block.tensor
            def _(eng):
                eng.wait_ge(wq_loaded, 48)
                for g in range(NCH):
                    if g >= 2:
                        eng.wait_ge(xT_ready, g - 1)
                    for j in range(4):
                        k = 4 * g + j
                        eng.wait_ge(xn_ready, k + 1)
                        mm = eng.transpose(psT[:, g % 2, j * P:(j + 1) * P], xn[:, k, :], ident[:, :])
                    mm.then_inc(xT_ps, 1)
                for k in range(NT):
                    if k % 4 == 0:
                        eng.wait_ge(xT_ready, k // 4 + 1)
                    if k >= 2:
                        eng.wait_ge(qkv_taken, k - 1)
                    eng.matmul(psQ[:, k % 2, 0:3 * D], xnT[:, k * P:(k + 1) * P], w_qkv[:, :],
                               start=True, stop=True).then_inc(qkv_ps, 1)
                eng.wait_ge(w_cast, 1)
                for k in range(NCH * M0):
                    n_, m = k // M0, k % M0
                    rhs = xnT[:, n_ * BANK:(n_ + 1) * BANK]
                    if k >= 2:
                        eng.wait_ge(sil_ready, k - 1)
                        eng.wait_ge(h_ready, k - 1)
                    eng.matmul(psG[:, k % 2, :], wg[:, m * P:(m + 1) * P], rhs, start=True, stop=True)\
                       .then_inc(gate_ps, 1)
                    eng.matmul(psU[:, k % 2, :], wu[:, m * P:(m + 1) * P], rhs, start=True, stop=True)\
                       .then_inc(up_ps, 1)
                eng.wait_ge(parts_ready, 1)
                for k in range(2 * NPART * 2):
                    i, x, g = k // 4, k // 2 % 2, k % 2
                    if k >= 2:
                        eng.wait_ge(pt_ready, k - 1)
                    for j in range(8):
                        mm = eng.transpose(psTb[:, k % 2, j * P:(j + 1) * P],
                                           parts[:, i, 8 * g + j, x * D:(x + 1) * D], ident_b[:, :])
                    mm.then_inc(pt_ps, 1)
                eng.wait_ge(h_ready, NCH * M0)
                for k in range(NT):
                    if k >= 2:
                        eng.wait_ge(base_ready, k - 1)
                    for m in range(M0):
                        mm = eng.matmul(psQ[:, k % 2, 0:D], hT[:, m, k * P:(k + 1) * P], wd[:, m, :],
                                        start=(m == 0), stop=(m == M0 - 1))
                    mm.then_inc(down_ps, 1)


def stage_attention0(nc, io, sb):
    v0, attn0, ident = sb["v0"], sb["attn0"], sb["ident"]
    BJ = BT // 2
    CPOS = 1.0 - 2.0 ** -23
    LN_MIN = math.log(2.0 ** -23)
    D_MAX = math.log(1.0 + CPOS) - LN_MIN
    U_MIN = math.sqrt((1.0 - CPOS) / 2)
    A4 = H_POLY[4]
    STEPS = 7
    Z_SCALE = math.sqrt(2.0) * A4
    Z_MAX = (math.acos(-CPOS) - HALF_PI) / Z_SCALE
    with ExitStack() as ctx:
        def t(name, shape, dt=F32):
            return ctx.enter_context(nc.sbuf_tensor(name, shape, dt))

        def sem(name):
            return ctx.enter_context(nc.semaphore(name))

        qst = t("qst", [KST, S], BF16)
        kst = t("kst", [KST, S], BF16)
        wt = t("wt", [P, BJ, S])
        wp = t("wp", [P, 2, BJ, S])
        aux = t("aux", [P, BJ + 1, S])
        s_buf = t("s_buf", [P, S])
        n_c = t("n_c", [P, NT])
        r_c = t("r_c", [P, NT])
        vh = t("vh", [P, NT, VC])
        o_sb = t("o_sb", [P, BANK])
        small = t("small0", [P, NT, 4])
        theta_bias, half_bias = t("theta_bias", [P, 1]), t("half_bias", [P, 1])
        c_ps = ctx.enter_context(nc.psum_tensor("c_ps", [P, 2, 2 * BANK], F32))
        o_ps = ctx.enter_context(nc.psum_tensor("o_ps", [P, BANK], F32))
        t_ps = ctx.enter_context(nc.psum_tensor("t_ps", [P, 4, P], F32))

        const_ready, stacks_loaded = sem("const_ready0"), sem("stacks_loaded")
        cos_ps, cos_read = sem("cos_ps"), sem("cos_read")
        diff_ready = sem("diff_ready")
        tanh_ready, atan_ready = sem("tanh_ready"), sem("atan_ready")
        poly, poly_ready, guard = sem("poly"), sem("poly_ready"), sem("guard")
        lnth_ready, score_ready = sem("lnth_ready"), sem("score_ready")
        rc_ready, vh_ready, pv_done = sem("rc_ready"), sem("vh_ready"), sem("pv_done")
        o_copied, o_turned, attn_ready = sem("o_copied"), sem("o_turned"), sem("attn_ready")
        rows_done = sem("rows_done")

        def w_slot(b, j):
            return j if j < BJ - 1 else BJ - 1 + b

        def halves_read(n, i):
            return 2 * (BT * n + i) + 2 + 2

        def place_p(n, j):
            return BT * n + j

        def place_t(n, j):
            return BT * n + BJ + j

        def before(h, b):
            return (h, 0) if b == 1 else (h - 1, 1)

        with nc.Block() as block:
            @block.sync
            def _(sp):
                with sp.Fori(0, H) as h:
                    sp.wait_ge(cos_ps, 2 * NT * h + 2)
                    for i in range(NPART):
                        for j in range(NPART):
                            row = HD0 * (NPART * j + i)
                            sp.dma_start(qst[row:row + HD0, :], io["parts"][i, 0, h, :, :]).then_inc(stacks_loaded, 16)
                            sp.dma_start(kst[row:row + HD0, :], io["parts"][j, 1, h, :, :]).then_inc(stacks_loaded, 16)
                for name, src in (("w_out0", io["w_out0_t"]), ("b_out0", io["b_out0"].partition_broadcast(P)),
                                  ("gamma", io["gamma"].partition_broadcast(P)),
                                  ("beta", io["beta"].partition_broadcast(P)),
                                  ("b_out1", io["b_out1"].partition_broadcast(P)), ("w_qkv1", io["w_qkv1"])):
                    sp.dma_start(sb[name][:, :], src).then_inc(sb["weights1_loaded"], 16)

            @block.vector
            def _(eng):
                eng.memset(theta_bias[:, :], 1.0 + HALF_PI)
                eng.memset(half_bias[:, :], 0.5)
                eng.memset(vh[:, :, HD0 + 2:VC], 0.0)
                eng.memset(vh[:, :, HD0 + 1:HD0 + 2], 1.0).then_inc(const_ready, 1)

                def difference(n, j):
                    eng.wait_ge(cos_read, halves_read(n, j))
                    eng.scalar_tensor_tensor(out=wt[:, j, :], in0=wt[:, j, :], scalar=LN_MIN, in1=aux[:, j % 2, :],
                                             op0=ALU.max, op1=ALU.subtract).then_inc(guard, 1)

                def limit(n, j):
                    eng.wait_ge(guard, BJ * n + j + 1)
                    eng.tensor_scalar(wt[:, j, :], wt[:, j, :], D_MAX, None, ALU.min).then_inc(diff_ready, 1)

                def poly_step(n, b, j, i):
                    u, w = wp[:, b, j, :], aux[:, w_slot(b, j), :]
                    at = (STEPS - 1) * (BJ * n + j)
                    if i == 0:
                        eng.wait_ge(cos_read, halves_read(n, BJ + j))
                        if not (isinstance(n, int) and n == 0 and j == 0):
                            eng.wait_ge(poly, at)
                        eng.scalar_tensor_tensor(out=s_buf[:, :], in0=u, scalar=U_MIN, in1=w, op0=ALU.max,
                                                 op1=ALU.subtract).then_inc(poly, 1)
                    elif i == 1:
                        eng.wait_ge(poly, at + 1)
                        eng.scalar_tensor_tensor(out=w, in0=u, scalar=U_MIN, in1=w, op0=ALU.max,
                                                 op1=ALU.add).then_inc(poly, 1)
                    elif i < STEPS - 1:
                        eng.wait_ge(poly, at + i)
                        eng.scalar_tensor_tensor(out=u, in0=w if i == 2 else u, scalar=H_POLY[5 - i] / A4,
                                                 in1=s_buf[:, :] if i == STEPS - 2 else w, op0=ALU.add,
                                                 op1=ALU.mult).then_inc(poly, 1)
                    else:
                        eng.wait_ge(poly, at + STEPS - 1)
                        eng.tensor_scalar(u, u, Z_MAX, None, ALU.min).then_inc(poly_ready, 1)

                def values(h, k, place, many):
                    eng.wait_ge(score_ready, place + many)
                    if not (isinstance(h, int) and h == 0):
                        eng.wait_ge(pv_done, place - NT + many)
                    recip = r_c[:, k:k + many]
                    eng.reciprocal(recip, n_c[:, k:k + many]).then_inc(rc_ready, many)
                    eng.wait_ge(rc_ready, place + many)
                    eng.tensor_copy(vh[:, k:k + many, HD0:HD0 + 1], recip.unsqueeze(2))
                    eng.tensor_tensor(vh[:, k:k + many, 0:HD0], v0[:, k:k + many, bass.ds(h * HD0, HD0)],
                                      recip.unsqueeze(2).to_broadcast([P, many, HD0]), ALU.mult)\
                       .then_inc(vh_ready, many)

                def finish(h):
                    eng.wait_ge(pv_done, NT * (h + 1) + BJ)
                    eng.tensor_copy(o_sb[:, :], o_ps[:, :]).then_inc(o_copied, 1)

                def finish_rows(h):
                    eng.wait_ge(o_turned, h + 1)
                    rows = t_ps[:, :, :].rearrange("p j (c r) -> p c j r", r=VC)
                    quad = small[:, :, :].rearrange("p (c j) r -> p c j r", j=4)
                    eng.reciprocal(quad[:, :, :, 0:1], rows[:, :, :, HD0 + 1:HD0 + 2]).then_inc(rows_done, 1)
                    eng.wait_ge(rows_done, h * 5 + 1)
                    eng.tensor_tensor(quad[:, :, :, 1:2], rows[:, :, :, HD0:HD0 + 1], quad[:, :, :, 0:1],
                                      ALU.mult).then_inc(rows_done, 1)
                    eng.wait_ge(rows_done, h * 5 + 2)
                    eng.tensor_scalar(small[:, :, 1:2], small[:, :, 1:2], 1e-12, None, ALU.max).then_inc(rows_done, 1)
                    eng.wait_ge(rows_done, h * 5 + 3)
                    eng.reciprocal(small[:, :, 2:3], small[:, :, 1:2]).then_inc(rows_done, 1)
                    eng.wait_ge(rows_done, h * 5 + 4)
                    eng.tensor_tensor(small[:, :, 3:4], small[:, :, 2:3], small[:, :, 0:1], ALU.mult)\
                       .then_inc(rows_done, 1)
                    eng.wait_ge(rows_done, h * 5 + 5)
                    for c in range(4):
                        last = eng.tensor_tensor(attn0[:, 4 * c:4 * c + 4, bass.ds(h * HD0, HD0)],
                                                 t_ps[:, :, VC * c:VC * c + HD0],
                                                 small[:, 4 * c:4 * c + 4, 3:4].to_broadcast([P, 4, HD0]), ALU.mult)
                    last.then_inc(attn_ready, 1)

                CUT = 5
                P_AT, FINISH_AT, T_AT = (11, 13), 14, (14, 15, 16, 17)
                P_FROM, T_FROM = (0, 2, BJ), (0, 1, 2, 3, BJ)

                def round_(h, b, first=False):
                    n = 2 * h + b
                    for j in range(BJ):
                        difference(n, j)
                        if j > 0:
                            limit(n, j - 1)
                    limit(n, BJ - 1)
                    hp, bp = before(h, b)
                    if not first:
                        for i in range(2 * STEPS + CUT, BJ * STEPS):
                            poly_step(n - 1, bp, i // STEPS, i % STEPS)
                    for i in range(2 * STEPS + CUT):
                        poly_step(n, b, i // STEPS, i % STEPS)
                        if i in P_AT and not first:
                            j = P_AT.index(i)
                            values(hp, BT * bp + BJ + P_FROM[j], place_p(n, P_FROM[j]), P_FROM[j + 1] - P_FROM[j])
                        if i == FINISH_AT and b == 0 and not first:
                            finish(hp)
                        if i == FINISH_AT + 1 and b == 0 and not first:
                            finish_rows(hp)
                        if i in T_AT:
                            j = T_AT.index(i)
                            values(h, BT * b + T_FROM[j], place_t(n, T_FROM[j]), T_FROM[j + 1] - T_FROM[j])

                round_(0, 0, first=True)
                round_(0, 1)
                with eng.Fori(1, H) as h:
                    round_(h, 0)
                    round_(h, 1)
                for i in range(2 * STEPS + CUT, BJ * STEPS):
                    poly_step(2 * H - 1, 1, i // STEPS, i % STEPS)
                values(H - 1, NT - BJ, place_p(2 * H, 0), BJ)
                finish(H - 1)
                finish_rows(H - 1)

            @block.scalar
            def _(eng):
                def halves(n, j0, func_a, func_b, j):
                    for i in range(2):
                        eng.wait_ge(cos_ps, 2 * (BT * n + j0 + j) + i + 1 + 2)
                        w = slice(i * 2 * BANK, (i + 1) * 2 * BANK)
                        func_a(w, c_ps[:, i, :])
                        func_b(w, c_ps[:, i, :]).then_inc(cos_read, 1)

                def logs(n, j, first):
                    if not first:
                        eng.wait_ge(pv_done, place_t(n - 1, j) + 1)
                    if j < 2:
                        if not first:
                            eng.wait_ge(poly_ready, BJ * (n - 1) + j + 1)
                    else:
                        eng.wait_ge(guard, BJ * n + j - 1)
                    halves(n, 0, lambda w, c: eng.activation(wt[:, j, w], c, ACT.Ln, bias=1.0, scale=1.0),
                           lambda w, c: eng.activation(aux[:, j % 2, w], c, ACT.Ln, bias=1.0, scale=-1.0), j)

                def roots(n, b, j, first):
                    if not first:
                        eng.wait_ge(pv_done, place_p(n - 1, j) + 1)
                    if j == 2 and not first:
                        eng.wait_ge(poly_ready, BJ * (n - 1) + 3)
                    halves(n, BJ, lambda w, c: eng.activation(wp[:, b, j, w], c, ACT.Sqrt, scale=-0.5,
                                                              bias=half_bias[:, 0:1]),
                           lambda w, c: eng.activation(aux[:, w_slot(b, j), w], c, ACT.Sqrt, scale=0.5,
                                                       bias=half_bias[:, 0:1]), j)

                def scores(tile, n, at, scale, place, tiles, first):
                    for g in range(2):
                        eng.activation(tile[:, 2 * g:2 * g + 2, :], tile[:, 2 * g:2 * g + 2, :], ACT.Ln, scale=scale,
                                       bias=theta_bias[:, 0:1]).then_inc(lnth_ready, 1)
                    for j in range(BJ):
                        if j % 2 == 0:
                            eng.wait_ge(lnth_ready, at + j // 2 + 1)
                        if not first:
                            eng.wait_ge(vh_ready, place(n, j) - NT + 1)
                        eng.activation(tile[:, j, :], tile[:, j, :], ACT.Exp, scale=GEXP,
                                       accum_out=n_c[:, tiles + j:tiles + j + 1]).then_inc(score_ready, 1)

                def scores_p(n, bp, first):
                    eng.wait_ge(poly_ready, BJ * n)
                    scores(wp[:, bp, :, :], n, 4 * n, Z_SCALE, place_p, BT * bp + BJ, first)

                def round_(h, b, first=False):
                    n = 2 * h + b
                    head0 = isinstance(h, int) and h == 0
                    for j in range(BJ):
                        logs(n, j, first)
                    eng.preload_act_table_set("sigmoid_and_others")
                    for g in range(2):
                        eng.wait_ge(diff_ready, BJ * n + 2 * g + 2)
                        eng.activation(wt[:, 2 * g:2 * g + 2, :], wt[:, 2 * g:2 * g + 2, :], ACT.Tanh, scale=0.25)\
                           .then_inc(tanh_ready, 1)
                    for g in range(2):
                        eng.wait_ge(tanh_ready, 2 * n + g + 1)
                        eng.activation(wt[:, 2 * g:2 * g + 2, :], wt[:, 2 * g:2 * g + 2, :], ACT.Arctan)\
                           .then_inc(atan_ready, 1)
                    for j in range(BJ):
                        roots(n, b, j, first)
                    eng.preload_act_table_set("natural_log_exp_and_others")
                    if not first:
                        scores_p(n, before(h, b)[1], head0)
                    eng.wait_ge(atan_ready, 2 * n + 2)
                    scores(wt, n, 4 * n + 2, -2.0, place_t, BT * b, head0)

                eng.preload_act_table_set("natural_log_exp_and_others")
                eng.wait_ge(const_ready, 1)
                round_(0, 0, first=True)
                round_(0, 1)
                with eng.Fori(1, H) as h:
                    round_(h, 0)
                    round_(h, 1)
                scores_p(2 * H, 1, False)

            @block.tensor
            def _(eng):
                def cosines(h, k):
                    if k == 0:
                        eng.wait_ge(stacks_loaded, 16 * 2 * NPART * NPART * (h + 1))
                    for i in range(2):
                        eng.wait_ge(cos_read, 2 * NT * h + 2 * k + i + 1)
                        for c in range(2):
                            n_ = 2 * i + c
                            mm = eng.matmul(c_ps[:, i, c * BANK:(c + 1) * BANK], kst[:, k * P:(k + 1) * P],
                                            qst[:, n_ * BANK:(n_ + 1) * BANK], start=True, stop=True)
                        mm.then_inc(cos_ps, 1)

                def weigh(tile, k, place, start=False, stop=False):
                    eng.wait_ge(vh_ready, place + 1)
                    for c in range(NCH):
                        mm = eng.matmul(o_ps[VC * c:VC * (c + 1), :], vh[:, k, :],
                                        tile[:, c * BANK:(c + 1) * BANK], start=start, stop=stop)
                    mm.then_inc(pv_done, 1)

                def turn(h):
                    eng.wait_ge(o_copied, h + 1)
                    eng.wait_ge(attn_ready, h + 1)
                    for j in range(4):
                        mm = eng.transpose(t_ps[:, j, :], o_sb[:, j * P:(j + 1) * P], ident[:, :])
                    mm.then_inc(o_turned, 1)

                def weigh_p(n, bp):
                    for j in range(BJ):
                        weigh(wp[:, bp, j, :], BT * bp + BJ + j, place_p(n, j), stop=(bp == 1 and j == BJ - 1))

                def round_(h, b, first=False, last=False):
                    n = 2 * h + b
                    if first:
                        cosines(h, BT * b)
                        cosines(h, BT * b + 1)
                    for j in range(2, BT):
                        cosines(h, BT * b + j)
                    if not first:
                        weigh_p(n, before(h, b)[1])
                    if b == 0 and not first:
                        turn(h - 1)
                    for j in range(BJ):
                        if j in (0, 2) and not last:
                            cosines(h if b == 0 else h + 1, BT * (1 - b) + j // 2)
                        weigh(wt[:, j, :], BT * b + j, place_t(n, j), start=(b == 0 and j == 0))

                eng.sem_inc(score_ready, BJ)
                eng.sem_inc(rc_ready, BJ)
                eng.sem_inc(vh_ready, BJ)
                eng.sem_inc(pv_done, BJ)
                eng.sem_inc(lnth_ready, 2)
                eng.sem_inc(cos_read, 2)
                eng.sem_inc(cos_ps, 2)
                eng.sem_inc(attn_ready, 1)
                round_(0, 0, first=True)
                round_(0, 1)
                with eng.Fori(1, H - 1) as h:
                    round_(h, 0)
                    round_(h, 1)
                round_(H - 1, 0)
                round_(H - 1, 1, last=True)
                weigh_p(2 * H, 1)
                turn(H - 1)


def norm_on_vector(eng, link, src, dst, stats, mv, var, sd, tmp, var_ready, sd_ready, n):
    for k in range(NT):
        last = eng.bn_stats(stats[:, k, :], src[:, k, :])
    link(last)
    for k in range(NT):
        last = eng.bn_aggr(mv[:, k, :], stats[:, k, :])
    link(last)
    eng.tensor_scalar(var[:, :], mv[:, :, 1], 1e-5, None, ALU.add).then_inc(var_ready, 1)
    eng.wait_ge(sd_ready, n)
    link(eng.reciprocal(tmp[:, :], sd[:, :]))
    link(eng.tensor_tensor(tmp[:, :], tmp[:, :], var[:, :], ALU.mult))
    link(eng.tensor_tensor(tmp[:, :], tmp[:, :], sd[:, :], ALU.add))
    link(eng.reciprocal(tmp[:, :], tmp[:, :]))
    link(eng.tensor_scalar(tmp[:, :], tmp[:, :], 2.0, None, ALU.mult))
    for k in range(NT):
        last = eng.tensor_scalar(dst[:, k, :], src[:, k, :], mv[:, k, 0:1], tmp[:, k:k + 1],
                                 ALU.subtract, ALU.mult)
    link(last)


def stage_project1(nc, io, sb):
    base, attn0, ident, xn2T = sb["base"], sb["attn0"], sb["ident"], sb["xn2T"]
    HB = 8
    HALF = HD1 // 2
    with ExitStack() as ctx:
        def t(name, shape, dt=F32):
            return ctx.enter_context(nc.sbuf_tensor(name, shape, dt))

        def sem(name):
            return ctx.enter_context(nc.semaphore(name))

        attn0T = t("attn0T", [P, S])
        xn = t("xn2", [P, NT, D])
        xa = t("xa", [P, NT, D])
        xaT = attn0T
        stats, mv = t("stats1", [P, NT, 6]), t("mv1", [P, NT, 2])
        var, sd, tmp = t("var1", [P, NT]), t("sd1", [P, NT]), t("tmp1", [P, NT])
        w_out, b_out, gamma, beta, b_out1 = (sb[n] for n in ("w_out0", "b_out0", "gamma", "beta", "b_out1"))
        w_qkv = sb["w_qkv1"]
        cos_t, sin_t = t("cos_t", [P, NT, HALF]), t("sin_t", [P, NT, 2, HALF])
        ident_h = t("ident_h", [P, P], F16)
        ra, rb = t("ra", [P, 2, BANK]), t("rb", [P, 2, BANK])
        hl = t("hl", [P, 2, 2 * H, 2, HD1], F16)
        v_st = t("v_st", [P, 2, H, 4, VW], F16)
        stg = t("stg1", [P, 2, 2 * H, BANK], F16)
        psA = ctx.enter_context(nc.psum_tensor("psA1", [P, 2, BANK], F32))
        psR = ctx.enter_context(nc.psum_tensor("psR1", [P, 4, BANK], F32))
        psB = ctx.enter_context(nc.psum_tensor("psB1", [P, 2, 2 * BANK], F16))

        loaded, dve, weights_loaded = sem("loaded1"), sem("dve_chain1"), sb["weights1_loaded"]
        turned, taken = sem("turned1"), sem("taken1")
        out_ps, x1_ready = sem("out_ps1"), sem("x1_ready")
        var_ready, sd_ready = sem("var_ready1"), sem("sd_ready1")
        xn_ready, xa_ready = sem("xn_ready1"), sem("xa_ready1")
        qkv_ps, rope_read = sem("qkv_ps1"), sem("rope_read")
        v_high, v_low = sem("v_high"), sem("v_low")
        rot_ready, hi_ready, lo_ready = sem("rot_ready"), sem("hi_ready"), sem("lo_ready")
        hl_ps, hl_taken = sem("hl_ps"), sem("hl_taken")
        v_stored = [sem("v_stored_0"), sem("v_stored_1")]
        qk_stored = [sem("qk_stored_0"), sem("qk_stored_1")]
        last_stored = sem("last_stored")

        with nc.Block() as block:
            @block.sync
            def _(sp):
                for dst, src in ((cos_t[:, :, :], io["cos_t"].rearrange("(n p) f -> p n f", p=P)),
                                 (sin_t[:, :, :, :], io["sin_t"].rearrange("(n p) a f -> p n a f", p=P))):
                    sp.dma_start(dst, src).then_inc(loaded, 16)
                for k in range(NT):
                    if k % 4 == 3 and k < NT - 1:
                        n_ = k // 4
                        sp.wait_ge(v_low, 2 * k + 2)
                        sp.dma_start(io["v1"][:, :, 4 * n_:4 * n_ + 4, :].rearrange("h p n e -> p h n e"),
                                     v_st[:, n_ % 2, :, :, :]).then_inc(v_stored[n_ % 2], 16)
                        sp.wait_ge(hl_taken, 4 * (k + 1))
                        for x in range(2):
                            sp.dma_start(io["qk1"][x, :, :, n_ * BANK:(n_ + 1) * BANK].rearrange("h p t -> p h t"),
                                         stg[:, n_ % 2, x * H:(x + 1) * H, :]).then_inc(qk_stored[n_ % 2], 16)
                    if k in (NT - 3, NT - 1):
                        k0, n_ = k - 1, NCH - 1
                        sp.wait_ge(v_low, 2 * k + 2)
                        sp.dma_start(io["v1"][:, :, k0:k + 1, :].rearrange("h p n e -> p h n e"),
                                     v_st[:, n_ % 2, :, k0 % 4:k % 4 + 1, :]).then_inc(last_stored, 16)
                        sp.wait_ge(hl_taken, 4 * (k + 1))
                        for x in range(2):
                            sp.dma_start(io["qk1"][x, :, :, k0 * P:(k + 1) * P].rearrange("h p t -> p h t"),
                                         stg[:, n_ % 2, x * H:(x + 1) * H, k0 % 4 * P:(k % 4 + 1) * P])\
                              .then_inc(last_stored, 16)
                for slot, times in enumerate((2, 1)):
                    sp.wait_ge(v_stored[slot], 16 * times)
                    sp.wait_ge(qk_stored[slot], 32 * times)
                sp.wait_ge(last_stored, 6 * 16)

            @block.vector
            def _(eng):
                n = [0]

                def link(ins):
                    n[0] += 1
                    ins.then_inc(dve, 1)
                    eng.wait_ge(dve, n[0])

                eng.wait_ge(weights_loaded, 16 * 6)
                eng.tensor_copy(ident_h[:, :], ident[:, :])
                eng.memset(v_st[:, :, :, :, HD1:HD1 + 1], QS)
                eng.memset(v_st[:, :, :, :, VN:VW], 0.0)
                link(eng.tensor_tensor(base[:, :, :], base[:, :, :],
                                       b_out[:, :].unsqueeze(1).to_broadcast([P, NT, D]), ALU.add))
                for k in range(NT):
                    eng.wait_ge(out_ps, k + 1)
                    eng.tensor_tensor(base[:, k, :], base[:, k, :], psR[:, k % 4, 0:D], ALU.add).then_inc(x1_ready, 1)
                eng.wait_ge(x1_ready, NT)
                norm_on_vector(eng, link, base, xn, stats, mv, var, sd, tmp, var_ready, sd_ready, 1)
                eng.sem_inc(xn_ready, 1)
                norm_on_vector(eng, link, xn, xa, stats, mv, var, sd, tmp, var_ready, sd_ready, 2)
                link(eng.tensor_tensor(xa[:, :, :], xa[:, :, :], gamma[:, :].unsqueeze(1).to_broadcast([P, NT, D]),
                                       ALU.mult))
                eng.tensor_tensor(xa[:, :, :], xa[:, :, :], beta[:, :].unsqueeze(1).to_broadcast([P, NT, D]),
                                  ALU.add).then_inc(xa_ready, 1)
                eng.tensor_tensor(base[:, :, :], base[:, :, :], b_out1[:, :].unsqueeze(1).to_broadcast([P, NT, D]),
                                  ALU.add)

                eng.wait_ge(loaded, 32)
                for k in range(NT):
                    for b in range(4):
                        u = 4 * k + b
                        src = psR[:, b, :].rearrange("p (h a f) -> p h a f", h=HB, a=2)
                        a_ = ra[:, u % 2, :].rearrange("p (h a f) -> p h a f", h=HB, a=2)
                        b_ = rb[:, u % 2, :].rearrange("p (h a f) -> p h a f", h=HB, a=2)
                        eng.wait_ge(qkv_ps, 6 * k + b + 1)
                        if u >= 2:
                            eng.wait_ge(lo_ready, u - 1)
                        eng.tensor_tensor(a_, src, cos_t[:, k, :].unsqueeze(1).unsqueeze(1)
                                          .to_broadcast([P, HB, 2, HALF]), ALU.mult)
                        eng.tensor_tensor(b_[:, :, 0, :], src[:, :, 1, :],
                                          sin_t[:, k, 0, :].unsqueeze(1).to_broadcast([P, HB, HALF]), ALU.mult)
                        eng.tensor_tensor(b_[:, :, 1, :], src[:, :, 0, :],
                                          sin_t[:, k, 1, :].unsqueeze(1).to_broadcast([P, HB, HALF]), ALU.mult)\
                           .then_inc(rope_read, 1)
                        eng.wait_ge(rope_read, u + 1)
                        eng.tensor_tensor(ra[:, u % 2, :], ra[:, u % 2, :], rb[:, u % 2, :], ALU.add)\
                           .then_inc(rot_ready, 1)
                    for b in range(2):
                        eng.wait_ge(v_high, 2 * k + b + 1)
                        vv = v_st[:, k // 4 % 2, b * HB:(b + 1) * HB, k % 4, :]
                        eng.scalar_tensor_tensor(out=vv[:, :, HD1 + 1:VN],
                                                 in0=psA[:, b, :].rearrange("p (h e) -> p h e", h=HB), scalar=QS,
                                                 in1=vv[:, :, 0:HD1], op0=ALU.mult, op1=ALU.subtract)\
                           .then_inc(v_low, 1)

            @block.scalar
            def _(eng):
                for g in range(NCH):
                    eng.wait_ge(turned, g + 1)
                    eng.activation(attn0T[:, g * BANK:(g + 1) * BANK], psA[:, g % 2, :], ACT.Copy).then_inc(taken, 1)
                for i in range(2):
                    eng.wait_ge(var_ready, i + 1)
                    eng.activation(sd[:, :], var[:, :], ACT.Sqrt).then_inc(sd_ready, 1)
                    for g in range(NCH):
                        eng.wait_ge(turned, NCH * (i + 1) + g + 1)
                        dst = (xn2T, xaT)[i]
                        eng.activation(dst[:, g * BANK:(g + 1) * BANK], psA[:, g % 2, :], ACT.Copy).then_inc(taken, 1)

                def high_qk(k, b):
                    u = 4 * k + b
                    eng.wait_ge(rot_ready, u + 1)
                    if k >= 2:
                        eng.wait_ge(hl_ps, 4 * (k - 1))
                    eng.activation(hl[:, k % 2, b * HB:(b + 1) * HB, 0, :],
                                   ra[:, u % 2, :].rearrange("p (h e) -> p h e", h=HB), ACT.Copy)\
                       .then_inc(hi_ready, 1)

                def high_v(k, b):
                    eng.wait_ge(qkv_ps, 6 * k + 5 + b)
                    if k == 8 or k == 12:
                        eng.wait_ge(v_stored[k // 4 % 2], 16)
                    eng.activation(v_st[:, k // 4 % 2, b * HB:(b + 1) * HB, k % 4, 0:HD1],
                                   psA[:, b, :].rearrange("p (h e) -> p h e", h=HB), ACT.Copy, scale=QS)\
                       .then_inc(v_high, 1)

                def stage(k, g):
                    eng.wait_ge(hl_ps, 4 * k + g + 1)
                    if k % 4 == 0 and k >= 8:
                        eng.wait_ge(qk_stored[k // 4 % 2], 32 * (k // 8))
                    eng.activation(stg[:, k // 4 % 2, g * HB:(g + 1) * HB, k % 4 * P:(k % 4 + 1) * P],
                                   psB[:, g % 2, :].rearrange("p (h t) -> p h t", h=HB), ACT.Copy)\
                       .then_inc(hl_taken, 1)

                for k in range(NT):
                    high_qk(k, 0)
                    if k >= 1:
                        stage(k - 1, 3)
                    high_v(k, 0)
                    high_qk(k, 1)
                    high_v(k, 1)
                    high_qk(k, 2)
                    stage(k, 0)
                    high_qk(k, 3)
                    stage(k, 1)
                    stage(k, 2)
                stage(NT - 1, 3)

            @block.gpsimd
            def _(eng):
                for u in range(4 * NT):
                    k, b = u // 4, u % 4
                    dst = hl[:, k % 2, b * HB:(b + 1) * HB, :, :]
                    eng.wait_ge(hi_ready, u + 1)
                    eng.tensor_tensor(dst[:, :, 1, :], ra[:, u % 2, :].rearrange("p (h e) -> p h e", h=HB),
                                      dst[:, :, 0, :], ALU.subtract).then_inc(lo_ready, 1)

            @block.tensor
            def _(eng):
                def turn(src, i):
                    for g in range(NCH):
                        if 4 * i + g >= 2:
                            eng.wait_ge(taken, 4 * i + g - 1)
                        for j in range(4):
                            mm = eng.transpose(psA[:, g % 2, j * P:(j + 1) * P], src[:, 4 * g + j, :], ident[:, :])
                        mm.then_inc(turned, 1)

                eng.wait_ge(weights_loaded, 16 * 6)
                turn(attn0, 0)
                for k in range(NT):
                    if k % 4 == 0:
                        eng.wait_ge(taken, k // 4 + 1)
                    if k >= 4:
                        eng.wait_ge(x1_ready, k - 3)
                    eng.matmul(psR[:, k % 4, 0:D], attn0T[:, k * P:(k + 1) * P], w_out[:, :], start=True, stop=True)\
                       .then_inc(out_ps, 1)
                eng.wait_ge(xn_ready, 1)
                turn(xn, 1)
                eng.wait_ge(xa_ready, 1)
                turn(xa, 2)

                def qkv(k, b):
                    if k >= 1:
                        if b < 4:
                            eng.wait_ge(rope_read, 4 * (k - 1) + b + 1)
                        else:
                            eng.wait_ge(v_low, 2 * (k - 1) + b - 3)
                    dst = psR[:, b, :] if b < 4 else psA[:, b - 4, :]
                    eng.matmul(dst, xaT[:, k * P:(k + 1) * P], w_qkv[:, b * BANK:(b + 1) * BANK],
                               start=True, stop=True).then_inc(qkv_ps, 1)

                def turn_halves(k, g):
                    eng.wait_ge(lo_ready, 4 * k + g + 1)
                    if 4 * k + g >= 2:
                        eng.wait_ge(hl_taken, 4 * k + g - 1)
                    for j in range(HB):
                        mm = eng.transpose(psB[:, g % 2, j * P:(j + 1) * P],
                                           hl[:, k % 2, g * HB + j, :, :].rearrange("p a e -> p (a e)"),
                                           ident_h[:, :])
                    mm.then_inc(hl_ps, 1)

                eng.wait_ge(taken, 3 * NCH)
                for b in range(6):
                    qkv(0, b)
                for k in range(NT):
                    more = k + 1 < NT
                    for b in range(4):
                        if more:
                            qkv(k + 1, b)
                        if b >= 1:
                            turn_halves(k, b - 1)
                    if more:
                        qkv(k + 1, 4)
                        qkv(k + 1, 5)
                    turn_halves(k, 3)


def stage_attention1(nc, io, sb):
    attn1, ident = sb["attn1"], sb["ident"]
    KP = NT // 2
    STEPS = NS * KP
    NMX = NT * NCH
    MX0, MX1 = 2, STEPS - 5
    mx_at = [min(NMX, max(0, -(-NMX * (i - MX0) // (MX1 - MX0)))) for i in range(STEPS + 1)]
    LOW, SUM = 2, 4
    LV = 4
    with ExitStack() as ctx:
        def t(name, shape, dt=F32):
            return ctx.enter_context(nc.sbuf_tensor(name, shape, dt))

        def sem(name):
            return ctx.enter_context(nc.semaphore(name))

        qa, qb = t("qa", [P, 2, S], F16), t("qb", [P, 2, S], F16)
        ka, kb = t("ka", [P, 2, S], F16), t("kb", [P, 2, S], F16)
        vh = t("vh1", [P, 2, NT, VW], F16)
        pr = t("pr", [P, NPR, 2, SC])
        hi, lo = t("hi", [P, NHL, 2, SC], F16), t("lo", [P, NHL, 2, SC], F16)
        mx4, mx = t("mx4", [P, NT, NCH]), t("mx", [P, NT])
        mrow = t("mrow", [NT, P], F16)
        sums, rden = t("sums", [P, TS, VN]), t("rden", [P, TS])
        s_ps = ctx.enter_context(nc.psum_tensor("s_ps", [P, 2, 2, SC], F32))
        pv_ps = ctx.enter_context(nc.psum_tensor("pv_ps", [P, 2, BANK], F32))
        mx_ps = ctx.enter_context(nc.psum_tensor("mx_ps", [P, 2, BANK], F32))

        const_ready, loaded, mrow_loaded = sem("const_ready"), sem("loaded_d"), sem("mrow_loaded")
        mx_done, mx_taken, mx_ready = sem("mx_done"), sem("mx_taken"), sem("mx_ready")
        mt_ps, mt_copied = sem("mt_ps"), sem("mt_copied")
        s_done, exp_done, hi_done = sem("s_done"), sem("exp_done"), sem("hi_done")
        lo_vector, lo_gpsimd = sem("lo_vector"), sem("lo_gpsimd")
        pv_done = sem("pv_done1")
        sums_taken, div_ready, attn_ready = sem("sums_taken"), sem("div_ready"), sem("attn_ready1")
        rest_loaded, v_loaded = sem("rest_loaded"), sem("v_loaded")

        def head(g, par):
            return 2 * g + par

        def on_vector(i):
            return i % LV == LV - 1

        def wait_low(eng, h, i):
            if on_vector(i):
                eng.wait_ge(lo_vector, STEPS // LV * (h + 1) + i // LV + 1)
            else:
                eng.wait_ge(lo_gpsimd, STEPS // LV * (LV - 1) * (h + 1) + i // LV * (LV - 1) + i % LV + 1)

        def low(eng, h, i, lo_done):
            eng.wait_ge(hi_done, STEPS * h + i + 1)
            eng.wait_ge(pv_done, STEPS * (h + 2) + i + 1 - NHL)
            eng.tensor_tensor(lo[:, i % NHL, :, :], pr_slot(i), hi[:, i % NHL, :, :],
                              ALU.subtract).then_inc(lo_done, 1)

        def pr_slot(i):
            return pr[:, i % NPR, :, :]

        with nc.Block() as block:
            @block.sync
            def _(sp):
                def load(g, par):
                    h = head(g, par)
                    sp.wait_ge(s_done, STEPS * (h + 1))
                    q, k = io["qk1"][0], io["qk1"][1]
                    for dst, src, sem_ in ((qa[:, par, :], q[h, :, :], loaded),
                                           (ka[0:HD1, par, :], k[h, 0:HD1, :], loaded),
                                           (ka[HD1:P, par, :], k[h, 0:HD1, :], loaded),
                                           (qb[0:HD1, par, :], q[h, 0:HD1, :], rest_loaded),
                                           (kb[0:HD1, par, :], k[h, HD1:P, :], rest_loaded)):
                        sp.dma_start(dst, src).then_inc(sem_, 16)
                    sp.wait_ge(pv_done, STEPS * (h + 1))
                    sp.dma_start(vh[:, par, :, :].rearrange("p n e -> p (n e)"),
                                 io["v1"][h, :, :, :].rearrange("p n e -> p (n e)")).then_inc(v_loaded, 16)

                def maxima(g, par):
                    sp.wait_ge(mt_copied, head(g, par) + 2)
                    sp.dma_start(qb[HD1:HD1 + 1, par, :].rearrange("a (n t) -> a n t", t=P),
                                 mrow[:, :]).then_inc(mrow_loaded, 16)

                with sp.Fori(0, H // 2) as g:
                    for par in range(2):
                        load(g, par)
                        maxima(g, par)
                for dst, src in ((sb["w1"][:, :], io["w1_t"]), (sb["w2"][:, :], io["w2_t"]),
                                 (sb["sc"][:, 0, :], io["w1_s"]), (sb["sc"][:, 1, :], io["w2_s"]),
                                 (sb["sc"][:, 2, :], io["h1_s"]), (sb["sc"][:, 3, :], io["h2_s"]),
                                 (sb["h1"][:, :, :], io["h1_t"].rearrange("(k p) o -> p k o", p=P))):
                    sp.dma_start(dst, src).then_inc(sb["weights2_loaded"], 16)

            @block.vector
            def _(eng):
                for par in range(2):
                    last = eng.memset(kb[HD1:HD1 + 1, par, :], MROW)
                last.then_inc(const_ready, 1)

                def reduce_bank(h, q):
                    eng.wait_ge(mx_done, NMX * h + q + 1)
                    eng.tensor_reduce(mx4[:, q // NCH, q % NCH:q % NCH + 1], mx_ps[:, q % 2, :], AX.X, ALU.max)\
                       .then_inc(mx_taken, 1)

                def maxima(h):
                    eng.wait_ge(mx_taken, NMX * (h + 1) + 2)
                    eng.tensor_reduce(mx[:, :], mx4[:, :, :], AX.X, ALU.max).then_inc(mx_ready, 1)

                def row(h):
                    eng.wait_ge(mt_ps, h + 1)
                    eng.wait_ge(mrow_loaded, 16 * h + 16)
                    eng.tensor_scalar(mrow[:, :], mx_ps[0:NT, 0, 0:P], -1.0 / MROW, None, ALU.mult)\
                       .then_inc(mt_copied, 1)

                def take(h, c):
                    n_ = NS * h + c
                    eng.wait_ge(sums_taken, n_ + 2)
                    eng.reciprocal(rden[:, :].unsqueeze(2), sums[:, :, HD1:HD1 + 1])
                    eng.tensor_tensor(sums[:, :, 0:HD1], sums[:, :, 0:HD1], sums[:, :, HD1 + 1:VN], ALU.add)\
                       .then_inc(div_ready, 1)
                    eng.wait_ge(div_ready, n_ + 1)
                    eng.tensor_tensor(attn1[:, c * TS:(c + 1) * TS, bass.ds(h * HD1, HD1)], sums[:, :, 0:HD1],
                                      rden[:, :].unsqueeze(2).to_broadcast([P, TS, HD1]), ALU.mult)\
                       .then_inc(attn_ready, 1)

                def one(g, par, first=False, last=False):
                    h = head(g, par)
                    for i in range(STEPS):
                        if not last:
                            for q in range(mx_at[i], mx_at[i + 1]):
                                reduce_bank(h + 1, q)
                            if i == MX1:
                                maxima(h + 1)
                            if i == MX1 + 2:
                                row(h + 1)
                        if i % KP == SUM and not (first and i == SUM):
                            take(h - 1 if i == SUM else h, (i // KP - 1) % NS)
                        if (i >= LOW or not first) and on_vector(i - LOW):
                            low(eng, h, i - LOW, lo_vector)
                    if last:
                        for i in range(STEPS - LOW, STEPS):
                            if on_vector(i):
                                low(eng, h, i, lo_vector)
                        take(h, NS - 1)

                for q in range(NMX):
                    reduce_bank(0, q)
                maxima(0)
                row(0)
                one(0, 0, first=True)
                one(0, 1)
                with eng.Fori(1, H // 2 - 1) as g:
                    one(g, 0)
                    one(g, 1)
                one(H // 2 - 1, 0)
                one(H // 2 - 1, 1, last=True)

            @block.gpsimd
            def _(eng):
                with eng.Fori(0, H) as h:
                    for i in range(STEPS):
                        if not on_vector(i):
                            low(eng, h, i, lo_gpsimd)

            @block.scalar
            def _(eng):
                eng.preload_act_table(ACT.Exp)

                def high(h, i):
                    eng.wait_ge(exp_done, STEPS * h + i + 3)
                    eng.wait_ge(pv_done, STEPS * (h + 2) + i + 1 - NHL)
                    eng.activation(hi[:, i % NHL, :, :], pr_slot(i), ACT.Copy).then_inc(hi_done, 1)

                def take(h, c):
                    eng.wait_ge(attn_ready, NS * h + c + 1)
                    eng.wait_ge(pv_done, STEPS * (h + 2) + (c + 1) * KP)
                    eng.activation(sums[:, :, :].rearrange("p (b j) e -> p b j e", b=2),
                                   pv_ps[:, :, :].rearrange("p b (j e) -> p b j e", e=OW)[:, :, :, 0:VN],
                                   ACT.Copy).then_inc(sums_taken, 1)

                def one(h, first=False, last=False):
                    for i in range(STEPS):
                        eng.wait_ge(s_done, STEPS * (h + 2) + i + 1)
                        wait_low(eng, h, i - NPR)
                        eng.activation(pr_slot(i), s_ps[:, i % 2, :, :], ACT.Exp, scale=SM).then_inc(exp_done, 1)
                        if i % KP == SUM and not (first and i == SUM):
                            take(h - 1 if i == SUM else h, (i // KP - 1) % NS)
                        if i >= 1 or not first:
                            high(h, i - 1)
                    if last:
                        high(h, STEPS - 1)
                        take(h, NS - 1)

                one(0, first=True)
                with eng.Fori(1, H - 1) as h:
                    one(h)
                one(H - 1, last=True)

            @block.tensor
            def _(eng):
                def mx_bank(h, par, q):
                    if q == 0:
                        eng.wait_ge(loaded, 16 * 3 * (h + 1))
                        eng.wait_ge(mt_copied, h + 1)
                    eng.wait_ge(mx_taken, NMX * h + q + 1)
                    j, c = q // NCH, q % NCH
                    eng.matmul(mx_ps[:, q % 2, :], qa[:, par, j * P:(j + 1) * P],
                               ka[:, par, c * BANK:(c + 1) * BANK], start=True, stop=True).then_inc(mx_done, 1)

                def mx_turn(h):
                    eng.wait_ge(rest_loaded, 16 * 2 * (h + 1))
                    eng.wait_ge(mx_ready, h + 1)
                    eng.transpose(mx_ps[0:NT, 0, 0:P], mx[:, :], ident[:, :]).then_inc(mt_ps, 1)

                def scores(h, par, i):
                    if i == 0:
                        eng.wait_ge(mrow_loaded, 16 * (h + 2))
                    eng.wait_ge(exp_done, STEPS * h + i + 1)
                    c, kp = i // KP, i % KP
                    w = slice(c * SC, (c + 1) * SC)
                    for n_ in range(2):
                        k = 2 * kp + n_
                        eng.matmul(s_ps[:, i % 2, n_, :], ka[:, par, k * P:(k + 1) * P], qa[:, par, w],
                                   start=True, stop=False)
                        mm = eng.matmul(s_ps[:, i % 2, n_, :], kb[0:HD1 + 1, par, k * P:(k + 1) * P],
                                        qb[0:HD1 + 1, par, w], start=False, stop=True)
                    mm.then_inc(s_done, 1)

                def weigh(h, par, i):
                    c, kp = i // KP % NS, i % KP
                    if i == 0:
                        eng.wait_ge(v_loaded, 16 * (h + 1))
                    if kp == 0:
                        eng.wait_ge(sums_taken, NS * h + c + 1)
                    wait_low(eng, h, i)
                    for n_ in range(2):
                        k = 2 * kp + n_
                        for j in range(TS):
                            for half, cols in ((hi, VN), (lo, HD1 + 1)):
                                mm = eng.matmul(pv_ps[:, j // 2, j % 2 * OW:j % 2 * OW + cols],
                                                half[:, i % NHL, n_, j * P:(j + 1) * P], vh[:, par, k, 0:cols],
                                                start=(k == 0 and j % 2 == 0 and half is hi),
                                                stop=(k == NT - 1 and half is lo), skip_group_check=True)
                    mm.then_inc(pv_done, 1)

                def one(g, par, first=False, last=False):
                    h = head(g, par)
                    for i in range(STEPS):
                        q0, q1 = (mx_at[i], mx_at[i + 1]) if not last else (0, 0)
                        for q in range(q0, min(q0 + 1, q1)):
                            mx_bank(h + 1, 1 - par, q)
                        if i + 1 < STEPS:
                            scores(h, par, i + 1)
                        elif not last:
                            scores(h + 1, 1 - par, 0)
                        for q in range(q0 + 1, q1):
                            mx_bank(h + 1, 1 - par, q)
                        if i == MX1 + 1 and not last:
                            mx_turn(h + 1)
                        if i >= SUM or not first:
                            weigh(h, par if i >= SUM else 1 - par, i - SUM)
                    if last:
                        for i in range(STEPS - SUM, STEPS):
                            weigh(h, par, i)

                eng.sem_inc(pv_done, 2 * STEPS)
                eng.sem_inc(lo_vector, STEPS // LV)
                eng.sem_inc(lo_gpsimd, STEPS - STEPS // LV)
                eng.sem_inc(s_done, 2 * STEPS)
                eng.sem_inc(mx_taken, 2)
                eng.sem_inc(mt_copied, 1)
                eng.sem_inc(exp_done, 2)
                eng.sem_inc(sums_taken, 1)
                eng.sem_inc(attn_ready, 1)
                eng.sem_inc(mrow_loaded, 16)
                eng.wait_ge(const_ready, 1)
                for q in range(NMX):
                    mx_bank(0, 0, q)
                mx_turn(0)
                scores(0, 0, 0)
                one(0, 0, first=True)
                one(0, 1)
                with eng.Fori(1, H // 2 - 1) as g:
                    one(g, 0)
                    one(g, 1)
                one(H // 2 - 1, 0)
                one(H // 2 - 1, 1, last=True)


def stage_output(nc, io, sb):
    base, attn1, xn2T, ident = sb["base"], sb["attn1"], sb["xn2T"], sb["ident"]
    MO = INNER // P
    with ExitStack() as ctx:
        def t(name, shape, dt=F32):
            return ctx.enter_context(nc.sbuf_tensor(name, shape, dt))

        def sem(name):
            return ctx.enter_context(nc.semaphore(name))

        w1, w2, h1, sc = sb["w1"], sb["w2"], sb["h1"], sb["sc"]
        h2 = t("h2", [P, M1, F1])
        w3, wo = t("w3", [P, M1, D]), t("wo", [P, MO, D])
        s3 = t("s3", [P, D])
        ha, hb = t("ha", [P, M1, S]), t("hb", [P, M1, S])
        sil = t("sil1", [P, 2, BANK])
        y = t("y", [P, NT, D])
        psG = ctx.enter_context(nc.psum_tensor("psG1", [P, 2, BANK], F32))
        psU = ctx.enter_context(nc.psum_tensor("psU1", [P, 2, BANK], F32))
        psH = ctx.enter_context(nc.psum_tensor("psH1", [P, 2, BANK], F32))
        psO = ctx.enter_context(nc.psum_tensor("psO1", [P, 2, BANK], F32))
        aT = t("aT", [P, 2, MO, P])
        turned, aT_ready = sem("turned_e"), sem("aT_ready")

        loaded, weights_loaded = sem("loaded_e"), sb["weights2_loaded"]
        gate_ps, up_ps, sil_ready, ha_ready = sem("gate_ps1"), sem("up_ps1"), sem("sil_ready1"), sem("ha_ready")
        hid_ps, hid_ready = sem("hid_ps"), sem("hid_ready")
        down_ps, out_ps, y_scaled, y_sum, y_ready = (sem("down_ps1"), sem("out_ps_e"), sem("y_scaled"),
                                                     sem("y_sum"), sem("y_ready"))
        stored = sem("stored")
        NM = NCH * M1

        with nc.Block() as block:
            @block.sync
            def _(sp):
                for dst, src in ((h2[:, :, :], io["h2_t"].rearrange("(k p) o -> p k o", p=P)),
                                 (w3[:, :, :], io["w3_t"].rearrange("(k p) o -> p k o", p=P)),
                                 (wo[:, :, :], io["w_out1"].rearrange("(k p) o -> p k o", p=P)),
                                 (s3[:, :], io["w3_s"].partition_broadcast(P))):
                    sp.dma_start(dst, src).then_inc(loaded, 16)
                out = io["out"].rearrange("a (n p) d -> p (a n) d", p=P)
                for g in range(4):
                    sp.wait_ge(y_ready, 4 * g + 4)
                    sp.dma_start(out[:, 4 * g:4 * g + 4, :], y[:, 4 * g:4 * g + 4, :]).then_inc(stored, 16)
                sp.wait_ge(stored, 64)

            @block.tensor
            def _(eng):
                eng.wait_ge(weights_loaded, 16 * 7)
                for k in range(NM):
                    n_, m = k // M1, k % M1
                    rhs = xn2T[:, n_ * BANK:(n_ + 1) * BANK]
                    if k >= 2:
                        eng.wait_ge(sil_ready, k - 1)
                        eng.wait_ge(ha_ready, k - 1)
                    eng.matmul(psG[:, k % 2, :], w1[:, m * P:(m + 1) * P], rhs, start=True, stop=True)\
                       .then_inc(gate_ps, 1)
                    eng.matmul(psU[:, k % 2, :], w2[:, m * P:(m + 1) * P], rhs, start=True, stop=True)\
                       .then_inc(up_ps, 1)
                for l, (w, src) in enumerate(((h1, ha), (h2, hb))):
                    if l == 1:
                        eng.wait_ge(loaded, 16 * 4)
                    for k in range(NM):
                        n_, m = k // M1, k % M1
                        if m == 0:
                            eng.wait_ge((ha_ready, hid_ready)[l], (n_ + 1) * M1)
                        if l * NM + k >= 2:
                            eng.wait_ge(hid_ready, l * NM + k - 1)
                        for j in range(M1):
                            mm = eng.matmul(psH[:, k % 2, :], w[:, j, m * P:(m + 1) * P],
                                            src[:, j, n_ * BANK:(n_ + 1) * BANK], start=(j == 0), stop=(j == M1 - 1))
                        mm.then_inc(hid_ps, 1)
                def turn(k):
                    for b in range(2):
                        if k >= 1:
                            eng.wait_ge(aT_ready, 2 * (k - 1) + b + 1)
                        for j in range(4):
                            mm = eng.transpose(psU[:, b, j * P:(j + 1) * P],
                                               attn1[:, k, (4 * b + j) * P:(4 * b + j + 1) * P], ident[:, :])
                        mm.then_inc(turned, 1)

                turn(0)
                for k in range(NT):
                    if k + 1 < NT:
                        turn(k + 1)
                    if k % 4 == 0:
                        eng.wait_ge(hid_ready, NM + (k // 4 + 1) * M1)
                    if k >= 2:
                        eng.wait_ge(y_sum, k - 1)
                    for j in range(M1):
                        mm = eng.matmul(psG[:, k % 2, 0:D], ha[:, j, k * P:(k + 1) * P], w3[:, j, :],
                                        start=(j == 0), stop=(j == M1 - 1))
                    mm.then_inc(down_ps, 1)
                    eng.wait_ge(aT_ready, 2 * k + 2)
                    for j in range(MO):
                        mm = eng.matmul(psO[:, k % 2, 0:D], aT[:, k % 2, j, :], wo[:, j, :],
                                        start=(j == 0), stop=(j == MO - 1))
                    mm.then_inc(out_ps, 1)

            @block.scalar
            def _(eng):
                for k in range(NM):
                    m = k % M1
                    eng.wait_ge(gate_ps, k + 1)
                    if k >= 2:
                        eng.wait_ge(ha_ready, k - 1)
                    eng.activation(sil[:, k % 2, :], psG[:, k % 2, :], ACT.Silu, scale=sc[:, 0, m:m + 1])\
                       .then_inc(sil_ready, 1)
                for l, dst in enumerate((hb, ha)):
                    for k in range(NM):
                        n_, m = k // M1, k % M1
                        eng.wait_ge(hid_ps, l * NM + k + 1)
                        eng.activation(dst[:, m, n_ * BANK:(n_ + 1) * BANK], psH[:, k % 2, :], ACT.Gelu,
                                       scale=sc[:, 2 + l, m:m + 1]).then_inc(hid_ready, 1)
                for k in range(NT):
                    for b in range(2):
                        eng.wait_ge(turned, 2 * k + b + 1)
                        if k >= 2:
                            eng.wait_ge(out_ps, k - 1)
                        eng.activation(aT[:, k % 2, 4 * b:4 * b + 4, :],
                                       psU[:, b, :].rearrange("p (j t) -> p j t", j=4), ACT.Copy)\
                           .then_inc(aT_ready, 1)

            @block.vector
            def _(eng):
                for k in range(NM):
                    n_, m = k // M1, k % M1
                    eng.wait_ge(up_ps, k + 1)
                    eng.wait_ge(sil_ready, k + 1)
                    eng.scalar_tensor_tensor(out=ha[:, m, n_ * BANK:(n_ + 1) * BANK], in0=psU[:, k % 2, :],
                                             scalar=sc[:, 1, m:m + 1], in1=sil[:, k % 2, :], op0=ALU.mult,
                                             op1=ALU.mult).then_inc(ha_ready, 1)
                for k in range(NT):
                    eng.wait_ge(down_ps, k + 1)
                    eng.tensor_tensor(y[:, k, :], psG[:, k % 2, 0:D], s3[:, :], ALU.mult).then_inc(y_scaled, 1)
                    eng.wait_ge(y_scaled, k + 1)
                    eng.wait_ge(out_ps, k + 1)
                    eng.tensor_tensor(y[:, k, :], y[:, k, :], psO[:, k % 2, 0:D], ALU.add).then_inc(y_sum, 1)
                    eng.wait_ge(y_sum, k + 1)
                    eng.tensor_tensor(y[:, k, :], y[:, k, :], base[:, k, :], ALU.add).then_inc(y_ready, 1)


def program(nc, io):
    with ExitStack() as ctx:
        def keep(stack, name, shape, dt=F32):
            return stack.enter_context(nc.sbuf_tensor(name, shape, dt))

        sb = dict(ident=keep(ctx, "ident", [P, P]), base=keep(ctx, "base", [P, NT, D]),
                  xn2T=keep(ctx, "xn2T", [P, S]))
        with ExitStack() as layer0:
            sb |= dict(ident_b=keep(layer0, "ident_b", [P, P], BF16), v0=keep(layer0, "v0", [P, NT, D]),
                       attn0=keep(layer0, "attn0", [P, NT, D]),
                       w_out0=keep(layer0, "w_out0", [P, D]), b_out0=keep(layer0, "b_out0", [P, D]),
                       gamma=keep(layer0, "gamma", [P, D]), beta=keep(layer0, "beta", [P, D]),
                       b_out1=keep(layer0, "b_out1", [P, D]), w_qkv1=keep(layer0, "w_qkv1", [P, 3 * INNER]),
                       weights1_loaded=layer0.enter_context(nc.semaphore("weights1_loaded")))
            stage_project0(nc, io, sb)
            stage_attention0(nc, io, sb)
            stage_project1(nc, io, sb)
        with ExitStack() as layer1:
            sb |= dict(attn1=keep(layer1, "attn1", [P, NT, INNER]), w1=keep(layer1, "w1", [P, F1]),
                       w2=keep(layer1, "w2", [P, F1]), sc=keep(layer1, "sc", [P, 4, M1]),
                       h1=keep(layer1, "h1", [P, M1, F1]),
                       weights2_loaded=layer1.enter_context(nc.semaphore("weights2_loaded")))
            stage_attention1(nc, io, sb)
            stage_output(nc, io, sb)


def kernel(**inputs):
    import numpy as _np
    import concourse.bacc as _bacc
    from concourse.bass_utils import run_bass_kernel_spmd as _run

    a = {k: _np.asarray(v) for k, v in inputs.items()}
    half = HD1 // 2
    freq = (_np.float32(1.0) / _np.float32(10000.0) ** (_np.arange(0, HD1, 2, dtype=_np.float32)
                                                        / _np.float32(HD1))).astype(_np.float32)
    ang = _np.arange(S, dtype=_np.float32)[:, None] * freq[None, :]
    cos_t = (QS * _np.cos(ang)).astype(_np.float32)
    sin_t = (QS * _np.sin(ang)).astype(_np.float32)
    ins = {
        "x": a["L0_attn_x"],
        "ident": _np.eye(P, dtype=_np.float32),
        "cos_t": cos_t,
        "sin_t": _np.stack([-sin_t, sin_t], axis=1),
        "w_qkv0_t": a["L0_attn_w_qkv"].T,
        "b_qkv0": a["L0_attn_b_qkv"],
        "w_out0_t": a["L0_attn_w_out"].T,
        "b_out0": a["L0_attn_b_out"],
        "w_gate_t": a["L0_ffn_w_gate"].T,
        "w_up_t": a["L0_ffn_w_up"].T,
        "w_down_t": a["L0_ffn_w_down"].T,
        "gamma": a["L1_attn_ln_gamma"],
        "beta": a["L1_attn_ln_beta"],
        "w_qkv1": a["L1_attn_w_qkv"],
        "w_out1": a["L1_attn_w_out"],
        "b_out1": a["L1_attn_b_out"],
        "w1_t": a["L1_ffn_w1_w"].T, "w1_s": a["L1_ffn_w1_s"].reshape(M1, P).T,
        "w2_t": a["L1_ffn_w2_w"].T, "w2_s": a["L1_ffn_w2_s"].reshape(M1, P).T,
        "h1_t": a["L1_ffn_h1_w"].T, "h1_s": a["L1_ffn_h1_s"].reshape(M1, P).T,
        "h2_t": a["L1_ffn_h2_w"].T, "h2_s": a["L1_ffn_h2_s"].reshape(M1, P).T,
        "w3_t": a["L1_ffn_w3_w"].T, "w3_s": a["L1_ffn_w3_s"],
    }
    nc = _bacc.Bacc("TRN2", target_bir_lowering=False, num_devices=1)
    arrays, io = {}, {}
    for name, v in ins.items():
        v = _np.ascontiguousarray(v)
        arrays[f"in_{name}"] = v
        io[name] = nc.dram_tensor(f"in_{name}", v.shape, mybir.dt.from_np(v.dtype), kind="ExternalInput").ap()
    io["parts"] = nc.dram_tensor("parts_dram", (NPART, 2, H, HD0, S), BF16).ap()
    io["qk1"] = nc.dram_tensor("qk1", (2, H, P, S), F16).ap()
    io["v1"] = nc.dram_tensor("v1", (H, P, NT, VW), F16).ap()
    io["out"] = nc.dram_tensor("out", (1, S, D), F32, kind="ExternalOutput").ap()
    program(nc, io)
    r = _run(nc, [arrays], core_ids=[0])
    return r.results[0]["out"]
```
